# Optimizing a Trainium2 kernel written in Bass

```python
import numpy as np
import jax
import jax.numpy as jnp

def _softmax(x, axis=-1):
    return jax.nn.softmax(x, axis=axis)

def _gelu(x):
    return jax.nn.gelu(x, approximate=True)

def _silu(x):
    return jax.nn.silu(x)

def _sigmoid(x):
    return jax.nn.sigmoid(x)

def _layernorm(x, axis=-1, eps=1e-05):
    m = jnp.mean(x, axis=axis, keepdims=True)
    v = jnp.var(x, axis=axis, keepdims=True)
    return (x - m) / jnp.sqrt(v + eps)

def _scatter_add(tgt, idx, src, axis=0):
    return tgt.at[idx].add(src)

def _segment_sum(src, seg, n):
    return jax.ops.segment_sum(src, seg, n)
kernel_name = 'mk_sandwich_d1_jaxref_r8_66630c'

def setup_inputs(seed: int=0):
    np.random.seed(seed)
    _w = jnp.asarray

    def _L0_attn_setup():
        import jax, jax.numpy as jnp
        import numpy as np
        import math
        DIM_EMBD = 128
        N_HEADS = 16
        DIM_HEAD = DIM_EMBD // N_HEADS
        LAMBDA_INIT = 0.8
        EPS = 1e-05
        key = jax.random.key(seed)
        ks = jax.random.split(key, 9)
        B, N = (2, 256)
        d2 = 2 * DIM_HEAD * N_HEADS
        xavier = lambda k, shp: jax.random.uniform(k, shp, jnp.float32, -1.0, 1.0) * math.sqrt(6.0 / (shp[0] + shp[1]))
        return {'X': jax.random.normal(ks[0], (B, N, DIM_EMBD), jnp.float32), 'W_q': xavier(ks[1], (d2, DIM_EMBD)), 'W_k': xavier(ks[2], (d2, DIM_EMBD)), 'W_v': xavier(ks[3], (d2, DIM_EMBD)), 'W_o': xavier(ks[4], (DIM_EMBD, d2)), 'lambda_q1': jax.random.normal(ks[5], (N_HEADS, DIM_HEAD), jnp.float32), 'lambda_k1': jax.random.normal(ks[6], (N_HEADS, DIM_HEAD), jnp.float32), 'lambda_q2': jax.random.normal(ks[7], (N_HEADS, DIM_HEAD), jnp.float32), 'lambda_k2': jax.random.normal(ks[8], (N_HEADS, DIM_HEAD), jnp.float32), 'rms_scale': jnp.ones((2 * DIM_HEAD,), jnp.float32)}
    _L0_attn_in = _L0_attn_setup()

    def _L0_ffn_setup():
        import jax, jax.numpy as jnp
        import numpy as np
        from functools import partial
        DIM = 128
        LIGHT_HID = 64
        HEAVY_HID = 512
        NUM_HEAVY = 128
        N_ITERS = 50
        K_ROUTE = 8.0
        EPS = 0.1

        def rms_norm(x, gamma):
            norm = jnp.linalg.norm(x, axis=-1, keepdims=True)
            normed = x / jnp.maximum(norm, 1e-12)
            return normed * x.shape[-1] ** 0.5 * gamma

        def ffn(x, gamma, w1, b1, w2, b2):
            h = rms_norm(x, gamma)
            h = jax.nn.gelu(h @ w1 + b1, approximate=False)
            return h @ w2 + b2

        def coor_descent_route(x, routing_token, num_tokens):
            s = jnp.einsum('bnd,d->bn', x, routing_token)
            constant = EPS * jnp.log(jnp.asarray(K_ROUTE, dtype=s.dtype))
            b0 = -jax.nn.relu(s)
            a0 = jnp.zeros((s.shape[0], 1), dtype=s.dtype)

            def step(carry, _):
                a_prev, b = carry
                a = constant - EPS * jax.nn.logsumexp((s + b) / EPS, axis=-1, keepdims=True)
                b = -jax.nn.relu(s + a)
                return ((a, b), None)
            (a, b), _ = jax.lax.scan(step, (a0, b0), None, length=N_ITERS)
            scores = jnp.exp((s + a + b) / EPS)
            sel_scores, sel_idx = jax.lax.top_k(scores, num_tokens)
            sel_scores = sel_scores + jax.lax.stop_gradient(1.0 - sel_scores)
            return (sel_scores, sel_idx)
        key = jax.random.key(seed)
        ks = jax.random.split(key, 12)

        def lin(k, fan_in, fan_out):
            lim = 1.0 / np.sqrt(fan_in)
            kw, kb = jax.random.split(k)
            w = jax.random.uniform(kw, (fan_in, fan_out), jnp.float32, -lim, lim)
            b = jax.random.uniform(kb, (fan_out,), jnp.float32, -lim, lim)
            return (w, b)
        x = jax.random.normal(ks[0], (4, 1024, DIM), jnp.float32)
        routing_token = jax.random.normal(ks[1], (DIM,), jnp.float32)
        gamma_light = jnp.ones((DIM,), jnp.float32)
        w1_l, b1_l = lin(ks[2], DIM, LIGHT_HID)
        w2_l, b2_l = lin(ks[3], LIGHT_HID, DIM)
        gamma_heavy = jnp.ones((DIM,), jnp.float32)
        w1_h, b1_h = lin(ks[4], DIM, HEAVY_HID)
        w2_h, b2_h = lin(ks[5], HEAVY_HID, DIM)
        return dict(x=x, routing_token=routing_token, gamma_light=gamma_light, w1_light=w1_l, b1_light=b1_l, w2_light=w2_l, b2_light=b2_l, gamma_heavy=gamma_heavy, w1_heavy=w1_h, b1_heavy=b1_h, w2_heavy=w2_h, b2_heavy=b2_h)
    _L0_ffn_in = _L0_ffn_setup()
    _d = {'L0_attn_X': _L0_attn_in['X'], 'L0_attn_W_q': _L0_attn_in['W_q'], 'L0_attn_W_k': _L0_attn_in['W_k'], 'L0_attn_W_v': _L0_attn_in['W_v'], 'L0_attn_W_o': _L0_attn_in['W_o'], 'L0_attn_lambda_q1': _L0_attn_in['lambda_q1'], 'L0_attn_lambda_k1': _L0_attn_in['lambda_k1'], 'L0_attn_lambda_q2': _L0_attn_in['lambda_q2'], 'L0_attn_lambda_k2': _L0_attn_in['lambda_k2'], 'L0_attn_rms_scale': _L0_attn_in['rms_scale'], 'L0_ffn_routing_token': _L0_ffn_in['routing_token'], 'L0_ffn_gamma_light': _L0_ffn_in['gamma_light'], 'L0_ffn_w1_light': _L0_ffn_in['w1_light'], 'L0_ffn_b1_light': _L0_ffn_in['b1_light'], 'L0_ffn_w2_light': _L0_ffn_in['w2_light'], 'L0_ffn_b2_light': _L0_ffn_in['b2_light'], 'L0_ffn_gamma_heavy': _L0_ffn_in['gamma_heavy'], 'L0_ffn_w1_heavy': _L0_ffn_in['w1_heavy'], 'L0_ffn_b1_heavy': _L0_ffn_in['b1_heavy'], 'L0_ffn_w2_heavy': _L0_ffn_in['w2_heavy'], 'L0_ffn_b2_heavy': _L0_ffn_in['b2_heavy']}
    _x0 = _d['L0_attn_X']
    _d['L0_attn_X'] = jax.random.normal(jax.random.fold_in(jax.random.key(seed), 1), (8, 512, 128), dtype=_x0.dtype)
    del _x0
    return _d

def reference(L0_attn_X, L0_attn_W_q, L0_attn_W_k, L0_attn_W_v, L0_attn_W_o, L0_attn_lambda_q1, L0_attn_lambda_k1, L0_attn_lambda_q2, L0_attn_lambda_k2, L0_attn_rms_scale, L0_ffn_routing_token, L0_ffn_gamma_light, L0_ffn_w1_light, L0_ffn_b1_light, L0_ffn_w2_light, L0_ffn_b2_light, L0_ffn_gamma_heavy, L0_ffn_w1_heavy, L0_ffn_b1_heavy, L0_ffn_w2_heavy, L0_ffn_b2_heavy):

    def _L0_attn_ref(X, W_q, W_k, W_v, W_o, lambda_q1, lambda_k1, lambda_q2, lambda_k2, rms_scale):
        import jax, jax.numpy as jnp
        import numpy as np
        import math
        DIM_EMBD = 128
        N_HEADS = 16
        DIM_HEAD = DIM_EMBD // N_HEADS
        LAMBDA_INIT = 0.8
        EPS = 1e-05
        B, N, _ = X.shape
        H, dh = (N_HEADS, DIM_HEAD)

        def split_heads(Y):
            return Y.reshape(B, N, H, 2 * dh).transpose(0, 2, 1, 3)
        Q = split_heads(X @ W_q.T)
        K = split_heads(X @ W_k.T)
        V = split_heads(X @ W_v.T)
        Q1, Q2 = (Q[..., :dh], Q[..., dh:])
        K1, K2 = (K[..., :dh], K[..., dh:])
        lam = jnp.exp(jnp.sum(lambda_q1 * lambda_k1, -1)) - jnp.exp(jnp.sum(lambda_q2 * lambda_k2, -1)) + LAMBDA_INIT
        lam = lam[None, :, None, None]
        scaling = 1.0 / math.sqrt(dh)
        causal = jnp.tril(jnp.ones((N, N), jnp.bool_))
        neg_inf = jnp.float32(-jnp.inf)
        A1 = jnp.einsum('bhqd,bhkd->bhqk', Q1, K1) * scaling
        A2 = jnp.einsum('bhqd,bhkd->bhqk', Q2, K2) * scaling
        A1 = jnp.where(causal, A1, neg_inf)
        A2 = jnp.where(causal, A2, neg_inf)
        attn = jax.nn.softmax(A1, -1) - lam * jax.nn.softmax(A2, -1)
        O = jnp.einsum('bhqk,bhkd->bhqd', attn, V)
        rms = jnp.sqrt(jnp.mean(O * O, -1, keepdims=True) + EPS)
        O = O / rms * rms_scale * (1.0 - LAMBDA_INIT)
        O = O.transpose(0, 2, 1, 3).reshape(B, N, H * 2 * dh)
        return O @ W_o.T

    def _L0_ffn_ref(x, routing_token, gamma_light, w1_light, b1_light, w2_light, b2_light, gamma_heavy, w1_heavy, b1_heavy, w2_heavy, b2_heavy):
        import jax, jax.numpy as jnp
        import numpy as np
        from functools import partial
        DIM = 128
        LIGHT_HID = 64
        HEAVY_HID = 512
        NUM_HEAVY = 128
        N_ITERS = 50
        K_ROUTE = 8.0
        EPS = 0.1

        def rms_norm(x, gamma):
            norm = jnp.linalg.norm(x, axis=-1, keepdims=True)
            normed = x / jnp.maximum(norm, 1e-12)
            return normed * x.shape[-1] ** 0.5 * gamma

        def ffn(x, gamma, w1, b1, w2, b2):
            h = rms_norm(x, gamma)
            h = jax.nn.gelu(h @ w1 + b1, approximate=False)
            return h @ w2 + b2

        def coor_descent_route(x, routing_token, num_tokens):
            s = jnp.einsum('bnd,d->bn', x, routing_token)
            constant = EPS * jnp.log(jnp.asarray(K_ROUTE, dtype=s.dtype))
            b0 = -jax.nn.relu(s)
            a0 = jnp.zeros((s.shape[0], 1), dtype=s.dtype)

            def step(carry, _):
                a_prev, b = carry
                a = constant - EPS * jax.nn.logsumexp((s + b) / EPS, axis=-1, keepdims=True)
                b = -jax.nn.relu(s + a)
                return ((a, b), None)
            (a, b), _ = jax.lax.scan(step, (a0, b0), None, length=N_ITERS)
            scores = jnp.exp((s + a + b) / EPS)
            sel_scores, sel_idx = jax.lax.top_k(scores, num_tokens)
            sel_scores = sel_scores + jax.lax.stop_gradient(1.0 - sel_scores)
            return (sel_scores, sel_idx)
        bsz = x.shape[0]
        light_out = ffn(x, gamma_light, w1_light, b1_light, w2_light, b2_light)
        sel_scores, sel_idx = coor_descent_route(x, routing_token, NUM_HEAVY)
        batch_range = jnp.arange(bsz)[:, None]
        routed = x[batch_range, sel_idx]
        routed_out = ffn(routed, gamma_heavy, w1_heavy, b1_heavy, w2_heavy, b2_heavy)
        routed_out = routed_out * sel_scores[..., None]
        heavy_out = jnp.zeros_like(x).at[batch_range, sel_idx].set(routed_out)
        return light_out + heavy_out
    x = L0_attn_X
    x = x + _layernorm(_L0_attn_ref(_layernorm(x, axis=-1), L0_attn_W_q, L0_attn_W_k, L0_attn_W_v, L0_attn_W_o, L0_attn_lambda_q1, L0_attn_lambda_k1, L0_attn_lambda_q2, L0_attn_lambda_k2, L0_attn_rms_scale), axis=-1)
    x = x + _layernorm(_L0_ffn_ref(_layernorm(x, axis=-1), L0_ffn_routing_token, L0_ffn_gamma_light, L0_ffn_w1_light, L0_ffn_b1_light, L0_ffn_w2_light, L0_ffn_b2_light, L0_ffn_gamma_heavy, L0_ffn_w1_heavy, L0_ffn_b1_heavy, L0_ffn_w2_heavy, L0_ffn_b2_heavy), axis=-1)
    return x

_drawn_inputs = setup_inputs


def setup_inputs(seed=0):
    import zlib

    import numpy as np

    out = dict(_drawn_inputs(seed))
    spreads = {'L0_attn_rms_scale': (1.0, 0.2),
     'L0_ffn_gamma_light': (1.0, 0.2),
     'L0_ffn_gamma_heavy': (1.0, 0.2)}
    factors = {'L0_ffn_b1_heavy': 3.149}
    for name, (base, spread) in spreads.items():
        noise = np.random.default_rng([zlib.crc32(name.encode()), seed]).standard_normal(out[name].shape)
        drawn = base * np.exp(spread * noise) if base else spread * noise
        out[name] = jnp.asarray(drawn.astype(out[name].dtype))
    for name, factor in factors.items():
        out[name] = (out[name] * factor).astype(out[name].dtype)
    return out
```

```python
from contextlib import ExitStack

import concourse.bass as bass
from concourse import mybir

F32 = mybir.dt.float32
BF16 = mybir.dt.bfloat16
ALU = mybir.AluOpType
ACT = mybir.ActivationFunctionType
AX = mybir.AxisListType

P = 128
B = 8
N = 512
D = 128
H = 16
DH = 8
QB = N // P
TILES = B * QB
D2 = 2 * DH * H
COMBOS = 2 * H
PAIRS = H // 2
SPLITS = 6
Q_PARTS = (0, 1, 2, 0, 1, 0)
K_PARTS = (0, 0, 0, 1, 1, 2)
KR = SPLITS * DH
KM = KR + 3
HV = 2 * DH + 1
LIGHT = 64
HEAVY = 512
HC = HEAVY // P
TOPK = 128
ITERS = 50
K_ROUTE = 8.0
REBASE = 10
CLIP = 60.0
LN_EPS = 1e-5
NEG = -1.0e30
CUT = -87.3365
SCALE = float(DH) ** -0.5
GROUPS = 5
REBASES = -(-(ITERS - 1) // REBASE)
LAMBDA_INIT = 0.8
LN2 = 0.6931471805599453
LOG_K = 2.0794415416798357
REBASES = -(-(ITERS - 1) // REBASE)
LAMBDA_INIT = 0.8
LN2 = 0.6931471805599453
LOG_K = 2.0794415416798357
REBASES = -(-(ITERS - 1) // REBASE)
LAMBDA_INIT = 0.8
LN2 = 0.6931471805599453
LOG_K = 2.0794415416798357
REBASES = -(-(ITERS - 1) // REBASE)
LAMBDA_INIT = 0.8
LN2 = 0.6931471805599453
LOG_K = 2.0794415416798357
REBASES = -(-(ITERS - 1) // REBASE)
LAMBDA_INIT = 0.8
LN2 = 0.6931471805599453
LOG_K = 2.0794415416798357
REBASES = -(-(ITERS - 1) // REBASE)
LAMBDA_INIT = 0.8
LN2 = 0.6931471805599453
LOG_K = 2.0794415416798357
REBASES = -(-(ITERS - 1) // REBASE)
LAMBDA_INIT = 0.8
LN2 = 0.6931471805599453
LOG_K = 2.0794415416798357
LOG_SHIFT = 32



class Chain:

    def __init__(self, engine, done, start=0):
        self.engine, self.done, self.start, self.n = engine, done, start, 0

    def __call__(self, instruction):
        self.n += 1
        instruction.then_inc(self.done, 1)
        self.engine.wait_ge(self.done, self.start + self.n)



class Chain:

    def __init__(self, engine, done, start=0):
        self.engine, self.done, self.start, self.n = engine, done, start, 0

    def __call__(self, instruction):
        self.n += 1
        instruction.then_inc(self.done, 1)
        self.engine.wait_ge(self.done, self.start + self.n)



class Chain:

    def __init__(self, engine, done, start=0):
        self.engine, self.done, self.start, self.n = engine, done, start, 0

    def __call__(self, instruction):
        self.n += 1
        instruction.then_inc(self.done, 1)
        self.engine.wait_ge(self.done, self.start + self.n)



class Chain:

    def __init__(self, engine, done, start=0):
        self.engine, self.done, self.start, self.n = engine, done, start, 0

    def __call__(self, instruction):
        self.n += 1
        instruction.then_inc(self.done, 1)
        self.engine.wait_ge(self.done, self.start + self.n)



class Chain:

    def __init__(self, engine, done, start=0):
        self.engine, self.done, self.start, self.n = engine, done, start, 0

    def __call__(self, instruction):
        self.n += 1
        instruction.then_inc(self.done, 1)
        self.engine.wait_ge(self.done, self.start + self.n)



class Chain:

    def __init__(self, engine, done, start=0):
        self.engine, self.done, self.start, self.n = engine, done, start, 0

    def __call__(self, instruction):
        self.n += 1
        instruction.then_inc(self.done, 1)
        self.engine.wait_ge(self.done, self.start + self.n)



class Chain:

    def __init__(self, engine, done, start=0):
        self.engine, self.done, self.start, self.n = engine, done, start, 0

    def __call__(self, instruction):
        self.n += 1
        instruction.then_inc(self.done, 1)
        self.engine.wait_ge(self.done, self.start + self.n)


def program(nc, X, Wq, Wk, Wv, Wo, lq1, lk1, lq2, lk2, rms_scale, route, g_l, w1_l, b1_l, w2_l, b2_l,
            g_h, w1_h, b1_h, w2_h, b2_h, out):
    ctx = ExitStack()
    with ctx:
        ctx.enter_context(nc.allow_non_contiguous_dma("small vectors and rearranged scratch"))

        def sb(name, shape, dt=F32):
            return ctx.enter_context(nc.sbuf_tensor(name, shape, dt))

        def sem(name):
            return ctx.enter_context(nc.semaphore(name))

        q_dram = nc.dram_tensor("q_scratch", (B, COMBOS, KR, N), BF16, kind="Internal").ap()
        k_dram = nc.dram_tensor("k_scratch", (B, COMBOS, KR, N), BF16, kind="Internal").ap()
        v_dram = nc.dram_tensor("v_scratch", (B, P, PAIRS, QB * 2 * HV), F32, kind="Internal").ap()
        u_dram = nc.dram_tensor("u_scratch", (TILES, P), F32, kind="Internal").ap()

        ident = sb("ident", [P, P])
        ident_bf = sb("ident_bf", [P, P], BF16)
        causal_bf = sb("causal_bf", [P, P], BF16)
        eps_col = sb("eps_col", [P, 1])
        shift_col = sb("shift_col", [P, 1])
        w_rows = sb("w_rows", [P, 8, P])
        w_qkv = sb("w_qkv", [P, 6, P])
        w_o = sb("w_o", [P, 2, P])
        o_scale = sb("o_scale", [P, 1])
        lam_in = sb("lam_in", [P, 4, H * DH])
        lam_prod = sb("lam_prod", [P, 2, H * DH])
        lam_sum = sb("lam_sum", [P, 2, H])
        coef = sb("coef", [P, H, 2])
        route_row = sb("route_row", [P, D])
        w1 = sb("w1", [P, LIGHT + HEAVY])
        w1g = sb("w1g", [P, LIGHT + HEAVY])
        gam = sb("gam", [P, 2])
        b1c = sb("b1c", [P, 1 + HC])
        w2h = sb("w2h", [P, HC, D])
        w2l = sb("w2l", [LIGHT, D])
        b2 = sb("b2", [P, 2, D])

        x = sb("x", [P, TILES, D])
        attn = sb("attn", [P, B, QB, H, 2 * DH])
        st = sb("st", [P, TILES, 6])
        mv = sb("mv", [P, TILES, 2])
        ve = sb("ve", [P, TILES])
        lg = sb("lg", [P, TILES])
        rs = sb("rs", [P, TILES])
        tn = sb("tn", [P, TILES])

        psum = ctx.enter_context(nc.psum_tensor("psum", [P, 8, N], F32))

        s_pool_go = sem("s_pool_go")
        s_x = sem("s_x")
        s_w = sem("s_w")
        s_const = sem("s_const")
        s_dve = sem("s_dve")
        s_stat = sem("s_stat")
        s_log = sem("s_log")
        s_exp0 = sem("s_exp0")
        s_wt = sem("s_wt")
        s_wtc = sem("s_wtc")
        dve_steps = [0]

        def dve_chain(dve):
            return Chain(dve, s_dve, dve_steps[0])

        def newton(dve, link, y, v, t):
            link(nc.vector.tensor_tensor(t, y, y, ALU.mult))
            link(nc.vector.tensor_tensor(t, t, v, ALU.mult))
            link(nc.vector.tensor_scalar(t, t, -0.5, 1.5, ALU.mult, ALU.add))
            link(nc.vector.tensor_tensor(y, y, t, ALU.mult))

        def row_stats(dve, link, src):
            for i in range(TILES):
                ins = nc.vector.bn_stats(st[:, i, :], src(i))
            link(ins)
            for i in range(TILES):
                ins = nc.vector.bn_aggr(mv[:, i, :], st[:, i, :])
            link(ins)
            link(nc.vector.tensor_scalar(ve[:, :], mv[:, :, 1], LN_EPS, None, ALU.add))

        W_DMAS = [0]
        with nc.Block() as block:
            @block.sync
            def _(sp):
                for b in range(B):
                    sp.dma_start(x[:, b * QB:(b + 1) * QB, :],
                                 X[b].rearrange("(t p) d -> p t d", p=P)).then_inc(s_x, 16)
                row = lambda v: v.rearrange("(a n) -> a n", a=1)
                col = lambda v: v.rearrange("(d a) -> d a", a=1)
                loads = [(w_rows[:, 2 * w + t, :], W[t * P:(t + 1) * P, :])
                         for w, W in enumerate((Wq, Wk, Wv)) for t in range(2)]
                loads += [(w_rows[:, 6 + t, :], Wo[:, t * P:(t + 1) * P]) for t in range(2)]
                loads += [(o_scale[r * 2 * DH:(r + 1) * 2 * DH, :], col(rms_scale)) for r in range(P // (2 * DH))]
                loads += [(lam_in[:, i, :], L.rearrange("h d -> (h d)").rearrange("(a n) -> a n", a=1)
                           .to_broadcast([P, H * DH])) for i, L in enumerate((lq1, lq2, lk1, lk2))]
                loads += [(route_row[:, :], row(route).to_broadcast([P, D])),
                          (w1[:, 0:LIGHT], w1_l), (w1[:, LIGHT:], w1_h),
                          (gam[:, 0:1], col(g_l)), (gam[:, 1:2], col(g_h)),
                          (b1c[0:LIGHT, 0:1], col(b1_l)), (b1c[:, 1:], b1_h.rearrange("(c p) -> p c", p=P)),
                          (w2h[:, :, :], w2_h.rearrange("(c p) d -> p c d", p=P)), (w2l[:, :], w2_l),
                          (b2[:, 0, :], row(b2_l).to_broadcast([P, D])),
                          (b2[:, 1, :], row(b2_h).to_broadcast([P, D]))]
                for dst, src in loads:
                    sp.dma_start(dst, src).then_inc(s_w, 16)
                W_DMAS[0] = 16 * len(loads)

            @block.gpsimd
            def _(pool):
                nc.gpsimd.memset(ident[:, :], 0.0).then_inc(s_const, 1)
                nc.gpsimd.memset(ident_bf[:, :], 0.0).then_inc(s_const, 1)
                nc.gpsimd.memset(causal_bf[:, :], 0.0).then_inc(s_const, 1)
                nc.gpsimd.memset(eps_col[:, :], LN_EPS).then_inc(s_const, 1)
                nc.gpsimd.memset(shift_col[:, :], 0.5 * LOG_SHIFT * LN2).then_inc(s_const, 1)
                pool.wait_ge(s_const, 5)
                for tile, op, fill in ((ident, ALU.not_equal, 1.0), (ident_bf, ALU.not_equal, 1.0),
                                       (causal_bf, ALU.is_ge, NEG)):
                    nc.gpsimd.affine_select(out=tile[:, :], in_=tile[:, :], compare_op=op, fill=fill, base=0,
                                            pattern=[[-1, P]], channel_multiplier=1).then_inc(s_const, 1)

            @block.tensor
            def _(pe):
                pe.wait_ge(s_const, 8)
                pe.wait_ge(s_w, W_DMAS[0])
                for i in range(8):
                    ins = nc.tensor.transpose(psum[:, i // 4, (i % 4) * P:(i % 4 + 1) * P], w_rows[:, i, :], ident[:, :])
                ins.then_inc(s_wt, 1)

            @block.vector
            def _(dve):
                link = dve_chain(dve)
                dve.wait_ge(s_w, W_DMAS[0])
                link(nc.vector.tensor_tensor(lam_prod[:, :, :], lam_in[:, 0:2, :], lam_in[:, 2:4, :], ALU.mult))
                nc.vector.tensor_reduce(lam_sum[:, :, :], lam_prod[:, :, :].rearrange("p a (h d) -> p a h d", d=DH),
                                        AX.X, ALU.add).then_inc(s_stat, 1)
                link(nc.vector.tensor_scalar(o_scale[:, :], o_scale[:, :], 1.0 - LAMBDA_INIT, None, ALU.mult))
                nc.vector.tensor_scalar(w1g[:, 0:LIGHT], w1[:, 0:LIGHT], gam[:, 0:1], None, ALU.mult)
                nc.vector.tensor_scalar(w1g[:, LIGHT:], w1[:, LIGHT:], gam[:, 1:2], None, ALU.mult)
                dve.wait_ge(s_wt, 1)
                nc.vector.tensor_copy(w_qkv[:, :, :].rearrange("p a n -> p (a n)"),
                                      psum[:, 0:2, :].rearrange("p a n -> p (a n)")[:, 0:6 * P])
                nc.vector.tensor_scalar(w_o[:, :, :], psum[:, 1, 2 * P:4 * P].rearrange("p (a n) -> p a n", a=2),
                                        o_scale[:, 0:1], None, ALU.mult)
                dve.wait_ge(s_x, 16 * B)
                row_stats(dve, link, lambda i: x[:, i, :])
                nc.vector.memset(coef[:, :, 0], 1.0).then_inc(s_stat, 1)
                dve.wait_ge(s_exp0, 2)
                newton(dve, link, rs[:, :], ve[:, :], tn[:, :])
                link(nc.vector.tensor_tensor(coef[:, :, 1], lam_sum[:, 1, :], lam_sum[:, 0, :], ALU.subtract))
                link(nc.vector.tensor_scalar(coef[:, :, 1], coef[:, :, 1], -LAMBDA_INIT, None, ALU.add))
                dve_steps[0] += link.n

            @block.scalar
            def _(act):
                act.wait_ge(s_stat, 1)
                nc.scalar.activation(lam_sum[:, :, :], lam_sum[:, :, :], ACT.Exp).then_inc(s_exp0, 1)
                act.wait_ge(s_stat, 2)
                nc.scalar.activation(lg[:, :], ve[:, :], ACT.Ln).then_inc(s_log, 1)
                act.wait_ge(s_log, 1)
                nc.scalar.activation(rs[:, :], lg[:, :], ACT.Exp, scale=-0.5).then_inc(s_exp0, 1)

        s_xn = sem("s_xn")
        s_xt = sem("s_xt")
        s_xtc = sem("s_xtc")
        s_proj = sem("s_proj")
        s_hi = sem("s_hi")
        s_res = sem("s_res")
        s_mid = sem("s_mid")
        s_res2 = sem("s_res2")
        s_low = sem("s_low")
        s_vp = sem("s_vp")
        s_v = sem("s_v")
        s_ones = sem("s_ones")
        s_qk_out = sem("s_qk_out")
        s_v_out = sem("s_v_out")
        QK_OUT = 2 * SPLITS * 2 * 16
        with ExitStack() as local:
            def tmp(name, shape, dt=F32):
                return local.enter_context(nc.sbuf_tensor(name, shape, dt))
            xn = tmp("xn", [P, 2, QB, D])
            xn_t = tmp("xn_t", [P, 2, N])
            parts = tmp("parts", [P, 4, 3, N], BF16)
            res = tmp("res", [P, 4, N])
            v_out = tmp("v_out", [P, PAIRS, QB, 2, HV])
            block = local.enter_context(nc.Block())

            @block.gpsimd
            def _(pool):
                nc.gpsimd.memset(v_out[:, :, :, :, :], 1.0).then_inc(s_ones, 1)
                with pool.Fori(0, B) as b:
                    for i in range(4):
                        pool.wait_ge(s_res, 4 * b + i + 1)
                        pool.sem_inc(s_pool_go, 1)
                        nc.gpsimd.tensor_copy(parts[:, i, 1, :], res[:, i, :]).then_inc(s_mid, 1)
                        pool.wait_ge(s_mid, 4 * b + i + 1)
                        nc.gpsimd.tensor_tensor(parts[:, i, 2, :], res[:, i, :], parts[:, i, 1, :],
                                                ALU.subtract).then_inc(s_low, 1)

            @block.vector
            def _(dve):
                with dve.Fori(0, B) as b:
                    for t in range(QB):
                        i = b * QB + t
                        nc.vector.tensor_scalar(xn[:, 0, t, :], x[:, i, :], mv[:, i, 0:1], rs[:, bass.ds(i, 1)],
                                                ALU.subtract, ALU.mult).then_inc(s_xn, 1)
                    for i in range(4):
                        dve.wait_ge(s_hi, 4 * b + i + 1)
                        nc.vector.tensor_tensor(res[:, i, :], psum[:, 1 + i, :], parts[:, i, 0, :],
                                                ALU.subtract).then_inc(s_res, 1)
                    for t in range(QB):
                        if t == 0:
                            dve.wait_ge(s_ones, 1)
                        dve.wait_ge(s_vp, QB * b + (t | 1) + 1)
                        nc.vector.tensor_copy(
                            v_out[:, :, t, :, 0:2 * DH],
                            psum[:, 5 + t // 2, (t % 2) * D2:(t % 2 + 1) * D2]
                            .rearrange("p (a h d) -> p a h d", a=PAIRS, h=2)).then_inc(s_v, 1)
                    dve.wait_ge(s_qk_out, QK_OUT * (b + 1))
                    dve.wait_ge(s_v_out, 16 * (b + 1))

            @block.tensor
            def _(pe):
                with pe.Fori(0, B) as b:
                    pe.wait_ge(s_xn, QB * (b + 1))
                    for t in range(QB):
                        ins = nc.tensor.transpose(psum[:, 0, t * P:(t + 1) * P], xn[:, 0, t, :], ident[:, :])
                    ins.then_inc(s_xt, 1)
                    pe.wait_ge(s_xtc, b + 1)
                    for i in range(4):
                        nc.tensor.matmul(psum[:, 1 + i, :], w_qkv[:, i, :], xn_t[:, 0, :],
                                         start=True, stop=True).then_inc(s_proj, 1)
                    for t in range(QB):
                        nc.tensor.matmul(psum[:, 5 + t // 2, (t % 2) * D2:(t % 2 + 1) * D2],
                                         xn_t[:, 0, t * P:(t + 1) * P],
                                         w_qkv[:, 4:6, :].rearrange("p a n -> p (a n)"),
                                         start=True, stop=True).then_inc(s_vp, 1)
                    pe.wait_ge(s_res, 4 * (b + 1))
                    pe.wait_ge(s_v, QB * (b + 1))

            @block.scalar
            def _(act):
                with act.Fori(0, B) as b:
                    act.wait_ge(s_xt, b + 1)
                    nc.scalar.copy(xn_t[:, 0, :], psum[:, 0, :]).then_inc(s_xtc, 1)
                    for i in range(4):
                        act.wait_ge(s_proj, 4 * b + i + 1)
                        nc.scalar.copy(parts[:, i, 0, :], psum[:, 1 + i, :]).then_inc(s_hi, 1)
                    act.wait_ge(s_qk_out, QK_OUT * (b + 1))

            @block.sync
            def _(sp):
                with sp.Fori(0, B) as b:
                    sp.wait_ge(s_low, 4 * (b + 1))
                    for which, dram, order in ((0, q_dram, Q_PARTS), (1, k_dram, K_PARTS)):
                        for j, part in enumerate(order):
                            for t in range(2):
                                sp.dma_start(dram[b, t * H:(t + 1) * H, j * DH:(j + 1) * DH, :],
                                             parts[:, 2 * which + t, part, :]).then_inc(s_qk_out, 16)
                    sp.wait_ge(s_v, QB * (b + 1))
                    sp.dma_start(v_dram[b], v_out[:, :, :, :, :].rearrange("p a t h v -> p a (t h v)"))\
                      .then_inc(s_v_out, 16)
                sp.wait_ge(s_qk_out, QK_OUT * B)
                sp.wait_ge(s_v_out, 16 * B)

        s_load = [sem(f"s_load{p}") for p in range(PAIRS)]
        s_vload = [sem(f"s_vload{p}") for p in range(PAIRS)]
        s_mrow = [sem(f"s_mrow{p}") for p in range(PAIRS)]
        s_kones = sem("s_kones")
        s_score = sem("s_score")
        s_prob = sem("s_prob")
        s_masked = sem("s_masked")
        s_pv = sem("s_pv")
        s_pvc = sem("s_pvc")
        s_ot = sem("s_ot")
        s_oh = sem("s_oh")
        s_rec = sem("s_rec")
        s_recl = sem("s_recl")
        s_o = sem("s_o")
        s_ring = sem("s_ring")
        s_ringc = sem("s_ringc")
        s_msplit = sem("s_msplit")
        s_mchain = sem("s_mchain")
        EXP_BANK, RING, PV_BANK, OT_BANK = (0, 2), (4, 5), 6, 7
        GROUP_CELLS = (
            ((0, 0, 0, 0), (1, 0, 1, 0)),
            ((2, 0, 0, 0), (3, 0, 1, 0)),
            ((0, 1, 0, 0), (0, 3, 0, 384), (1, 1, 1, 0), (1, 3, 1, 384)),
            ((2, 1, 0, 0), (2, 3, 0, 384), (3, 1, 1, 0), (3, 3, 1, 384)),
            ((0, 2, 0, 0), (2, 2, 0, 256), (1, 2, 1, 0), (3, 2, 1, 256)))
        MAX_TILES = tuple(((c, 3, 0),) for c in range(4)) + tuple(((c, 2, 0), (c, 0, 384)) for c in range(4)) \
            + (((0, 1, 0), (2, 1, 256)), ((1, 1, 0), (3, 1, 256)))
        MT = len(MAX_TILES)
        STEP_TILES = []
        for step in range(PAIRS + 1):
            tiles = []
            if step >= 1:
                tiles += [("m", step - 1, k) for k in range(MT)]
            if step >= 2:
                tiles.insert(8, ("t", step - 2, 0))
            if step == PAIRS:
                tiles.append(("t", PAIRS - 1, 0))
            STEP_TILES.append(tiles)
        RING_ORDER = [t for tiles in STEP_TILES for t in tiles]
        RING_N = len(RING_ORDER)
        RING_AT = {t: i for i, t in enumerate(RING_ORDER)}

        with ExitStack() as local:
            def tmp(name, shape, dt=F32):
                return local.enter_context(nc.sbuf_tensor(name, shape, dt))
            q_st = tmp("q_st", [P, 2 * PAIRS, N], BF16)
            k_st = tmp("k_st", [P, 2 * PAIRS, N], BF16)
            v_aug = tmp("v_aug", [P, PAIRS, QB * 2 * HV])
            probs = tmp("probs", [P, 2, GROUPS, 2, N])
            nmax = tmp("nmax", [P, 2, QB, 4])
            nres = tmp("nres", [P, 2, QB, 4])
            nparts = tmp("nparts", [P, 2, QB, 4, 3], BF16)
            nrow = tmp("nrow", [12, 2, N], BF16)
            o_t = tmp("o_t", [P, N])
            recip = tmp("recip", [P, QB, 4])
            o_half = tmp("o_half", [P, 2, QB, 4, 2 * DH])
            block = local.enter_context(nc.Block())

            def rows(pair, c):
                return 64 * (c % 2), 2 * pair + c // 2

            @block.sync
            def _(sp):
                def load(b, p, wait_b=None):
                    if wait_b is not None:
                        sp.wait_ge(s_score, GROUPS * (PAIRS * wait_b + p + 1))
                    for half in range(2):
                        for tile, dram in ((q_st, q_dram), (k_st, k_dram)):
                            sp.dma_start(tile[64 * half:64 * half + KR, 2 * p:2 * p + 2, :],
                                         dram[b, 4 * p + half:4 * p + half + 3:2].rearrange("s r n -> r s n"))\
                              .then_inc(s_load[p], 16)

                def load_v(b, p, wait_b=None):
                    if wait_b is not None:
                        sp.wait_ge(s_pv, PAIRS * wait_b + p + 1)
                    sp.dma_start(v_aug[:, p, :], v_dram[b, :, p, :]).then_inc(s_vload[p], 16)

                def max_rows(b, p):
                    sp.wait_ge(s_ringc, RING_N * b + RING_AT[("t", p, 0)] + 1)
                    for c in range(4):
                        r0, s = rows(p, c)
                        sp.dma_start(q_st[r0 + KR:r0 + KM, s, :], nrow[3 * c:3 * c + 3, p % 2, :])\
                          .then_inc(s_mrow[p], 16)

                sp.wait_ge(s_kones, 1)
                for p in range(PAIRS):
                    load(0, p)
                    load_v(0, p)
                for p in range(PAIRS):
                    max_rows(0, p)
                with sp.Fori(0, B - 1) as b:
                    for step in range(PAIRS + 1):
                        if step < PAIRS:
                            load(b + 1, step, b)
                        if step >= 2:
                            max_rows(b + 1, step - 2)
                        if step >= 1:
                            load_v(b + 1, step - 1, b)
                    max_rows(b + 1, PAIRS - 1)

            @block.gpsimd
            def _(pool):
                nc.gpsimd.memset(k_st[:, :, :], 1.0).then_inc(s_kones, 1)

                def split_max(b, p, n):
                    last = [t for t in RING_ORDER if t[0] == "m" and t[1] == p][-1]
                    pool.wait_ge(s_ringc, RING_N * b + RING_AT[last] + 1)
                    if n is not None:
                        pool.wait_ge(s_ring, n)
                    link = Chain(pool, s_mchain, 4 * (PAIRS * b + p))
                    pool.sem_inc(s_pool_go, 1)
                    a, r, o = nmax[:, p % 2], nres[:, p % 2], nparts[:, p % 2]
                    link(nc.gpsimd.tensor_copy(o[:, :, :, 0], a))
                    link(nc.gpsimd.tensor_tensor(r, a, o[:, :, :, 0], ALU.subtract))
                    pool.sem_inc(s_pool_go, 1)
                    link(nc.gpsimd.tensor_copy(o[:, :, :, 1], r))
                    link(nc.gpsimd.tensor_tensor(r, r, o[:, :, :, 1], ALU.subtract))
                    pool.sem_inc(s_pool_go, 1)
                    nc.gpsimd.tensor_copy(o[:, :, :, 2], r).then_inc(s_msplit, 1)

                def mask(b, p, g):
                    pool.wait_ge(s_prob, GROUPS * (PAIRS * b + p) + g + 1)
                    cells = probs[:, p % 2, g]
                    if g < 2:
                        views = (cells[:, :, 0:P],)
                    elif g < 4:
                        views = (cells[:, :, 0:P], cells[:, :, 3 * P:4 * P])
                    else:
                        views = (cells.rearrange("p a (k n) -> p (a k) n", n=2 * P)[:, :, 0:P],)
                    pool.sem_inc(s_pool_go, 1)
                    for v in views:
                        ins = nc.gpsimd.affine_select(out=v, in_=v, compare_op=ALU.is_ge, fill=0.0, base=0,
                                                      pattern=[[0, v.shape[1]], [1, P]], channel_multiplier=-1)
                    ins.then_inc(s_masked, 1)

                def join(b, p):
                    pool.wait_ge(s_oh, PAIRS * b + p + 1)
                    oh = o_half[:, p % 2].rearrange("p t (h a) d -> p t h a d", a=2)
                    nc.gpsimd.tensor_tensor(attn[:, b, :, 2 * p:2 * p + 2, :], oh[:, :, :, 0, :], oh[:, :, :, 1, :],
                                            ALU.add).then_inc(s_o, 1)

                for p in range(PAIRS):
                    split_max(0, p, None if p < 2 else RING_AT[("t", p - 2, 0)] + 1)

                def body(b, more):
                    for p in range(PAIRS):
                        for g in range(GROUPS):
                            mask(b, p, g)
                        if more and p >= 1:
                            split_max(b + 1, p - 1, RING_N * (b + 1) + RING_AT[("t", p - 3, 0)] + 1 if p >= 3
                                      else RING_N * (b + 1))
                        if p >= 1:
                            join(b, p - 1)
                    if more:
                        split_max(b + 1, PAIRS - 1, RING_N * (b + 1) + RING_AT[("t", PAIRS - 3, 0)] + 1)
                    join(b, PAIRS - 1)

                body(0, True)
                with pool.Fori(1, B - 1) as b:
                    body(b, True)
                body(B - 1, False)

            @block.tensor
            def _(pe):
                def ring_tile(b, tile):
                    n = RING_AT[tile]
                    kind, p, k = tile
                    bank = psum[:, RING[n % 2], :]
                    if n >= 2 or not isinstance(b, int) or b >= 1:
                        pe.wait_ge(s_ringc, RING_N * b + n - 1)
                    if kind == "t":
                        pe.wait_ge(s_msplit, PAIRS * b + p + 1)
                        dst = bank.bitcast(BF16)
                        for t in range(QB):
                            ins = nc.tensor.transpose(dst[0:12, t * P:(t + 1) * P],
                                                      nparts[:, p % 2, t].rearrange("p c a -> p (c a)"),
                                                      ident_bf[:, :])
                        ins.then_inc(s_ring, 1)
                        return
                    if k == 0:
                        pe.wait_ge(s_load[p], 64 * (b + 1))
                    cells = MAX_TILES[k]
                    for c, qb, col in cells:
                        r0, s = rows(p, c)
                        nc.tensor.matmul(bank[:, col:col + (qb + 1) * P],
                                         q_st[r0:r0 + KR, s, qb * P:(qb + 1) * P],
                                         k_st[r0:r0 + KR, s, 0:(qb + 1) * P], start=True, stop=False)
                        ins = nc.tensor.matmul(bank[:, col + qb * P:col + (qb + 1) * P], ident_bf[:, :],
                                               causal_bf[:, :], start=False, stop=True)
                    ins.then_inc(s_ring, 1)

                def scores(b, p, g):
                    n = GROUPS * (PAIRS * b + p) + g
                    if g == 0:
                        pe.wait_ge(s_mrow[p], 64 * (b + 1))
                    if not isinstance(n, int) or n >= 2:
                        pe.wait_ge(s_prob, n - 1)
                    base = EXP_BANK[(GROUPS * p + g) % 2]
                    for c, kb, bank, col in GROUP_CELLS[g]:
                        r0, s = rows(p, c)
                        ins = nc.tensor.matmul(psum[:, base + bank, col:col + N - kb * P],
                                               k_st[r0:r0 + KM, s, kb * P:(kb + 1) * P],
                                               q_st[r0:r0 + KM, s, kb * P:N], start=True, stop=True)
                    ins.then_inc(s_score, 1)

                def values(b, p, part):
                    if part == 0:
                        pe.wait_ge(s_vload[p], 16 * (b + 1))
                        n = PAIRS * b + p
                        if not isinstance(n, int) or n >= 1:
                            pe.wait_ge(s_pvc, n)
                    groups = ((0, 1), (2, 3), (4,))[part]
                    pe.wait_ge(s_masked, GROUPS * (PAIRS * b + p) + groups[-1] + 1)
                    for kb in ((0,), (1, 3), (2,))[part]:
                        for c in range(4):
                            g, bank, col = [(g, bank, col) for g in groups
                                            for cc, k, bank, col in GROUP_CELLS[g] if (cc, k) == (c, kb)][0]
                            v = v_aug[:, p, :].rearrange("p (t h v) -> p t h v", t=QB, h=2)[:, kb, c // 2, :]
                            ins = nc.tensor.matmul(psum[32 * c:32 * c + HV, PV_BANK, kb * P:N], v,
                                                   probs[:, p % 2, g, bank, col:col + N - kb * P],
                                                   start=(kb == 0), stop=(kb == 2), tile_position=(0, 32 * c),
                                                   skip_group_check=True)
                    if part == 2:
                        ins.then_inc(s_pv, 1)

                def o_transpose(b, p):
                    n = PAIRS * b + p
                    pe.wait_ge(s_pvc, n + 1)
                    if not isinstance(n, int) or n >= 1:
                        pe.wait_ge(s_oh, n)
                    for t in range(QB):
                        ins = nc.tensor.transpose(psum[:, OT_BANK, t * P:(t + 1) * P], o_t[:, t * P:(t + 1) * P],
                                                  ident[:, :])
                    ins.then_inc(s_ot, 1)

                for tiles in STEP_TILES:
                    for tile in tiles:
                        ring_tile(0, tile)

                def body(b, more):
                    for p in range(PAIRS):
                        tiles = list(STEP_TILES[p]) if more else []
                        for g in range(GROUPS):
                            scores(b, p, g)
                            if p >= 1 and g in (1, 2, 3):
                                values(b, p - 1, g - 1)
                            for _ in range(3 if g == 3 else 2):
                                if tiles:
                                    ring_tile(b + 1, tiles.pop(0))
                        if p >= 1:
                            o_transpose(b, p - 1)
                        assert not tiles
                    tiles = list(STEP_TILES[PAIRS]) if more else []
                    for part in range(3):
                        for _ in range(3):
                            if tiles:
                                ring_tile(b + 1, tiles.pop(0))
                        values(b, PAIRS - 1, part)
                    for tile in tiles:
                        ring_tile(b + 1, tile)
                    o_transpose(b, PAIRS - 1)

                body(0, True)
                with pe.Fori(1, B - 1) as b:
                    body(b, True)
                body(B - 1, False)

            @block.scalar
            def _(act):
                def body(b):
                    for p in range(PAIRS):
                        for g in range(GROUPS):
                            n = GROUPS * (PAIRS * b + p) + g
                            act.wait_ge(s_score, n + 1)
                            if g == 0:
                                k = PAIRS * b + p - 1
                                if not isinstance(k, int) or k >= 1:
                                    act.wait_ge(s_pv, k)
                            base = EXP_BANK[(GROUPS * p + g) % 2]
                            nc.scalar.activation(probs[:, p % 2, g], psum[:, base:base + 2, :], ACT.Exp,
                                                 scale=SCALE).then_inc(s_prob, 1)
                body(0)
                with act.Fori(1, B) as b:
                    body(b)

            @block.vector
            def _(dve):
                def ring_tile(b, tile):
                    n = RING_AT[tile]
                    kind, p, k = tile
                    bank = psum[:, RING[n % 2], :]
                    dve.wait_ge(s_ring, RING_N * b + n + 1)
                    if kind == "t":
                        if p >= 2:
                            dve.wait_ge(s_mrow[p - 2], 64 * (b + 1))
                        elif not isinstance(b, int) or b >= 1:
                            dve.wait_ge(s_mrow[PAIRS - 2 + p], 64 * b)
                        nc.vector.tensor_copy(nrow[:, p % 2, :], bank.bitcast(BF16)[0:12, 0:N]).then_inc(s_ringc, 1)
                        return
                    m = nmax[:, p % 2]
                    if k == 0:
                        if p >= 2:
                            dve.wait_ge(s_msplit, PAIRS * b + p - 1)
                        elif not isinstance(b, int) or b >= 1:
                            dve.wait_ge(s_msplit, PAIRS * b + p - 1)
                    cells = MAX_TILES[k]
                    if len(cells) == 2 and cells[0][1] == cells[1][1]:
                        c, qb, _ = cells[0]
                        ins = nc.vector.tensor_reduce(m[:, qb, c:c + 3:2], bank.rearrange("p (a n) -> p a n", a=2),
                                                      AX.X, ALU.max, negate=True)
                    else:
                        for c, qb, col in cells:
                            ins = nc.vector.tensor_reduce(m[:, qb, c:c + 1], bank[:, col:col + (qb + 1) * P],
                                                          AX.X, ALU.max, negate=True)
                    ins.then_inc(s_ringc, 1)

                def pv_copy(b, p):
                    n = PAIRS * b + p
                    dve.wait_ge(s_pv, n + 1)
                    if not isinstance(n, int) or n >= 1:
                        dve.wait_ge(s_ot, n)
                    nc.vector.tensor_copy(o_t[:, :], psum[:, PV_BANK, :]).then_inc(s_pvc, 1)

                def normalise(b, p):
                    n = PAIRS * b + p
                    dve.wait_ge(s_ot, n + 1)
                    ot = psum[:, OT_BANK, :].rearrange("p (t c v) -> p t c v", t=QB, c=4)
                    nc.vector.reciprocal(recip[:, :, :], ot[:, :, :, 2 * DH]).then_inc(s_rec, 1)
                    dve.wait_ge(s_rec, n + 1)
                    cf = coef[:, 2 * p:2 * p + 2, :].rearrange("p h a -> p (h a)")[:, None, :].to_broadcast([P, QB, 4])
                    nc.vector.tensor_tensor(recip[:, :, :], recip[:, :, :], cf, ALU.mult).then_inc(s_recl, 1)
                    dve.wait_ge(s_recl, n + 1)
                    if not isinstance(n, int) or n >= 2:
                        dve.wait_ge(s_o, n - 1)
                    nc.vector.tensor_tensor(o_half[:, p % 2], ot[:, :, :, 0:2 * DH],
                                            recip[:, :, :, None].to_broadcast([P, QB, 4, 2 * DH]),
                                            ALU.mult).then_inc(s_oh, 1)

                nc.vector.memset(psum[:, PV_BANK, :], 0.0)
                for tiles in STEP_TILES:
                    for tile in tiles:
                        ring_tile(0, tile)

                def body(b, more):
                    for p in range(PAIRS):
                        tiles = list(STEP_TILES[p]) if more else []
                        for g in range(GROUPS):
                            if p >= 1 and g == 3:
                                pv_copy(b, p - 1)
                            for _ in range(3 if g == 3 else 2):
                                if tiles:
                                    ring_tile(b + 1, tiles.pop(0))
                        if p >= 1:
                            normalise(b, p - 1)
                    tiles = list(STEP_TILES[PAIRS]) if more else []
                    for _ in range(9):
                        if tiles:
                            ring_tile(b + 1, tiles.pop(0))
                    pv_copy(b, PAIRS - 1)
                    for tile in tiles:
                        ring_tile(b + 1, tile)
                    normalise(b, PAIRS - 1)

                body(0, True)
                with dve.Fori(1, B - 1) as b:
                    body(b, True)
                body(B - 1, False)

        s_sq = sem("s_sq")
        s_ss = sem("s_ss")
        s_hl = sem("s_hl")
        s_hr = sem("s_hr")
        s_hn = sem("s_hn")
        s_hng = sem("s_hng")
        s_at = sem("s_at")
        s_atc = sem("s_atc")
        s_op = sem("s_op")
        s_opc = sem("s_opc")
        s_ln = sem("s_ln")
        HR = B * QB * H
        with ExitStack() as local:
            def tmp(name, shape, dt=F32):
                return local.enter_context(nc.sbuf_tensor(name, shape, dt))
            sq = tmp("sq", [P, 2, QB, H, 2 * DH])
            hv = tmp("hv", [P, HR])
            hy = tmp("hy", [P, HR])
            ht = tmp("ht", [P, HR])
            a_t = tmp("a_t", [P, 2, 2, N])
            ao = tmp("ao", [P, TILES, D])
            block = local.enter_context(nc.Block())

            @block.gpsimd
            def _(pool):
                for b in range(B):
                    if b >= 2:
                        pool.wait_ge(s_ss, b - 1)
                    nc.gpsimd.tensor_tensor(sq[:, b % 2], attn[:, b], attn[:, b], ALU.mult).then_inc(s_sq, 1)
                pool.wait_ge(s_hn, 1)
                for b in range(B):
                    r = hy[:, b * QB * H:(b + 1) * QB * H].rearrange("p (t h) -> p t h", t=QB)
                    nc.gpsimd.tensor_tensor(attn[:, b], attn[:, b],
                                            r[:, :, :, None].to_broadcast([P, QB, H, 2 * DH]),
                                            ALU.mult).then_inc(s_hng, 1)

            @block.scalar
            def _(act):
                act.wait_ge(s_ss, B + 1)
                nc.scalar.activation(hy[:, :], hv[:, :], ACT.Ln).then_inc(s_hl, 1)
                act.wait_ge(s_hl, 1)
                nc.scalar.activation(hy[:, :], hy[:, :], ACT.Exp, scale=-0.5).then_inc(s_hr, 1)
                for b in range(B):
                    act.wait_ge(s_at, b + 1)
                    if b >= 2:
                        act.wait_ge(s_op, b - 1)
                    base = 4 * (b % 2)
                    nc.scalar.copy(a_t[:, b % 2], psum[:, base:base + 2, :]).then_inc(s_atc, 1)
                act.wait_ge(s_ln, 1)
                nc.scalar.activation(lg[:, :], ve[:, :], ACT.Ln).then_inc(s_hl, 1)
                act.wait_ge(s_hl, 2)
                nc.scalar.activation(rs[:, :], lg[:, :], ACT.Exp, scale=-0.5).then_inc(s_hr, 1)

            @block.tensor
            def _(pe):
                for b in range(B):
                    base = 4 * (b % 2)
                    pe.wait_ge(s_hng, b + 1)
                    if b >= 2:
                        pe.wait_ge(s_atc, b - 1)
                    for k in range(2):
                        for t in range(QB):
                            ins = nc.tensor.transpose(psum[:, base + k, t * P:(t + 1) * P],
                                                      attn[:, b, t].rearrange("p h d -> p (h d)")[:, k * P:(k + 1) * P],
                                                      ident[:, :])
                    ins.then_inc(s_at, 1)
                    pe.wait_ge(s_atc, b + 1)
                    if b >= 2:
                        pe.wait_ge(s_opc, b - 1)
                    for t in range(QB):
                        for k in range(2):
                            ins = nc.tensor.matmul(psum[:, base + 2, t * P:(t + 1) * P],
                                                   a_t[:, b % 2, k, t * P:(t + 1) * P], w_o[:, k, :],
                                                   start=(k == 0), stop=(k == 1))
                    ins.then_inc(s_op, 1)

            @block.vector
            def _(dve):
                link = dve_chain(dve)
                for b in range(B):
                    dve.wait_ge(s_sq, b + 1)
                    nc.vector.tensor_reduce(hv[:, b * QB * H:(b + 1) * QB * H],
                                            sq[:, b % 2].rearrange("p t h d -> p (t h) d"),
                                            AX.X, ALU.add).then_inc(s_ss, 1)
                dve.wait_ge(s_ss, B)
                nc.vector.tensor_scalar(hv[:, :], hv[:, :], 1.0 / (2 * DH), LN_EPS, ALU.mult, ALU.add)\
                  .then_inc(s_ss, 1)
                dve.wait_ge(s_hr, 1)
                link(nc.vector.tensor_tensor(ht[:, :], hy[:, :], hy[:, :], ALU.mult))
                link(nc.vector.tensor_tensor(ht[:, :], ht[:, :], hv[:, :], ALU.mult))
                link(nc.vector.tensor_scalar(ht[:, :], ht[:, :], -0.5, 1.5, ALU.mult, ALU.add))
                nc.vector.tensor_tensor(hy[:, :], hy[:, :], ht[:, :], ALU.mult).then_inc(s_hn, 1)
                for b in range(B):
                    dve.wait_ge(s_op, b + 1)
                    nc.vector.tensor_copy(ao[:, b * QB:(b + 1) * QB, :].rearrange("p t d -> p (t d)"),
                                          psum[:, 4 * (b % 2) + 2, :]).then_inc(s_opc, 1)
                dve.wait_ge(s_opc, B)
                row_stats(dve, link, lambda i: ao[:, i, :])
                nc.vector.memset(tn[:, :], 0.0).then_inc(s_ln, 1)
                dve.wait_ge(s_hr, 2)
                newton(dve, link, rs[:, :], ve[:, :], tn[:, :])
                for i in range(TILES):
                    ins = nc.vector.tensor_scalar(ao[:, i, :], ao[:, i, :], mv[:, i, 0:1], rs[:, i:i + 1],
                                                  ALU.subtract, ALU.mult)
                link(ins)
                link(nc.vector.tensor_tensor(x[:, :, :], x[:, :, :], ao[:, :, :], ALU.add))
                dve_steps[0] += link.n

        s_l2 = sem("s_l2")
        s_f1 = sem("s_f1")
        s_f2 = sem("s_f2")
        s_fy = sem("s_fy")
        s_xr = sem("s_xr")
        s_ft = sem("s_ft")
        s_ftc = sem("s_ftc")
        s_hid = sem("s_hid")
        s_gelu = sem("s_gelu")
        s_ff = sem("s_ff")
        s_ffc = sem("s_ffc")
        s_tu = sem("s_tu")
        s_tuc = sem("s_tuc")
        s_udma = sem("s_udma")
        s_r = sem("s_r")
        s_ra = sem("s_ra")
        s_zdone = sem("s_zdone")
        s_zt = sem("s_zt")
        s_ln2 = sem("s_ln2")
        s_out = sem("s_out")
        s_fin = sem("s_fin")
        with ExitStack() as local:
            def tmp(name, shape, dt=F32):
                return local.enter_context(nc.sbuf_tensor(name, shape, dt))
            xn2 = tmp("xn2", [P, TILES, D])
            prod = tmp("prod", [P, D])
            ss = tmp("ss", [P, TILES])
            u_col = tmp("u_col", [P, TILES])
            u_t = tmp("u_t", [TILES, P])
            xr_t = tmp("xr_t", [P, 2, N])
            hid = tmp("hid", [P, 2, 1 + HC, N])
            light = tmp("light", [P, TILES, D])
            heavy = tmp("heavy", [P, TILES, D])
            u = tmp("u", [B, N])
            z = tmp("z", [B, N])
            e = tmp("e", [B, N])
            f = tmp("f", [B, N])
            key = tmp("key", [B, 2, N])
            sel = tmp("sel", [B, N])
            top = tmp("top", [B, 8])
            umax = tmp("umax", [B, 1])
            zmax = tmp("zmax", [B, 1])
            zsum = tmp("zsum", [B, 1])
            beta = tmp("beta", [B, 1])
            nb = tmp("nb", [B, 1])
            ts = tmp("ts", [B, 1])
            tt = tmp("tt", [B, 1])
            wcol = tmp("wcol", [P, QB, B])
            block = local.enter_context(nc.Block())
            HID_BANKS = (1, 2, 3, 4)

            @block.scalar
            def _(act):
                act.wait_ge(s_l2, 1)
                nc.scalar.activation(lg[:, :], ve[:, :], ACT.Ln).then_inc(s_f1, 1)
                act.wait_ge(s_f1, 1)
                nc.scalar.activation(rs[:, :], lg[:, :], ACT.Exp, scale=-0.5).then_inc(s_f2, 1)
                act.wait_ge(s_l2, 2)
                nc.scalar.activation(lg[:, :], ss[:, :], ACT.Ln, scale=float(2 ** LOG_SHIFT)).then_inc(s_f1, 1)
                act.wait_ge(s_f1, 2)
                nc.scalar.activation(lg[:, :], lg[:, :], ACT.Exp, scale=-0.5, bias=shift_col[:, 0:1])\
                   .then_inc(s_f2, 1)
                def log_sum(n):
                    act.wait_ge(s_r, 3 * n + 1)
                    nc.scalar.activation(e[:, :], z[:, :], ACT.Exp, accum_out=zsum[:, :]).then_inc(s_ra, 1)
                    act.wait_ge(s_ra, 3 * n + 1)
                    nc.scalar.activation(zsum[:, :], zsum[:, :], ACT.Ln).then_inc(s_ra, 1)
                act.wait_ge(s_r, 1)
                nc.scalar.activation(e[:, :], z[:, :], ACT.Exp, accum_out=zsum[:, :]).then_inc(s_ra, 1)
                act.wait_ge(s_ra, 1)
                nc.scalar.activation(ts[:, :], zsum[:, :], ACT.Ln).then_inc(s_ra, 1)
                for r in range(REBASES):
                    act.wait_ge(s_r, 2 + 2 * r)
                    nc.scalar.activation(f[:, :], z[:, :], ACT.Exp).then_inc(s_ra, 1)
                    act.wait_ge(s_r, 3 + 2 * r)
                    nc.scalar.activation(ts[:, :], tt[:, :], ACT.Ln).then_inc(s_ra, 1)
                act.wait_ge(s_r, 2 + 2 * REBASES)
                nc.scalar.activation(e[:, :], z[:, :], ACT.Exp).then_inc(s_ra, 1)
                for b in range(B):
                    for c in range(1 + HC):
                        act.wait_ge(s_hid, (1 + HC) * b + c + 1)
                        if b >= 2 and c == 0:
                            act.wait_ge(s_ff, b - 1)
                        m = LIGHT if c == 0 else P
                        nc.scalar.activation(hid[0:m, b % 2, c, :], psum[0:m, HID_BANKS[((1 + HC) * b + c) % 4], :],
                                             ACT.Gelu, bias=b1c[0:m, c:c + 1]).then_inc(s_gelu, 1)
                act.wait_ge(s_ln2, 1)
                nc.scalar.activation(lg[:, :], ve[:, :], ACT.Ln).then_inc(s_f1, 1)
                act.wait_ge(s_f1, 3)
                nc.scalar.activation(rs[:, :], lg[:, :], ACT.Exp, scale=-0.5).then_inc(s_f2, 1)

            @block.tensor
            def _(pe):
                pe.wait_ge(s_fy, 1)
                nc.tensor.transpose(psum[0:TILES, 7, 0:P], u_col[:, :], ident[:, :]).then_inc(s_tu, 1)
                for b in range(B):
                    pe.wait_ge(s_xr, b + 1)
                    if b >= 1:
                        pe.wait_ge(s_ftc, b)
                    for t in range(QB):
                        ins = nc.tensor.transpose(psum[:, 0, t * P:(t + 1) * P], xn2[:, b * QB + t, :], ident[:, :])
                    ins.then_inc(s_ft, 1)
                    pe.wait_ge(s_ftc, b + 1)
                    for c in range(1 + HC):
                        n = (1 + HC) * b + c
                        if n >= 4:
                            pe.wait_ge(s_gelu, n - 3)
                        m = LIGHT if c == 0 else P
                        w0 = 0 if c == 0 else LIGHT + (c - 1) * P
                        nc.tensor.matmul(psum[0:m, HID_BANKS[n % 4], :], w1g[:, w0:w0 + m], xr_t[:, b % 2, :],
                                         start=True, stop=True).then_inc(s_hid, 1)
                    pe.wait_ge(s_gelu, (1 + HC) * (b + 1))
                    if b >= 1:
                        pe.wait_ge(s_ffc, b)
                    for t in range(QB):
                        nc.tensor.matmul(psum[:, 5, t * P:(t + 1) * P], hid[0:LIGHT, b % 2, 0, t * P:(t + 1) * P],
                                         w2l[:, :], start=True, stop=True)
                        for c in range(HC):
                            ins = nc.tensor.matmul(psum[:, 6, t * P:(t + 1) * P],
                                                   hid[:, b % 2, 1 + c, t * P:(t + 1) * P], w2h[:, c, :],
                                                   start=(c == 0), stop=(c == HC - 1))
                    ins.then_inc(s_ff, 1)
                pe.wait_ge(s_zdone, 1)
                for t in range(QB):
                    ins = nc.tensor.transpose(psum[:, 7, t * B:(t + 1) * B], sel[:, t * P:(t + 1) * P],
                                              ident[0:B, 0:B])
                ins.then_inc(s_zt, 1)

            @block.gpsimd
            def _(pool):
                for b in range(B):
                    pool.wait_ge(s_ft, b + 1)

            @block.sync
            def _(sp):
                sp.wait_ge(s_tuc, 1)
                sp.dma_start(u_dram[:, :], u_t[:, :]).then_inc(s_udma, 16)
                sp.wait_ge(s_udma, 16)
                sp.dma_start(u[:, :], u_dram.rearrange("(b t) p -> b (t p)", b=B)).then_inc(s_udma, 16)
                for b in range(B):
                    sp.wait_ge(s_fin, b + 1)
                    sp.dma_start(out[b].rearrange("(t p) d -> p t d", p=P), heavy[:, b * QB:(b + 1) * QB, :])\
                      .then_inc(s_out, 16)
                sp.wait_ge(s_out, 16 * B)

            @block.vector
            def _(dve):
                link = dve_chain(dve)
                row_stats(dve, link, lambda i: x[:, i, :])
                nc.vector.memset(tn[:, :], 0.0).then_inc(s_l2, 1)
                dve.wait_ge(s_f2, 1)
                newton(dve, link, rs[:, :], ve[:, :], tn[:, :])
                link(nc.vector.tensor_tensor(ss[:, :], rs[:, :], rs[:, :], ALU.mult))
                link(nc.vector.tensor_tensor(ss[:, :], ss[:, :], mv[:, :, 1], ALU.mult))
                link(nc.vector.tensor_scalar(ss[:, :], ss[:, :], float(D), 1e-24, ALU.mult, ALU.max))
                nc.vector.memset(tn[:, :], 0.0).then_inc(s_l2, 1)
                for i in range(TILES):
                    ins = nc.vector.tensor_scalar(xn2[:, i, :], x[:, i, :], mv[:, i, 0:1], rs[:, i:i + 1],
                                                  ALU.subtract, ALU.mult)
                link(ins)
                for i in range(TILES):
                    ins = nc.vector.tensor_tensor_reduce(out=prod[:, :], in0=xn2[:, i, :], in1=route_row[:, :],
                                                         scale=1.0, scalar=0.0, op0=ALU.mult, op1=ALU.add,
                                                         accum_out=u_col[:, i:i + 1])
                    link(ins)
                nc.vector.tensor_scalar(u_col[:, :], u_col[:, :], 10.0, None, ALU.mult).then_inc(s_fy, 1)
                dve.wait_ge(s_f2, 2)
                newton(dve, link, lg[:, :], ss[:, :], tn[:, :])
                link(nc.vector.tensor_scalar(lg[:, :], lg[:, :], float(D) ** 0.5, None, ALU.mult))
                for b in range(B):
                    for i in range(b * QB, (b + 1) * QB):
                        ins = nc.vector.tensor_scalar(xn2[:, i, :], xn2[:, i, :], lg[:, i:i + 1], None, ALU.mult)
                    ins.then_inc(s_xr, 1)
                dve.wait_ge(s_tu, 1)
                nc.vector.tensor_copy(u_t[:, :], psum[0:TILES, 7, 0:P]).then_inc(s_tuc, 1)
                dve.wait_ge(s_udma, 32)
                link(nc.vector.reduce_max(umax[:, :], u[:, :], AX.X))
                link(nc.vector.tensor_scalar(zmax[:, :], umax[:, :], 0.0, None, ALU.min))
                nc.vector.tensor_scalar(z[:, :], u[:, :], 0.0, zmax[:, 0:1], ALU.min, ALU.subtract).then_inc(s_r, 1)
                dve.wait_ge(s_ra, 2)
                link(nc.vector.tensor_scalar(beta[:, :], ts[:, :], zmax[:, 0:1], LOG_K, ALU.add, ALU.subtract))
                steps = 0
                for r in range(REBASES):
                    nc.vector.tensor_scalar(z[:, :], u[:, :], beta[:, 0:1], CLIP, ALU.subtract, ALU.min)\
                      .then_inc(s_r, 1)
                    link(nc.vector.memset(tt[:, :], 1.0))
                    dve.wait_ge(s_ra, 3 + 2 * r)
                    for _ in range(min(REBASE, ITERS - 1 - REBASE * r)):
                        link(nc.vector.tensor_scalar(key[:, 0, :], f[:, :], tt[:, 0:1], None, ALU.min, ALU.add,
                                                     accum_out=ts[:, :]))
                        link(nc.vector.tensor_scalar(tt[:, :], ts[:, :], 1.0 / K_ROUTE, None, ALU.mult))
                        steps += 1
                    nc.vector.tensor_copy(nb[:, :], tt[:, :]).then_inc(s_r, 1)
                    dve.wait_ge(s_ra, 4 + 2 * r)
                    link(nc.vector.tensor_tensor(beta[:, :], beta[:, :], ts[:, :], ALU.add))
                assert steps == ITERS - 1
                nc.vector.tensor_scalar(z[:, :], u[:, :], beta[:, 0:1], 0.0, ALU.subtract, ALU.min).then_inc(s_r, 1)
                dve.wait_ge(s_r, 2 + 2 * REBASES)
                link(nc.vector.tensor_scalar(key[:, 0, :], z[:, :], CUT, None, ALU.max))
                for k in range(TOPK // 8):
                    link(nc.vector.max(top[:, :], key[:, k % 2, :]))
                    link(nc.vector.match_replace(out=key[:, (k + 1) % 2, :], in_to_replace=top[:, :],
                                                 in_values=key[:, k % 2, :], imm_value=2 * CUT))
                link(nc.vector.tensor_scalar(sel[:, :], key[:, (TOPK // 8) % 2, :], 1.5 * CUT, None, ALU.is_lt))
                dve.wait_ge(s_ra, 3 + 2 * REBASES)
                link(nc.vector.tensor_scalar(f[:, :], e[:, :], -1.0, 1.0, ALU.mult, ALU.add))
                link(nc.vector.tensor_tensor(e[:, :], e[:, :], f[:, :], ALU.add))
                nc.vector.tensor_tensor(sel[:, :], sel[:, :], e[:, :], ALU.mult).then_inc(s_zdone, 1)
                for b in range(B):
                    dve.wait_ge(s_ft, b + 1)
                    if b >= 2:
                        dve.wait_ge(s_hid, (1 + HC) * (b - 1))
                    nc.vector.tensor_copy(xr_t[:, b % 2, :], psum[:, 0, :]).then_inc(s_ftc, 1)
                    dve.wait_ge(s_ff, b + 1)
                    row = slice(b * QB, (b + 1) * QB)
                    nc.vector.tensor_tensor(light[:, row, :], psum[:, 5, :].rearrange("p (t d) -> p t d", t=QB),
                                            b2[:, 0:1, :].to_broadcast([P, QB, D]), ALU.add)
                    ins = nc.vector.tensor_tensor(heavy[:, row, :], psum[:, 6, :].rearrange("p (t d) -> p t d", t=QB),
                                                  b2[:, 1:2, :].to_broadcast([P, QB, D]), ALU.add)
                    ins.then_inc(s_ffc, 1)
                dve.wait_ge(s_ffc, B)
                dve.wait_ge(s_zt, 1)
                link(nc.vector.tensor_copy(wcol[:, :, :].rearrange("p t b -> p (t b)"), psum[:, 7, 0:TILES]))
                for i in range(TILES):
                    ins = nc.vector.scalar_tensor_tensor(out=heavy[:, i, :], in0=heavy[:, i, :],
                                                         scalar=wcol[:, i % QB, i // QB:i // QB + 1],
                                                         in1=light[:, i, :], op0=ALU.mult, op1=ALU.add)
                link(ins)
                row_stats(dve, link, lambda i: heavy[:, i, :])
                nc.vector.memset(tn[:, :], 0.0).then_inc(s_ln2, 1)
                dve.wait_ge(s_f2, 3)
                newton(dve, link, rs[:, :], ve[:, :], tn[:, :])
                for b in range(B):
                    for i in range(b * QB, (b + 1) * QB):
                        ins = nc.vector.tensor_scalar(heavy[:, i, :], heavy[:, i, :], mv[:, i, 0:1], rs[:, i:i + 1],
                                                      ALU.subtract, ALU.mult)
                    link(ins)
                    row = slice(b * QB, (b + 1) * QB)
                    nc.vector.tensor_tensor(heavy[:, row, :], heavy[:, row, :], x[:, row, :],
                                            ALU.add).then_inc(s_fin, 1)
                dve_steps[0] += link.n


_INS = ['L0_attn_X', 'L0_attn_W_q', 'L0_attn_W_k', 'L0_attn_W_v', 'L0_attn_W_o', 'L0_attn_lambda_q1',
        'L0_attn_lambda_k1', 'L0_attn_lambda_q2', 'L0_attn_lambda_k2', 'L0_attn_rms_scale',
        'L0_ffn_routing_token', 'L0_ffn_gamma_light', 'L0_ffn_w1_light', 'L0_ffn_b1_light', 'L0_ffn_w2_light',
        'L0_ffn_b2_light', 'L0_ffn_gamma_heavy', 'L0_ffn_w1_heavy', 'L0_ffn_b1_heavy', 'L0_ffn_w2_heavy',
        'L0_ffn_b2_heavy']


def kernel(**inputs):
    import numpy as _np
    import concourse.bacc as _bacc
    from concourse import mybir as _mybir
    from concourse.bass_utils import run_bass_kernel_spmd as _run

    nc = _bacc.Bacc("TRN2", target_bir_lowering=False, num_devices=1)
    arrays, args = {}, []
    for name in _INS:
        a = _np.ascontiguousarray(inputs[name])
        arrays[f"in_{name}_dram"] = a
        args.append(nc.dram_tensor(f"in_{name}_dram", a.shape, _mybir.dt.from_np(a.dtype), kind="ExternalInput").ap())
    args.append(nc.dram_tensor("out_0_dram", (B, N, D), F32, kind="ExternalOutput").ap())
    program(nc, *args)
    r = _run(nc, [arrays], core_ids=[0])
    return r.results[0]["out_0_dram"]
```

```python
from contextlib import ExitStack

import concourse.bass as bass
from concourse import mybir

F32 = mybir.dt.float32
BF16 = mybir.dt.bfloat16
U32 = mybir.dt.uint32
ALU = mybir.AluOpType
ACT = mybir.ActivationFunctionType
AX = mybir.AxisListType

P = 128
B = 8
N = 512
D = 128
H = 16
DH = 8
QB = N // P
TILES = B * QB
D2 = 2 * DH * H
COMBOS = 2 * H
PAIRS = H // 2
SPLITS = 6
KR = SPLITS * DH
KM = KR + 3
HV = 2 * DH + 1
LIGHT = 64
HEAVY = 512
HC = HEAVY // P
TOPK = 128
ITERS = 50
K_ROUTE = 8.0
REBASE = 10
CLIP = 60.0
LN_EPS = 1e-5
NEG = -1.0e30
CUT = -87.3365
SCALE = float(DH) ** -0.5
GROUPS = 5
REBASES = -(-(ITERS - 1) // REBASE)
LAMBDA_INIT = 0.8
LN2 = 0.6931471805599453
LOG_K = 2.0794415416798357
LOG_SHIFT = 32


class Chain:

    def __init__(self, engine, done, start=0):
        self.engine, self.done, self.start, self.n = engine, done, start, 0

    def __call__(self, instruction):
        self.n += 1
        instruction.then_inc(self.done, 1)
        self.engine.wait_ge(self.done, self.start + self.n)



class Chain:

    def __init__(self, engine, done, start=0):
        self.engine, self.done, self.start, self.n = engine, done, start, 0

    def __call__(self, instruction):
        self.n += 1
        instruction.then_inc(self.done, 1)
        self.engine.wait_ge(self.done, self.start + self.n)



class Chain:

    def __init__(self, engine, done, start=0):
        self.engine, self.done, self.start, self.n = engine, done, start, 0

    def __call__(self, instruction):
        self.n += 1
        instruction.then_inc(self.done, 1)
        self.engine.wait_ge(self.done, self.start + self.n)



class Chain:

    def __init__(self, engine, done, start=0):
        self.engine, self.done, self.start, self.n = engine, done, start, 0

    def __call__(self, instruction):
        self.n += 1
        instruction.then_inc(self.done, 1)
        self.engine.wait_ge(self.done, self.start + self.n)



class Chain:

    def __init__(self, engine, done, start=0):
        self.engine, self.done, self.start, self.n = engine, done, start, 0

    def __call__(self, instruction):
        self.n += 1
        instruction.then_inc(self.done, 1)
        self.engine.wait_ge(self.done, self.start + self.n)



class Chain:

    def __init__(self, engine, done, start=0):
        self.engine, self.done, self.start, self.n = engine, done, start, 0

    def __call__(self, instruction):
        self.n += 1
        instruction.then_inc(self.done, 1)
        self.engine.wait_ge(self.done, self.start + self.n)



class Chain:

    def __init__(self, engine, done, start=0):
        self.engine, self.done, self.start, self.n = engine, done, start, 0

    def __call__(self, instruction):
        self.n += 1
        instruction.then_inc(self.done, 1)
        self.engine.wait_ge(self.done, self.start + self.n)



class Chain:

    def __init__(self, engine, done, start=0):
        self.engine, self.done, self.start, self.n = engine, done, start, 0

    def __call__(self, instruction):
        self.n += 1
        instruction.then_inc(self.done, 1)
        self.engine.wait_ge(self.done, self.start + self.n)


def program(nc, X, Wq, Wk, Wv, Wo, lq1, lk1, lq2, lk2, rms_scale, route, g_l, w1_l, b1_l, w2_l, b2_l,
            g_h, w1_h, b1_h, w2_h, b2_h, out):
    ctx = ExitStack()
    with ctx:
        ctx.enter_context(nc.allow_non_contiguous_dma("small vectors and rearranged scratch"))

        def sb(name, shape, dt=F32):
            return ctx.enter_context(nc.sbuf_tensor(name, shape, dt))

        def sem(name):
            return ctx.enter_context(nc.semaphore(name))

        q_dram = nc.dram_tensor("q_scratch", (B, COMBOS, KM, N), BF16, kind="Internal").ap()
        k_dram = nc.dram_tensor("k_scratch", (B, COMBOS, KR, N), BF16, kind="Internal").ap()
        v_dram = nc.dram_tensor("v_scratch", (B, P, PAIRS, QB * 2 * HV), F32, kind="Internal").ap()
        u_dram = nc.dram_tensor("u_scratch", (TILES, P), F32, kind="Internal").ap()

        ident = sb("ident", [P, P])
        ident_bf = sb("ident_bf", [P, P], BF16)
        causal_bf = sb("causal_bf", [P, P], BF16)
        eps_col = sb("eps_col", [P, 1])
        shift_col = sb("shift_col", [P, 1])
        w_rows = sb("w_rows", [P, 8, P])
        w_qkv = sb("w_qkv", [P, 6, P])
        w_o = sb("w_o", [P, 2, P])
        o_scale = sb("o_scale", [P, 1])
        lam_in = sb("lam_in", [P, 4, H * DH])
        lam_prod = sb("lam_prod", [P, 2, H * DH])
        lam_sum = sb("lam_sum", [P, 2, H])
        coef = sb("coef", [P, H, 2])
        route_row = sb("route_row", [P, D])
        w1 = sb("w1", [P, LIGHT + HEAVY])
        w1g = sb("w1g", [P, LIGHT + HEAVY])
        gam = sb("gam", [P, 2])
        b1c = sb("b1c", [P, 1 + HC])
        w2h = sb("w2h", [P, HC, D])
        w2l = sb("w2l", [LIGHT, D])
        b2 = sb("b2", [P, 2, D])

        x = sb("x", [P, TILES, D])
        attn = sb("attn", [P, B, QB, H, 2 * DH])
        st = sb("st", [P, TILES, 6])
        mv = sb("mv", [P, TILES, 2])
        ve = sb("ve", [P, TILES])
        lg = sb("lg", [P, TILES])
        rs = sb("rs", [P, TILES])
        tn = sb("tn", [P, TILES])

        psum = ctx.enter_context(nc.psum_tensor("psum", [P, 8, N], F32))

        s_pool_go = sem("s_pool_go")
        s_x = sem("s_x")
        s_w = sem("s_w")
        s_const = sem("s_const")
        s_dve = sem("s_dve")
        s_stat = sem("s_stat")
        s_log = sem("s_log")
        s_exp0 = sem("s_exp0")
        s_wt = sem("s_wt")
        s_wtc = sem("s_wtc")
        dve_steps = [0]

        def dve_chain(dve):
            return Chain(dve, s_dve, dve_steps[0])

        def newton(dve, link, y, v, t):
            link(nc.vector.tensor_tensor(t, y, y, ALU.mult))
            link(nc.vector.tensor_tensor(t, t, v, ALU.mult))
            link(nc.vector.tensor_scalar(t, t, -0.5, 1.5, ALU.mult, ALU.add))
            link(nc.vector.tensor_tensor(y, y, t, ALU.mult))

        def row_stats(dve, link, src):
            for i in range(TILES):
                ins = nc.vector.bn_stats(st[:, i, :], src(i))
            link(ins)
            for i in range(TILES):
                ins = nc.vector.bn_aggr(mv[:, i, :], st[:, i, :])
            link(ins)
            link(nc.vector.tensor_scalar(ve[:, :], mv[:, :, 1], LN_EPS, None, ALU.add))

        W_DMAS = [0]
        with nc.Block() as block:
            @block.sync
            def _(sp):
                for b in range(B):
                    sp.dma_start(x[:, b * QB:(b + 1) * QB, :],
                                 X[b].rearrange("(t p) d -> p t d", p=P)).then_inc(s_x, 16)
                row = lambda v: v.rearrange("(a n) -> a n", a=1)
                col = lambda v: v.rearrange("(d a) -> d a", a=1)
                loads = [(w_rows[:, 2 * w + t, :], W[t * P:(t + 1) * P, :])
                         for w, W in enumerate((Wq, Wk, Wv)) for t in range(2)]
                loads += [(w_rows[:, 6 + t, :], Wo[:, t * P:(t + 1) * P]) for t in range(2)]
                loads += [(o_scale[r * 2 * DH:(r + 1) * 2 * DH, :], col(rms_scale)) for r in range(P // (2 * DH))]
                loads += [(lam_in[:, i, :], L.rearrange("h d -> (h d)").rearrange("(a n) -> a n", a=1)
                           .to_broadcast([P, H * DH])) for i, L in enumerate((lq1, lq2, lk1, lk2))]
                loads += [(route_row[:, :], row(route).to_broadcast([P, D])),
                          (w1[:, 0:LIGHT], w1_l), (w1[:, LIGHT:], w1_h),
                          (gam[:, 0:1], col(g_l)), (gam[:, 1:2], col(g_h)),
                          (b1c[0:LIGHT, 0:1], col(b1_l)), (b1c[:, 1:], b1_h.rearrange("(c p) -> p c", p=P)),
                          (w2h[:, :, :], w2_h.rearrange("(c p) d -> p c d", p=P)), (w2l[:, :], w2_l),
                          (b2[:, 0, :], row(b2_l).to_broadcast([P, D])),
                          (b2[:, 1, :], row(b2_h).to_broadcast([P, D]))]
                for dst, src in loads:
                    sp.dma_start(dst, src).then_inc(s_w, 16)
                W_DMAS[0] = 16 * len(loads)

            @block.gpsimd
            def _(pool):
                nc.gpsimd.memset(ident[:, :], 0.0).then_inc(s_const, 1)
                nc.gpsimd.memset(ident_bf[:, :], 0.0).then_inc(s_const, 1)
                nc.gpsimd.memset(causal_bf[:, :], 0.0).then_inc(s_const, 1)
                nc.gpsimd.memset(eps_col[:, :], LN_EPS).then_inc(s_const, 1)
                nc.gpsimd.memset(shift_col[:, :], 0.5 * LOG_SHIFT * LN2).then_inc(s_const, 1)
                pool.wait_ge(s_const, 5)
                for tile, op, fill in ((ident, ALU.not_equal, 1.0), (ident_bf, ALU.not_equal, 1.0),
                                       (causal_bf, ALU.is_ge, NEG)):
                    nc.gpsimd.affine_select(out=tile[:, :], in_=tile[:, :], compare_op=op, fill=fill, base=0,
                                            pattern=[[-1, P]], channel_multiplier=1).then_inc(s_const, 1)

            @block.tensor
            def _(pe):
                pe.wait_ge(s_const, 8)
                pe.wait_ge(s_w, W_DMAS[0])
                for i in range(8):
                    ins = nc.tensor.transpose(psum[:, i // 4, (i % 4) * P:(i % 4 + 1) * P], w_rows[:, i, :], ident[:, :])
                ins.then_inc(s_wt, 1)

            @block.vector
            def _(dve):
                link = dve_chain(dve)
                dve.wait_ge(s_w, W_DMAS[0])
                link(nc.vector.tensor_tensor(lam_prod[:, :, :], lam_in[:, 0:2, :], lam_in[:, 2:4, :], ALU.mult))
                nc.vector.tensor_reduce(lam_sum[:, :, :], lam_prod[:, :, :].rearrange("p a (h d) -> p a h d", d=DH),
                                        AX.X, ALU.add).then_inc(s_stat, 1)
                link(nc.vector.tensor_scalar(o_scale[:, :], o_scale[:, :], 1.0 - LAMBDA_INIT, None, ALU.mult))
                nc.vector.tensor_scalar(w1g[:, 0:LIGHT], w1[:, 0:LIGHT], gam[:, 0:1], None, ALU.mult)
                nc.vector.tensor_scalar(w1g[:, LIGHT:], w1[:, LIGHT:], gam[:, 1:2], None, ALU.mult)
                dve.wait_ge(s_wt, 1)
                nc.vector.tensor_copy(w_qkv[:, :, :].rearrange("p a n -> p (a n)"),
                                      psum[:, 0:2, :].rearrange("p a n -> p (a n)")[:, 0:6 * P])
                nc.vector.tensor_scalar(w_o[:, :, :], psum[:, 1, 2 * P:4 * P].rearrange("p (a n) -> p a n", a=2),
                                        o_scale[:, 0:1], None, ALU.mult)
                dve.wait_ge(s_x, 16 * B)
                row_stats(dve, link, lambda i: x[:, i, :])
                nc.vector.memset(coef[:, :, 0], 1.0).then_inc(s_stat, 1)
                dve.wait_ge(s_exp0, 2)
                newton(dve, link, rs[:, :], ve[:, :], tn[:, :])
                link(nc.vector.tensor_tensor(coef[:, :, 1], lam_sum[:, 1, :], lam_sum[:, 0, :], ALU.subtract))
                link(nc.vector.tensor_scalar(coef[:, :, 1], coef[:, :, 1], -LAMBDA_INIT, None, ALU.add))
                dve_steps[0] += link.n

            @block.scalar
            def _(act):
                act.wait_ge(s_stat, 1)
                nc.scalar.activation(lam_sum[:, :, :], lam_sum[:, :, :], ACT.Exp).then_inc(s_exp0, 1)
                act.wait_ge(s_stat, 2)
                nc.scalar.activation(lg[:, :], ve[:, :], ACT.Ln).then_inc(s_log, 1)
                act.wait_ge(s_log, 1)
                nc.scalar.activation(rs[:, :], lg[:, :], ACT.Exp, scale=-0.5).then_inc(s_exp0, 1)

        s_xn = sem("s_xn")
        s_xt = sem("s_xt")
        s_xtc = sem("s_xtc")
        s_proj = sem("s_proj")
        s_hi = sem("s_hi")
        s_res = sem("s_res")
        s_mid = sem("s_mid")
        s_res2 = sem("s_res2")
        s_low = sem("s_low")
        s_vp = sem("s_vp")
        s_v = sem("s_v")
        s_ones = sem("s_ones")
        s_zrow = sem("s_zrow")
        s_zout = sem("s_zout")
        s_qk_out = [sem(f"s_qk_out{s}") for s in range(2)]
        s_v_out = [sem(f"s_v_out{s}") for s in range(2)]
        Q_RUNS = ((0, 3), (0, 2), (0, 1))
        K_RUNS = ((0, 3), (1, 2), (2, 1))
        QK_OUT = 2 * 2 * 3 * 16

        def slot(i, part):
            return part if i < 2 else 2 - part

        def positive(count):
            return not isinstance(count, int) or count > 0

        def over_row_pairs(engine, body):
            for s in range(2):
                body(0, s, True)
            with engine.Fori(1, B // 2 - 1) as j:
                for s in range(2):
                    body(j, s, True)
            for s in range(2):
                body(B // 2 - 1, s, s == 0)

        with ExitStack() as local:
            def tmp(name, shape, dt=F32):
                return local.enter_context(nc.sbuf_tensor(name, shape, dt))
            xn = tmp("xn", [P, 2, QB, D])
            xn_t = tmp("xn_t", [P, 2, N])
            parts = tmp("parts", [P, 2, 4, 3, N], BF16)
            res = tmp("res", [P, 4, N])
            v_out = tmp("v_out", [P, 2, PAIRS, QB, 2, HV])
            zrow = tmp("zrow", [COMBOS, (KM - KR) * N], BF16)
            block = local.enter_context(nc.Block())

            @block.gpsimd
            def _(pool):
                nc.gpsimd.memset(v_out[:, :, :, :, :, :], 1.0).then_inc(s_ones, 1)
                nc.gpsimd.memset(zrow[:, :], 0.0).then_inc(s_zrow, 1)

                def body(j, s, _):
                    b = 2 * j + s
                    for i in range(4):
                        pool.wait_ge(s_mid, 4 * b + i + 1)
                        pool.sem_inc(s_pool_go, 1)
                        nc.gpsimd.tensor_tensor(parts[:, s, i, slot(i, 2), :], res[:, i, :], parts[:, s, i, 1, :],
                                                ALU.subtract).then_inc(s_low, 1)

                over_row_pairs(pool, body)

            @block.vector
            def _(dve):
                def normed(b, s):
                    for t in range(QB):
                        i = b * QB + t
                        m, r = (mv[:, i, 0:1], rs[:, i:i + 1]) if isinstance(i, int) else \
                            (mv[:, i, 0:1], rs[:, bass.ds(i, 1)])
                        nc.vector.tensor_scalar(xn[:, s, t, :], x[:, i, :], m, r,
                                                ALU.subtract, ALU.mult).then_inc(s_xn, 1)

                def body(j, s, more):
                    b = 2 * j + s
                    if more:
                        if positive(b):
                            dve.wait_ge(s_xt, b)
                        normed(b + 1, 1 - s)
                    for i in range(4):
                        dve.wait_ge(s_hi, 4 * b + i + 1)
                        if positive(b):
                            dve.wait_ge(s_low, 4 * b + i - 3)
                        nc.vector.tensor_tensor(res[:, i, :], psum[:, 1 + i, :], parts[:, s, i, slot(i, 0), :],
                                                ALU.subtract).then_inc(s_res, 1)
                    for t in range(QB):
                        if t == 0:
                            if isinstance(b, int) and b == 0:
                                dve.wait_ge(s_ones, 1)
                            if positive(j):
                                dve.wait_ge(s_v_out[s], 16 * j)
                        dve.wait_ge(s_vp, QB * b + (t | 1) + 1)
                        nc.vector.tensor_copy(
                            v_out[:, s, :, t, :, 0:2 * DH],
                            psum[:, 5 + t // 2, (t % 2) * D2:(t % 2 + 1) * D2]
                            .rearrange("p (a h d) -> p a h d", a=PAIRS, h=2)).then_inc(s_v, 1)

                normed(0, 0)
                over_row_pairs(dve, body)

            @block.tensor
            def _(pe):
                def transposed(b, s):
                    pe.wait_ge(s_xn, QB * (b + 1))
                    for t in range(QB):
                        ins = nc.tensor.transpose(psum[:, 0, t * P:(t + 1) * P], xn[:, s, t, :], ident[:, :])
                    ins.then_inc(s_xt, 1)

                def body(j, s, more):
                    b = 2 * j + s
                    pe.wait_ge(s_xtc, b + 1)
                    for i in range(4):
                        if positive(b):
                            pe.wait_ge(s_res, 4 * b + i - 3)
                        nc.tensor.matmul(psum[:, 1 + i, :], w_qkv[:, i, :], xn_t[:, s, :],
                                         start=True, stop=True).then_inc(s_proj, 1)
                    if more:
                        transposed(b + 1, 1 - s)
                    for t in range(QB):
                        if positive(b) and t % 2 == 0:
                            pe.wait_ge(s_v, QB * b + t - 2)
                        nc.tensor.matmul(psum[:, 5 + t // 2, (t % 2) * D2:(t % 2 + 1) * D2],
                                         xn_t[:, s, t * P:(t + 1) * P],
                                         w_qkv[:, 4:6, :].rearrange("p a n -> p (a n)"),
                                         start=True, stop=True).then_inc(s_vp, 1)

                transposed(0, 0)
                over_row_pairs(pe, body)

            @block.scalar
            def _(act):
                def copied(b, s):
                    act.wait_ge(s_xt, b + 1)
                    if positive(b - 1):
                        act.wait_ge(s_vp, QB * (b - 1))
                    nc.scalar.copy(xn_t[:, s, :], psum[:, 0, :]).then_inc(s_xtc, 1)

                def middle(b, s, i):
                    act.wait_ge(s_res, 4 * b + i + 1)
                    nc.scalar.copy(parts[:, s, i, 1, :], res[:, i, :]).then_inc(s_mid, 1)

                def body(j, s, more):
                    b = 2 * j + s
                    if positive(j):
                        act.wait_ge(s_qk_out[s], QK_OUT * j)
                    for i in range(4):
                        act.wait_ge(s_proj, 4 * b + i + 1)
                        nc.scalar.copy(parts[:, s, i, slot(i, 0), :], psum[:, 1 + i, :]).then_inc(s_hi, 1)
                        if i > 0:
                            middle(b, s, i - 1)
                    if more:
                        copied(b + 1, 1 - s)
                    middle(b, s, 3)

                copied(0, 0)
                over_row_pairs(act, body)

            @block.sync
            def _(sp):
                sp.wait_ge(s_zrow, 1)
                for b in range(B):
                    sp.dma_start(q_dram[b, :, KR:KM, :], zrow[:, :].rearrange("c (r n) -> c r n", n=N))\
                      .then_inc(s_zout, 16)

                def body(j, s, _):
                    b = 2 * j + s
                    for which, dram, runs in ((0, q_dram, Q_RUNS), (1, k_dram, K_RUNS)):
                        for t in range(2):
                            i = 2 * which + t
                            sp.wait_ge(s_low, 4 * b + i + 1)
                            first_row = 0
                            for first, count in runs:
                                sp.dma_start(dram[b, t * H:(t + 1) * H, 0:KR, :]
                                             .rearrange("c (d j) n -> c d j n", j=SPLITS)[:, :, first_row:first_row + count, :],
                                             parts[:, s, i, first:first + count, :]).then_inc(s_qk_out[s], 16)
                                first_row += count
                    sp.wait_ge(s_v, QB * (b + 1))
                    sp.dma_start(v_dram[b], v_out[:, s].rearrange("p a t h v -> p a (t h v)"))\
                      .then_inc(s_v_out[s], 16)

                over_row_pairs(sp, body)
                for s in range(2):
                    sp.wait_ge(s_qk_out[s], QK_OUT * B // 2)
                    sp.wait_ge(s_v_out[s], 16 * B // 2)
                sp.wait_ge(s_zout, 16 * B)

        s_load = [sem(f"s_load{p}") for p in range(PAIRS)]
        s_vload = [sem(f"s_vload{p}") for p in range(PAIRS)]
        s_mrow = [sem(f"s_mrow{p}") for p in range(PAIRS)]
        s_kones = sem("s_kones")
        s_score = sem("s_score")
        s_prob = sem("s_prob")
        s_masked = sem("s_masked")
        s_pv = sem("s_pv")
        s_pvc = sem("s_pvc")
        s_ot = sem("s_ot")
        s_oh = sem("s_oh")
        s_rec = sem("s_rec")
        s_recl = sem("s_recl")
        s_o = sem("s_o")
        s_max = sem("s_max")
        s_maxr = sem("s_maxr")
        s_msplit = sem("s_msplit")
        s_mchain = sem("s_mchain")
        s_mt = sem("s_mt")
        s_mtc = sem("s_mtc")
        s_zero = sem("s_zero")
        EXP_BANK, RING, PV_BANK, OT_BANK = (0, 2), (4, 5), 6, 7
        MAX_AHEAD = PAIRS - 2
        ROWS_AHEAD = MAX_AHEAD - 1
        GROUP_CELLS = (
            ((0, 0, 0, 0), (1, 0, 1, 0)),
            ((2, 0, 0, 0), (3, 0, 1, 0)),
            ((0, 1, 0, 0), (0, 3, 0, 384), (1, 1, 1, 0), (1, 3, 1, 384)),
            ((2, 1, 0, 0), (2, 3, 0, 384), (3, 1, 1, 0), (3, 3, 1, 384)),
            ((0, 2, 0, 0), (1, 2, 0, 256), (2, 2, 1, 0), (3, 2, 1, 256)))
        MAX_TILES = tuple((3, (c,)) for c in range(4)) + tuple((2, (c,)) for c in range(4)) \
            + ((1, (0, 1)), (1, (2, 3)), (0, (0, 1, 2, 3)))
        MT = len(MAX_TILES)
        SLOT_TILES = (2, 2, 2, 3, 2)

        def pair_at(b, p, shift):
            row, pair = b + (p + shift) // PAIRS, (p + shift) % PAIRS
            if isinstance(row, int) and not 0 <= row < B:
                return None
            return row, pair, PAIRS * row + pair

        with ExitStack() as local:
            def tmp(name, shape, dt=F32):
                return local.enter_context(nc.sbuf_tensor(name, shape, dt))
            q_st = tmp("q_st", [P, 2 * PAIRS, N], BF16)
            k_st = tmp("k_st", [P, COMBOS, N], BF16)
            v_aug = tmp("v_aug", [P, PAIRS, QB * 2 * HV])
            probs = tmp("probs", [P, 2, GROUPS, 2, N])
            nmax = tmp("nmax", [P, 2, QB, 4])
            nres = tmp("nres", [P, 2, QB, 4])
            nparts = tmp("nparts", [P, 2, QB, 4, 3], BF16)
            nrow = tmp("nrow", [12, 2, N], BF16)
            o_t = tmp("o_t", [P, N])
            recip = tmp("recip", [P, QB, 4])
            o_half = tmp("o_half", [P, 2, QB, 4, 2 * DH])
            block = local.enter_context(nc.Block())

            def rows(pair, c):
                return 64 * (c % 2), 2 * pair + c // 2

            def over_rows(engine, body):
                body(0)
                with engine.Fori(1, B - 1) as b:
                    body(b)
                body(B - 1)

            @block.sync
            def _(sp):
                def load(at):
                    b, p, _ = at
                    for half in range(2):
                        src = slice(4 * p + half, 4 * p + half + 3, 2)
                        sp.dma_start(q_st[64 * half:64 * half + KM, 2 * p:2 * p + 2, :],
                                     q_dram[b, src].rearrange("s r n -> r s n")).then_inc(s_load[p], 16)
                        sp.dma_start(k_st[64 * half:64 * half + KR, src, :],
                                     k_dram[b, src].rearrange("s r n -> r s n")).then_inc(s_load[p], 16)

                def load_v(at):
                    b, p, _ = at
                    sp.dma_start(v_aug[:, p, :], v_dram[b, :, p, :]).then_inc(s_vload[p], 16)

                def max_rows(at):
                    _, p, n = at
                    sp.wait_ge(s_mtc, n + 1)
                    for c in range(4):
                        r0, s = rows(p, c)
                        sp.dma_start(q_st[r0 + KR:r0 + KM, s, :], nrow[3 * c:3 * c + 3, p % 2, :])\
                          .then_inc(s_mrow[p], 16)

                def body(b):
                    for p in range(PAIRS):
                        n = PAIRS * b + p
                        at = pair_at(b, p, ROWS_AHEAD)
                        if at:
                            max_rows(at)
                        prev = pair_at(b, p, -1)
                        at = pair_at(b, p, PAIRS - 1)
                        if prev and at:
                            sp.wait_ge(s_pv, prev[2] + 1)
                            load_v(at)
                        at = pair_at(b, p, PAIRS)
                        if at:
                            sp.wait_ge(s_score, GROUPS * (n + 1))
                            load(at)

                sp.wait_ge(s_kones, 4)
                for p in range(PAIRS):
                    load((0, p, p))
                    load_v((0, p, p))
                for p in range(ROWS_AHEAD):
                    max_rows((0, p, p))
                over_rows(sp, body)

            @block.gpsimd
            def _(pool):
                nc.gpsimd.memset(q_st[:, :, :].bitcast(U32), 0).then_inc(s_kones, 1)
                nc.gpsimd.memset(k_st[:, :, :].bitcast(U32), 0).then_inc(s_kones, 1)
                pool.wait_ge(s_kones, 2)
                for half in range(2):
                    nc.gpsimd.memset(k_st[64 * half:64 * half + 64, half::2, :], 1.0).then_inc(s_kones, 1)

                def split_max(at):
                    _, p, n = at
                    pool.wait_ge(s_maxr, MT * (n + 1))
                    if positive(n - 1):
                        pool.wait_ge(s_mt, n - 1)
                    pool.sem_inc(s_pool_go, 1)
                    link = Chain(pool, s_mchain, 4 * n)
                    a, r, o = nmax[:, p % 2], nres[:, p % 2], nparts[:, p % 2]
                    link(nc.gpsimd.tensor_copy(o[:, :, :, 0], a))
                    link(nc.gpsimd.tensor_tensor(r, a, o[:, :, :, 0], ALU.subtract))
                    pool.sem_inc(s_pool_go, 1)
                    link(nc.gpsimd.tensor_copy(o[:, :, :, 1], r))
                    link(nc.gpsimd.tensor_tensor(r, r, o[:, :, :, 1], ALU.subtract))
                    pool.sem_inc(s_pool_go, 1)
                    nc.gpsimd.tensor_copy(o[:, :, :, 2], r).then_inc(s_msplit, 1)

                def mask(n, p, g):
                    pool.wait_ge(s_prob, GROUPS * n + g + 1)
                    cells = probs[:, p % 2, g]
                    if g < 2:
                        views = (cells[:, :, 0:P],)
                    elif g < 4:
                        views = (cells[:, :, 0:P], cells[:, :, 3 * P:4 * P])
                    else:
                        views = (cells.rearrange("p a (k n) -> p (a k) n", n=2 * P)[:, :, 0:P],)
                    pool.sem_inc(s_pool_go, 1)
                    for v in views:
                        ins = nc.gpsimd.affine_select(out=v, in_=v, compare_op=ALU.is_ge, fill=0.0, base=0,
                                                      pattern=[[0, v.shape[1]], [1, P]], channel_multiplier=-1)
                    ins.then_inc(s_masked, 1)

                def join(at):
                    b, p, n = at
                    pool.wait_ge(s_oh, n + 1)
                    oh = o_half[:, p % 2].rearrange("p t (h a) d -> p t h a d", a=2)
                    nc.gpsimd.tensor_tensor(attn[:, b, :, 2 * p:2 * p + 2, :], oh[:, :, :, 0, :], oh[:, :, :, 1, :],
                                            ALU.add).then_inc(s_o, 1)

                def body(b):
                    for p in range(PAIRS):
                        n = PAIRS * b + p
                        for g in range(GROUPS):
                            mask(n, p, g)
                            at = pair_at(b, p, -2)
                            if g == 0 and at:
                                join(at)
                            at = pair_at(b, p, MAX_AHEAD - 1)
                            if g == 1 and at and (at[2] if isinstance(at[2], int) else MAX_AHEAD) >= MAX_AHEAD:
                                split_max(at)

                for n in range(MAX_AHEAD):
                    split_max((0, n, n))
                over_rows(pool, body)
                for shift in (-2, -1):
                    join(pair_at(B, 0, shift) or pair_at(B - 1, 0, PAIRS + shift))

            @block.tensor
            def _(pe):
                def max_tile(at, k):
                    _, p, n = at
                    i = MT * n + k
                    bank = psum[:, RING[(MT * p + k) % 2], :]
                    if k == 0:
                        b = at[0]
                        pe.wait_ge(s_load[p], 64 * (b + 1))
                    if positive(i - 1):
                        pe.wait_ge(s_maxr, i - 1)
                    qb, combos = MAX_TILES[k]
                    w = (qb + 1) * P
                    for a, c in enumerate(combos):
                        nc.tensor.matmul(bank[:, a * w:(a + 1) * w], q_st[:, rows(p, c)[1], qb * P:w],
                                         k_st[:, 4 * p + c, 0:w], start=True, stop=False)
                        ins = nc.tensor.matmul(bank[:, (a + 1) * w - P:(a + 1) * w], ident_bf[:, :],
                                               causal_bf[:, :], start=False, stop=True)
                    ins.then_inc(s_max, 1)

                def max_transpose(at):
                    _, p, n = at
                    pe.wait_ge(s_msplit, n + 1)
                    if positive(n - ROWS_AHEAD - 1):
                        pe.wait_ge(s_oh, n - ROWS_AHEAD - 1)
                    if positive(n):
                        pe.wait_ge(s_mtc, n)
                    dst = psum[:, OT_BANK, :].bitcast(BF16)
                    for t in range(QB):
                        ins = nc.tensor.transpose(dst[0:12, t * P:(t + 1) * P],
                                                  nparts[:, p % 2, t].rearrange("p c a -> p (c a)"), ident_bf[:, :])
                    ins.then_inc(s_mt, 1)

                def scores(b, p, g):
                    i = GROUPS * (PAIRS * b + p) + g
                    if g == 0:
                        pe.wait_ge(s_mrow[p], 64 * (b + 1))
                    if positive(i - 1):
                        pe.wait_ge(s_prob, i - 1)
                    base = EXP_BANK[(GROUPS * p + g) % 2]
                    for c, kb, bank, col in GROUP_CELLS[g]:
                        ins = nc.tensor.matmul(psum[:, base + bank, col:col + N - kb * P],
                                               k_st[:, 4 * p + c, kb * P:(kb + 1) * P],
                                               q_st[:, rows(p, c)[1], kb * P:N], start=True, stop=True)
                    ins.then_inc(s_score, 1)

                def values(at, part):
                    b, p, n = at
                    if part == 0:
                        pe.wait_ge(s_vload[p], 16 * (b + 1))
                        if positive(n):
                            pe.wait_ge(s_pvc, n)
                    groups = ((0, 1), (2, 3), (4,))[part]
                    pe.wait_ge(s_masked, GROUPS * n + groups[-1] + 1)
                    for kb in ((0,), (1, 3), (2,))[part]:
                        for c in range(4):
                            g, bank, col = [(g, bank, col) for g in groups
                                            for cc, k, bank, col in GROUP_CELLS[g] if (cc, k) == (c, kb)][0]
                            v = v_aug[:, p, :].rearrange("p (t h v) -> p t h v", t=QB, h=2)[:, kb, c // 2, :]
                            ins = nc.tensor.matmul(psum[32 * c:32 * c + HV, PV_BANK, kb * P:N], v,
                                                   probs[:, p % 2, g, bank, col:col + N - kb * P],
                                                   start=(kb == 0), stop=(kb == 2), tile_position=(0, 32 * c),
                                                   skip_group_check=True)
                    if part == 2:
                        ins.then_inc(s_pv, 1)

                def out_transpose(at):
                    _, p, n = at
                    pe.wait_ge(s_pvc, n + 1)
                    if positive(n):
                        pe.wait_ge(s_oh, n)
                    m = n + 1 + ROWS_AHEAD
                    pe.wait_ge(s_mtc, min(m + 1, PAIRS * B) if isinstance(m, int) else m + 1)
                    for t in range(QB):
                        ins = nc.tensor.transpose(psum[:, OT_BANK, t * P:(t + 1) * P], o_t[:, t * P:(t + 1) * P],
                                                  ident[:, :])
                    ins.then_inc(s_ot, 1)

                def body(b):
                    for p in range(PAIRS):
                        prev = pair_at(b, p, -1)
                        ahead = pair_at(b, p, MAX_AHEAD)
                        k = 0
                        for g in range(GROUPS):
                            scores(b, p, g)
                            if prev and g in (1, 2, 3):
                                values(prev, g - 1)
                            for _ in range(SLOT_TILES[g]):
                                if ahead:
                                    max_tile(ahead, k)
                                    k += 1
                            if g == 2 and pair_at(b, p, ROWS_AHEAD):
                                max_transpose(pair_at(b, p, ROWS_AHEAD))
                        if prev:
                            out_transpose(prev)

                pe.wait_ge(s_zero, 1)
                for n in range(MAX_AHEAD):
                    for k in range(MT):
                        max_tile((0, n, n), k)
                    if n >= 1:
                        max_transpose((0, n - 1, n - 1))
                over_rows(pe, body)
                last = (B - 1, PAIRS - 1, PAIRS * B - 1)
                for part in range(3):
                    values(last, part)
                out_transpose(last)

            @block.scalar
            def _(act):
                def rows_copy(at):
                    _, p, n = at
                    act.wait_ge(s_mt, n + 1)
                    if positive(n - 1):
                        b = at[0]
                        if p >= 2:
                            act.wait_ge(s_mrow[p - 2], 64 * (b + 1))
                        else:
                            act.wait_ge(s_mrow[PAIRS - 2 + p], 64 * b)
                    nc.scalar.copy(nrow[:, p % 2, :], psum[:, OT_BANK, :].bitcast(BF16)[0:12, 0:N]).then_inc(s_mtc, 1)

                def pv_copy(at):
                    _, p, n = at
                    act.wait_ge(s_pv, n + 1)
                    if positive(n):
                        act.wait_ge(s_ot, n)
                    nc.scalar.copy(o_t[:, :], psum[:, PV_BANK, :]).then_inc(s_pvc, 1)

                def body(b):
                    for p in range(PAIRS):
                        n = PAIRS * b + p
                        for g in range(GROUPS):
                            act.wait_ge(s_score, GROUPS * n + g + 1)
                            if g == 0 and positive(n - 1):
                                act.wait_ge(s_pv, n - 1)
                            base = EXP_BANK[(GROUPS * p + g) % 2]
                            nc.scalar.activation(probs[:, p % 2, g], psum[:, base:base + 2, :], ACT.Exp,
                                                 scale=SCALE).then_inc(s_prob, 1)
                            if g == 2 and pair_at(b, p, ROWS_AHEAD):
                                rows_copy(pair_at(b, p, ROWS_AHEAD))
                            if g == 3 and pair_at(b, p, -1):
                                pv_copy(pair_at(b, p, -1))

                for n in range(ROWS_AHEAD):
                    rows_copy((0, n, n))
                over_rows(act, body)
                pv_copy((B - 1, PAIRS - 1, PAIRS * B - 1))

            @block.vector
            def _(dve):
                def max_tile(at, k):
                    _, p, n = at
                    bank = psum[:, RING[(MT * p + k) % 2], :]
                    if k == 0 and positive(n - 1):
                        dve.wait_ge(s_msplit, n - 1)
                    dve.wait_ge(s_max, MT * n + k + 1)
                    qb, combos = MAX_TILES[k]
                    w = (qb + 1) * P
                    nc.vector.tensor_reduce(nmax[:, p % 2, qb, combos[0]:combos[-1] + 1],
                                            bank[:, 0:len(combos) * w].rearrange("p (a n) -> p a n", n=w),
                                            AX.X, ALU.max, negate=True).then_inc(s_maxr, 1)

                def normalise(at):
                    _, p, n = at
                    dve.wait_ge(s_ot, n + 1)
                    ot = psum[:, OT_BANK, :].rearrange("p (t c v) -> p t c v", t=QB, c=4)
                    nc.vector.reciprocal(recip[:, :, :], ot[:, :, :, 2 * DH]).then_inc(s_rec, 1)
                    dve.wait_ge(s_rec, n + 1)
                    cf = coef[:, 2 * p:2 * p + 2, :].rearrange("p h a -> p (h a)")[:, None, :].to_broadcast([P, QB, 4])
                    nc.vector.tensor_tensor(recip[:, :, :], recip[:, :, :], cf, ALU.mult).then_inc(s_recl, 1)
                    dve.wait_ge(s_recl, n + 1)
                    if positive(n - 1):
                        dve.wait_ge(s_o, n - 1)
                    nc.vector.tensor_tensor(o_half[:, p % 2], ot[:, :, :, 0:2 * DH],
                                            recip[:, :, :, None].to_broadcast([P, QB, 4, 2 * DH]),
                                            ALU.mult).then_inc(s_oh, 1)

                def body(b):
                    for p in range(PAIRS):
                        ahead = pair_at(b, p, MAX_AHEAD)
                        k = 0
                        for g in range(GROUPS):
                            for _ in range(SLOT_TILES[g]):
                                if ahead:
                                    max_tile(ahead, k)
                                    k += 1
                            if g == 0 and pair_at(b, p, -2):
                                normalise(pair_at(b, p, -2))

                nc.vector.memset(psum[:, PV_BANK, :], 0.0).then_inc(s_zero, 1)
                for n in range(MAX_AHEAD):
                    for k in range(MT):
                        max_tile((0, n, n), k)
                over_rows(dve, body)
                normalise((B - 1, PAIRS - 2, PAIRS * B - 2))
                normalise((B - 1, PAIRS - 1, PAIRS * B - 1))

        s_sq = sem("s_sq")
        s_ss = sem("s_ss")
        s_hl = sem("s_hl")
        s_hr = sem("s_hr")
        s_hn = sem("s_hn")
        s_hng = sem("s_hng")
        s_at = sem("s_at")
        s_atc = sem("s_atc")
        s_op = sem("s_op")
        s_opc = sem("s_opc")
        s_ln = sem("s_ln")
        HR = B * QB * H
        with ExitStack() as local:
            def tmp(name, shape, dt=F32):
                return local.enter_context(nc.sbuf_tensor(name, shape, dt))
            sq = tmp("sq", [P, 2, QB, H, 2 * DH])
            hv = tmp("hv", [P, HR])
            hy = tmp("hy", [P, HR])
            ht = tmp("ht", [P, HR])
            a_t = tmp("a_t", [P, 2, 2, N])
            ao = tmp("ao", [P, TILES, D])
            block = local.enter_context(nc.Block())

            @block.gpsimd
            def _(pool):
                for b in range(B):
                    if b >= 2:
                        pool.wait_ge(s_ss, b - 1)
                    nc.gpsimd.tensor_tensor(sq[:, b % 2], attn[:, b], attn[:, b], ALU.mult).then_inc(s_sq, 1)
                pool.wait_ge(s_hn, 1)
                for b in range(B):
                    r = hy[:, b * QB * H:(b + 1) * QB * H].rearrange("p (t h) -> p t h", t=QB)
                    nc.gpsimd.tensor_tensor(attn[:, b], attn[:, b],
                                            r[:, :, :, None].to_broadcast([P, QB, H, 2 * DH]),
                                            ALU.mult).then_inc(s_hng, 1)

            @block.scalar
            def _(act):
                act.wait_ge(s_ss, B + 1)
                nc.scalar.activation(hy[:, :], hv[:, :], ACT.Ln).then_inc(s_hl, 1)
                act.wait_ge(s_hl, 1)
                nc.scalar.activation(hy[:, :], hy[:, :], ACT.Exp, scale=-0.5).then_inc(s_hr, 1)
                for b in range(B):
                    act.wait_ge(s_at, b + 1)
                    if b >= 2:
                        act.wait_ge(s_op, b - 1)
                    base = 4 * (b % 2)
                    nc.scalar.copy(a_t[:, b % 2], psum[:, base:base + 2, :]).then_inc(s_atc, 1)
                act.wait_ge(s_ln, 1)
                nc.scalar.activation(lg[:, :], ve[:, :], ACT.Ln).then_inc(s_hl, 1)
                act.wait_ge(s_hl, 2)
                nc.scalar.activation(rs[:, :], lg[:, :], ACT.Exp, scale=-0.5).then_inc(s_hr, 1)

            @block.tensor
            def _(pe):
                for b in range(B):
                    base = 4 * (b % 2)
                    pe.wait_ge(s_hng, b + 1)
                    if b >= 2:
                        pe.wait_ge(s_atc, b - 1)
                    for k in range(2):
                        for t in range(QB):
                            ins = nc.tensor.transpose(psum[:, base + k, t * P:(t + 1) * P],
                                                      attn[:, b, t].rearrange("p h d -> p (h d)")[:, k * P:(k + 1) * P],
                                                      ident[:, :])
                    ins.then_inc(s_at, 1)
                    pe.wait_ge(s_atc, b + 1)
                    if b >= 2:
                        pe.wait_ge(s_opc, b - 1)
                    for t in range(QB):
                        for k in range(2):
                            ins = nc.tensor.matmul(psum[:, base + 2, t * P:(t + 1) * P],
                                                   a_t[:, b % 2, k, t * P:(t + 1) * P], w_o[:, k, :],
                                                   start=(k == 0), stop=(k == 1))
                    ins.then_inc(s_op, 1)

            @block.vector
            def _(dve):
                link = dve_chain(dve)
                for b in range(B):
                    dve.wait_ge(s_sq, b + 1)
                    nc.vector.tensor_reduce(hv[:, b * QB * H:(b + 1) * QB * H],
                                            sq[:, b % 2].rearrange("p t h d -> p (t h) d"),
                                            AX.X, ALU.add).then_inc(s_ss, 1)
                dve.wait_ge(s_ss, B)
                nc.vector.tensor_scalar(hv[:, :], hv[:, :], 1.0 / (2 * DH), LN_EPS, ALU.mult, ALU.add)\
                  .then_inc(s_ss, 1)
                dve.wait_ge(s_hr, 1)
                link(nc.vector.tensor_tensor(ht[:, :], hy[:, :], hy[:, :], ALU.mult))
                link(nc.vector.tensor_tensor(ht[:, :], ht[:, :], hv[:, :], ALU.mult))
                link(nc.vector.tensor_scalar(ht[:, :], ht[:, :], -0.5, 1.5, ALU.mult, ALU.add))
                nc.vector.tensor_tensor(hy[:, :], hy[:, :], ht[:, :], ALU.mult).then_inc(s_hn, 1)
                for b in range(B):
                    dve.wait_ge(s_op, b + 1)
                    nc.vector.tensor_copy(ao[:, b * QB:(b + 1) * QB, :].rearrange("p t d -> p (t d)"),
                                          psum[:, 4 * (b % 2) + 2, :]).then_inc(s_opc, 1)
                dve.wait_ge(s_opc, B)
                row_stats(dve, link, lambda i: ao[:, i, :])
                nc.vector.memset(tn[:, :], 0.0).then_inc(s_ln, 1)
                dve.wait_ge(s_hr, 2)
                newton(dve, link, rs[:, :], ve[:, :], tn[:, :])
                for i in range(TILES):
                    ins = nc.vector.tensor_scalar(ao[:, i, :], ao[:, i, :], mv[:, i, 0:1], rs[:, i:i + 1],
                                                  ALU.subtract, ALU.mult)
                link(ins)
                link(nc.vector.tensor_tensor(x[:, :, :], x[:, :, :], ao[:, :, :], ALU.add))
                dve_steps[0] += link.n

        s_l2 = sem("s_l2")
        s_f1 = sem("s_f1")
        s_f2 = sem("s_f2")
        s_fy = sem("s_fy")
        s_xr = sem("s_xr")
        s_ft = sem("s_ft")
        s_ftc = sem("s_ftc")
        s_hid = sem("s_hid")
        s_gelu = sem("s_gelu")
        s_ff = sem("s_ff")
        s_ffc = sem("s_ffc")
        s_tu = sem("s_tu")
        s_tuc = sem("s_tuc")
        s_udma = sem("s_udma")
        s_r = sem("s_r")
        s_ra = sem("s_ra")
        s_zdone = sem("s_zdone")
        s_zt = sem("s_zt")
        s_ln2 = sem("s_ln2")
        s_out = sem("s_out")
        s_fin = sem("s_fin")
        with ExitStack() as local:
            def tmp(name, shape, dt=F32):
                return local.enter_context(nc.sbuf_tensor(name, shape, dt))
            xn2 = tmp("xn2", [P, TILES, D])
            prod = tmp("prod", [P, D])
            ss = tmp("ss", [P, TILES])
            u_col = tmp("u_col", [P, TILES])
            u_t = tmp("u_t", [TILES, P])
            xr_t = tmp("xr_t", [P, 2, N])
            hid = tmp("hid", [P, 2, 1 + HC, N])
            light = tmp("light", [P, TILES, D])
            heavy = tmp("heavy", [P, TILES, D])
            u = tmp("u", [B, N])
            z = tmp("z", [B, N])
            e = tmp("e", [B, N])
            f = tmp("f", [B, N])
            key = tmp("key", [B, 2, N])
            sel = tmp("sel", [B, N])
            top = tmp("top", [B, 8])
            umax = tmp("umax", [B, 1])
            zmax = tmp("zmax", [B, 1])
            zsum = tmp("zsum", [B, 1])
            beta = tmp("beta", [B, 1])
            nb = tmp("nb", [B, 1])
            ts = tmp("ts", [B, 1])
            tt = tmp("tt", [B, 1])
            wcol = tmp("wcol", [P, QB, B])
            block = local.enter_context(nc.Block())
            HID_BANKS = (1, 2, 3, 4)

            @block.scalar
            def _(act):
                act.wait_ge(s_l2, 1)
                nc.scalar.activation(lg[:, :], ve[:, :], ACT.Ln).then_inc(s_f1, 1)
                act.wait_ge(s_f1, 1)
                nc.scalar.activation(rs[:, :], lg[:, :], ACT.Exp, scale=-0.5).then_inc(s_f2, 1)
                act.wait_ge(s_l2, 2)
                nc.scalar.activation(lg[:, :], ss[:, :], ACT.Ln, scale=float(2 ** LOG_SHIFT)).then_inc(s_f1, 1)
                act.wait_ge(s_f1, 2)
                nc.scalar.activation(lg[:, :], lg[:, :], ACT.Exp, scale=-0.5, bias=shift_col[:, 0:1])\
                   .then_inc(s_f2, 1)
                def log_sum(n):
                    act.wait_ge(s_r, 3 * n + 1)
                    nc.scalar.activation(e[:, :], z[:, :], ACT.Exp, accum_out=zsum[:, :]).then_inc(s_ra, 1)
                    act.wait_ge(s_ra, 3 * n + 1)
                    nc.scalar.activation(zsum[:, :], zsum[:, :], ACT.Ln).then_inc(s_ra, 1)
                act.wait_ge(s_r, 1)
                nc.scalar.activation(e[:, :], z[:, :], ACT.Exp, accum_out=zsum[:, :]).then_inc(s_ra, 1)
                act.wait_ge(s_ra, 1)
                nc.scalar.activation(ts[:, :], zsum[:, :], ACT.Ln).then_inc(s_ra, 1)
                for r in range(REBASES):
                    act.wait_ge(s_r, 2 + 2 * r)
                    nc.scalar.activation(f[:, :], z[:, :], ACT.Exp).then_inc(s_ra, 1)
                    act.wait_ge(s_r, 3 + 2 * r)
                    nc.scalar.activation(ts[:, :], tt[:, :], ACT.Ln).then_inc(s_ra, 1)
                act.wait_ge(s_r, 2 + 2 * REBASES)
                nc.scalar.activation(e[:, :], z[:, :], ACT.Exp).then_inc(s_ra, 1)
                for b in range(B):
                    for c in range(1 + HC):
                        act.wait_ge(s_hid, (1 + HC) * b + c + 1)
                        if b >= 2 and c == 0:
                            act.wait_ge(s_ff, b - 1)
                        m = LIGHT if c == 0 else P
                        nc.scalar.activation(hid[0:m, b % 2, c, :], psum[0:m, HID_BANKS[((1 + HC) * b + c) % 4], :],
                                             ACT.Gelu, bias=b1c[0:m, c:c + 1]).then_inc(s_gelu, 1)
                act.wait_ge(s_ln2, 1)
                nc.scalar.activation(lg[:, :], ve[:, :], ACT.Ln).then_inc(s_f1, 1)
                act.wait_ge(s_f1, 3)
                nc.scalar.activation(rs[:, :], lg[:, :], ACT.Exp, scale=-0.5).then_inc(s_f2, 1)

            @block.tensor
            def _(pe):
                pe.wait_ge(s_fy, 1)
                nc.tensor.transpose(psum[0:TILES, 7, 0:P], u_col[:, :], ident[:, :]).then_inc(s_tu, 1)
                for b in range(B):
                    pe.wait_ge(s_xr, b + 1)
                    if b >= 1:
                        pe.wait_ge(s_ftc, b)
                    for t in range(QB):
                        ins = nc.tensor.transpose(psum[:, 0, t * P:(t + 1) * P], xn2[:, b * QB + t, :], ident[:, :])
                    ins.then_inc(s_ft, 1)
                    pe.wait_ge(s_ftc, b + 1)
                    for c in range(1 + HC):
                        n = (1 + HC) * b + c
                        if n >= 4:
                            pe.wait_ge(s_gelu, n - 3)
                        m = LIGHT if c == 0 else P
                        w0 = 0 if c == 0 else LIGHT + (c - 1) * P
                        nc.tensor.matmul(psum[0:m, HID_BANKS[n % 4], :], w1g[:, w0:w0 + m], xr_t[:, b % 2, :],
                                         start=True, stop=True).then_inc(s_hid, 1)
                    pe.wait_ge(s_gelu, (1 + HC) * (b + 1))
                    if b >= 1:
                        pe.wait_ge(s_ffc, b)
                    for t in range(QB):
                        nc.tensor.matmul(psum[:, 5, t * P:(t + 1) * P], hid[0:LIGHT, b % 2, 0, t * P:(t + 1) * P],
                                         w2l[:, :], start=True, stop=True)
                        for c in range(HC):
                            ins = nc.tensor.matmul(psum[:, 6, t * P:(t + 1) * P],
                                                   hid[:, b % 2, 1 + c, t * P:(t + 1) * P], w2h[:, c, :],
                                                   start=(c == 0), stop=(c == HC - 1))
                    ins.then_inc(s_ff, 1)
                pe.wait_ge(s_zdone, 1)
                for t in range(QB):
                    ins = nc.tensor.transpose(psum[:, 7, t * B:(t + 1) * B], sel[:, t * P:(t + 1) * P],
                                              ident[0:B, 0:B])
                ins.then_inc(s_zt, 1)

            @block.gpsimd
            def _(pool):
                for b in range(B):
                    pool.wait_ge(s_ft, b + 1)

            @block.sync
            def _(sp):
                sp.wait_ge(s_tuc, 1)
                sp.dma_start(u_dram[:, :], u_t[:, :]).then_inc(s_udma, 16)
                sp.wait_ge(s_udma, 16)
                sp.dma_start(u[:, :], u_dram.rearrange("(b t) p -> b (t p)", b=B)).then_inc(s_udma, 16)
                for b in range(B):
                    sp.wait_ge(s_fin, b + 1)
                    sp.dma_start(out[b].rearrange("(t p) d -> p t d", p=P), heavy[:, b * QB:(b + 1) * QB, :])\
                      .then_inc(s_out, 16)
                sp.wait_ge(s_out, 16 * B)

            @block.vector
            def _(dve):
                link = dve_chain(dve)
                row_stats(dve, link, lambda i: x[:, i, :])
                nc.vector.memset(tn[:, :], 0.0).then_inc(s_l2, 1)
                dve.wait_ge(s_f2, 1)
                newton(dve, link, rs[:, :], ve[:, :], tn[:, :])
                link(nc.vector.tensor_tensor(ss[:, :], rs[:, :], rs[:, :], ALU.mult))
                link(nc.vector.tensor_tensor(ss[:, :], ss[:, :], mv[:, :, 1], ALU.mult))
                link(nc.vector.tensor_scalar(ss[:, :], ss[:, :], float(D), 1e-24, ALU.mult, ALU.max))
                nc.vector.memset(tn[:, :], 0.0).then_inc(s_l2, 1)
                for i in range(TILES):
                    ins = nc.vector.tensor_scalar(xn2[:, i, :], x[:, i, :], mv[:, i, 0:1], rs[:, i:i + 1],
                                                  ALU.subtract, ALU.mult)
                link(ins)
                for i in range(TILES):
                    ins = nc.vector.tensor_tensor_reduce(out=prod[:, :], in0=xn2[:, i, :], in1=route_row[:, :],
                                                         scale=1.0, scalar=0.0, op0=ALU.mult, op1=ALU.add,
                                                         accum_out=u_col[:, i:i + 1])
                    link(ins)
                nc.vector.tensor_scalar(u_col[:, :], u_col[:, :], 10.0, None, ALU.mult).then_inc(s_fy, 1)
                dve.wait_ge(s_f2, 2)
                newton(dve, link, lg[:, :], ss[:, :], tn[:, :])
                link(nc.vector.tensor_scalar(lg[:, :], lg[:, :], float(D) ** 0.5, None, ALU.mult))
                for b in range(B):
                    for i in range(b * QB, (b + 1) * QB):
                        ins = nc.vector.tensor_scalar(xn2[:, i, :], xn2[:, i, :], lg[:, i:i + 1], None, ALU.mult)
                    ins.then_inc(s_xr, 1)
                dve.wait_ge(s_tu, 1)
                nc.vector.tensor_copy(u_t[:, :], psum[0:TILES, 7, 0:P]).then_inc(s_tuc, 1)
                dve.wait_ge(s_udma, 32)
                link(nc.vector.reduce_max(umax[:, :], u[:, :], AX.X))
                link(nc.vector.tensor_scalar(zmax[:, :], umax[:, :], 0.0, None, ALU.min))
                nc.vector.tensor_scalar(z[:, :], u[:, :], 0.0, zmax[:, 0:1], ALU.min, ALU.subtract).then_inc(s_r, 1)
                dve.wait_ge(s_ra, 2)
                link(nc.vector.tensor_scalar(beta[:, :], ts[:, :], zmax[:, 0:1], LOG_K, ALU.add, ALU.subtract))
                steps = 0
                for r in range(REBASES):
                    nc.vector.tensor_scalar(z[:, :], u[:, :], beta[:, 0:1], CLIP, ALU.subtract, ALU.min)\
                      .then_inc(s_r, 1)
                    link(nc.vector.memset(tt[:, :], 1.0))
                    dve.wait_ge(s_ra, 3 + 2 * r)
                    for _ in range(min(REBASE, ITERS - 1 - REBASE * r)):
                        link(nc.vector.tensor_scalar(key[:, 0, :], f[:, :], tt[:, 0:1], None, ALU.min, ALU.add,
                                                     accum_out=ts[:, :]))
                        link(nc.vector.tensor_scalar(tt[:, :], ts[:, :], 1.0 / K_ROUTE, None, ALU.mult))
                        steps += 1
                    nc.vector.tensor_copy(nb[:, :], tt[:, :]).then_inc(s_r, 1)
                    dve.wait_ge(s_ra, 4 + 2 * r)
                    link(nc.vector.tensor_tensor(beta[:, :], beta[:, :], ts[:, :], ALU.add))
                assert steps == ITERS - 1
                nc.vector.tensor_scalar(z[:, :], u[:, :], beta[:, 0:1], 0.0, ALU.subtract, ALU.min).then_inc(s_r, 1)
                dve.wait_ge(s_r, 2 + 2 * REBASES)
                link(nc.vector.tensor_scalar(key[:, 0, :], z[:, :], CUT, None, ALU.max))
                for k in range(TOPK // 8):
                    link(nc.vector.max(top[:, :], key[:, k % 2, :]))
                    link(nc.vector.match_replace(out=key[:, (k + 1) % 2, :], in_to_replace=top[:, :],
                                                 in_values=key[:, k % 2, :], imm_value=2 * CUT))
                link(nc.vector.tensor_scalar(sel[:, :], key[:, (TOPK // 8) % 2, :], 1.5 * CUT, None, ALU.is_lt))
                dve.wait_ge(s_ra, 3 + 2 * REBASES)
                link(nc.vector.tensor_scalar(f[:, :], e[:, :], -1.0, 1.0, ALU.mult, ALU.add))
                link(nc.vector.tensor_tensor(e[:, :], e[:, :], f[:, :], ALU.add))
                nc.vector.tensor_tensor(sel[:, :], sel[:, :], e[:, :], ALU.mult).then_inc(s_zdone, 1)
                for b in range(B):
                    dve.wait_ge(s_ft, b + 1)
                    if b >= 2:
                        dve.wait_ge(s_hid, (1 + HC) * (b - 1))
                    nc.vector.tensor_copy(xr_t[:, b % 2, :], psum[:, 0, :]).then_inc(s_ftc, 1)
                    dve.wait_ge(s_ff, b + 1)
                    row = slice(b * QB, (b + 1) * QB)
                    nc.vector.tensor_tensor(light[:, row, :], psum[:, 5, :].rearrange("p (t d) -> p t d", t=QB),
                                            b2[:, 0:1, :].to_broadcast([P, QB, D]), ALU.add)
                    ins = nc.vector.tensor_tensor(heavy[:, row, :], psum[:, 6, :].rearrange("p (t d) -> p t d", t=QB),
                                                  b2[:, 1:2, :].to_broadcast([P, QB, D]), ALU.add)
                    ins.then_inc(s_ffc, 1)
                dve.wait_ge(s_ffc, B)
                dve.wait_ge(s_zt, 1)
                link(nc.vector.tensor_copy(wcol[:, :, :].rearrange("p t b -> p (t b)"), psum[:, 7, 0:TILES]))
                for i in range(TILES):
                    ins = nc.vector.scalar_tensor_tensor(out=heavy[:, i, :], in0=heavy[:, i, :],
                                                         scalar=wcol[:, i % QB, i // QB:i // QB + 1],
                                                         in1=light[:, i, :], op0=ALU.mult, op1=ALU.add)
                link(ins)
                row_stats(dve, link, lambda i: heavy[:, i, :])
                nc.vector.memset(tn[:, :], 0.0).then_inc(s_ln2, 1)
                dve.wait_ge(s_f2, 3)
                newton(dve, link, rs[:, :], ve[:, :], tn[:, :])
                for b in range(B):
                    for i in range(b * QB, (b + 1) * QB):
                        ins = nc.vector.tensor_scalar(heavy[:, i, :], heavy[:, i, :], mv[:, i, 0:1], rs[:, i:i + 1],
                                                      ALU.subtract, ALU.mult)
                    link(ins)
                    row = slice(b * QB, (b + 1) * QB)
                    nc.vector.tensor_tensor(heavy[:, row, :], heavy[:, row, :], x[:, row, :],
                                            ALU.add).then_inc(s_fin, 1)
                dve_steps[0] += link.n


_INS = ['L0_attn_X', 'L0_attn_W_q', 'L0_attn_W_k', 'L0_attn_W_v', 'L0_attn_W_o', 'L0_attn_lambda_q1',
        'L0_attn_lambda_k1', 'L0_attn_lambda_q2', 'L0_attn_lambda_k2', 'L0_attn_rms_scale',
        'L0_ffn_routing_token', 'L0_ffn_gamma_light', 'L0_ffn_w1_light', 'L0_ffn_b1_light', 'L0_ffn_w2_light',
        'L0_ffn_b2_light', 'L0_ffn_gamma_heavy', 'L0_ffn_w1_heavy', 'L0_ffn_b1_heavy', 'L0_ffn_w2_heavy',
        'L0_ffn_b2_heavy']


def kernel(**inputs):
    import numpy as _np
    import concourse.bacc as _bacc
    from concourse import mybir as _mybir
    from concourse.bass_utils import run_bass_kernel_spmd as _run

    nc = _bacc.Bacc("TRN2", target_bir_lowering=False, num_devices=1)
    arrays, args = {}, []
    for name in _INS:
        a = _np.ascontiguousarray(inputs[name])
        arrays[f"in_{name}_dram"] = a
        args.append(nc.dram_tensor(f"in_{name}_dram", a.shape, _mybir.dt.from_np(a.dtype), kind="ExternalInput").ap())
    args.append(nc.dram_tensor("out_0_dram", (B, N, D), F32, kind="ExternalOutput").ap())
    program(nc, *args)
    r = _run(nc, [arrays], core_ids=[0])
    return r.results[0]["out_0_dram"]
```

```python
from contextlib import ExitStack

import concourse.bass as bass
from concourse import mybir

F32 = mybir.dt.float32
BF16 = mybir.dt.bfloat16
U32 = mybir.dt.uint32
ALU = mybir.AluOpType
ACT = mybir.ActivationFunctionType
AX = mybir.AxisListType

P = 128
B = 8
N = 512
D = 128
H = 16
DH = 8
QB = N // P
TILES = B * QB
D2 = 2 * DH * H
COMBOS = 2 * H
PAIRS = H // 2
SPLITS = 6
KR = SPLITS * DH
KM = KR + 3
HV = 2 * DH + 1
LIGHT = 64
HEAVY = 512
HC = HEAVY // P
TOPK = 128
ITERS = 50
K_ROUTE = 8.0
REBASE = 13
T_SHIFT = 16
CLIP = 60.0
GELUS_BESIDE = (1, 1, 1, 1)
LN_EPS = 1e-5
NEG = -1.0e30
CUT = -87.3365
SCALE = float(DH) ** -0.5
GROUPS = 5
REBASES = -(-(ITERS - 1) // REBASE)
LAMBDA_INIT = 0.8
LN2 = 0.6931471805599453
LOG_K = 2.0794415416798357
LOG_SHIFT = 32


class Chain:

    def __init__(self, engine, done, start=0):
        self.engine, self.done, self.start, self.n = engine, done, start, 0

    def __call__(self, instruction):
        self.n += 1
        instruction.then_inc(self.done, 1)
        self.engine.wait_ge(self.done, self.start + self.n)


def program(nc, X, Wq, Wk, Wv, Wo, lq1, lk1, lq2, lk2, rms_scale, route, g_l, w1_l, b1_l, w2_l, b2_l,
            g_h, w1_h, b1_h, w2_h, b2_h, out):
    ctx = ExitStack()
    with ctx:
        ctx.enter_context(nc.allow_non_contiguous_dma("small vectors and rearranged scratch"))

        def sb(name, shape, dt=F32):
            return ctx.enter_context(nc.sbuf_tensor(name, shape, dt))

        def sem(name):
            return ctx.enter_context(nc.semaphore(name))

        q_dram = nc.dram_tensor("q_scratch", (B, COMBOS, KM, N), BF16, kind="Internal").ap()
        k_dram = nc.dram_tensor("k_scratch", (B, COMBOS, KR, N), BF16, kind="Internal").ap()
        v_dram = nc.dram_tensor("v_scratch", (B, P, PAIRS, QB * 2 * HV), F32, kind="Internal").ap()

        ident = sb("ident", [P, P])
        ident_bf = sb("ident_bf", [P, P], BF16)
        causal_bf = sb("causal_bf", [P, P], BF16)
        shift_col = sb("shift_col", [P, 1])
        w_rows = sb("w_rows", [P, 8, P])
        w_qkv = sb("w_qkv", [P, 6, P])
        w_o = sb("w_o", [P, 2, P])
        o_scale = sb("o_scale", [P, 1])
        lam_in = sb("lam_in", [P, 4, H * DH])
        lam_prod = sb("lam_prod", [P, 2, H * DH])
        lam_sum = sb("lam_sum", [P, 2, H])
        coef = sb("coef", [P, H, 2])
        route_row = sb("route_row", [P, D])
        w1 = sb("w1", [P, LIGHT + HEAVY])
        w1g = sb("w1g", [P, LIGHT + HEAVY])
        gam = sb("gam", [P, 2])
        b1c = sb("b1c", [P, 1 + HC])
        w2h = sb("w2h", [P, HC, D])
        w2l = sb("w2l", [LIGHT + 1, D])
        b2 = sb("b2", [P, 1, D])

        x = sb("x", [P, TILES, D])
        attn = sb("attn", [P, B, QB, H, 2 * DH])
        hv = sb("hv", [P, B * QB * H])
        hy = sb("hy", [P, B * QB * H])
        ht = sb("ht", [P, B * QB * H])
        st = sb("st", [P, TILES, 6])
        mv = sb("mv", [P, TILES, 2])
        ve = sb("ve", [P, TILES])
        lg = sb("lg", [P, TILES])
        rs = sb("rs", [P, TILES])
        tn = sb("tn", [P, TILES])

        stacks = ctx.enter_context(ExitStack())
        q_st = stacks.enter_context(nc.sbuf_tensor("q_st", [P, 2 * PAIRS, N], BF16))
        k_st = stacks.enter_context(nc.sbuf_tensor("k_st", [P, COMBOS, N], BF16))
        v_aug = stacks.enter_context(nc.sbuf_tensor("v_aug", [P, PAIRS, QB * 2 * HV], F32))
        v_out = stacks.enter_context(nc.sbuf_tensor("v_out", [P, 2, PAIRS, QB, 2, HV], F32))
        probs_flat = stacks.enter_context(nc.sbuf_tensor("probs", [P, 2 * GROUPS * 2 * N], F32))
        probs = probs_flat[:, :].rearrange("p (s g a n) -> p s g a n", s=2, g=GROUPS, a=2)
        parts = probs_flat[:, 0:2 * 4 * 3 * N // 2].bitcast(BF16)\
            .rearrange("p (s i a n) -> p s i a n", s=2, i=4, a=3)

        psum = ctx.enter_context(nc.psum_tensor("psum", [P, 8, N], F32))

        s_pool_go = sem("s_pool_go")
        s_x = [sem(f"s_x{h}") for h in range(2)]
        s_w = sem("s_w")
        s_const = sem("s_const")
        s_kones = sem("s_kones")
        s_wr = sem("s_wr")
        s_dve = sem("s_dve")
        s_stat = sem("s_stat")
        s_log = sem("s_log")
        s_exp0 = sem("s_exp0")
        s_wt = sem("s_wt")
        dve_steps = [0]

        def dve_chain(dve):
            return Chain(dve, s_dve, dve_steps[0])

        def newton(dve, link, y, v, t):
            link(nc.vector.tensor_tensor(t, y, y, ALU.mult))
            link(nc.vector.tensor_tensor(t, t, v, ALU.mult))
            link(nc.vector.tensor_scalar(t, t, -0.5, 1.5, ALU.mult, ALU.add))
            link(nc.vector.tensor_tensor(y, y, t, ALU.mult))

        def half_tiles(h):
            return slice(h * TILES // 2, (h + 1) * TILES // 2)

        def input_means(dve, link, h):
            s = half_tiles(h)
            for i in range(s.start, s.stop):
                ins = nc.vector.bn_stats(st[:, i, :], x[:, i, :])
            link(ins)
            for i in range(s.start, s.stop):
                ins = nc.vector.bn_aggr(mv[:, i, :], st[:, i, :])
            link(ins)
            nc.vector.tensor_scalar(ve[:, s], mv[:, s, 1], LN_EPS, None, ALU.add).then_inc(s_stat, 1)

        def input_roots(act, h):
            s = half_tiles(h)
            act.wait_ge(s_stat, h + 1)
            nc.scalar.activation(lg[:, s], ve[:, s], ACT.Ln).then_inc(s_log, 1)
            act.wait_ge(s_log, h + 1)
            nc.scalar.activation(rs[:, s], lg[:, s], ACT.Exp, scale=-0.5).then_inc(s_exp0, 1)

        def input_newton(dve, link, h):
            s = half_tiles(h)
            dve.wait_ge(s_exp0, h + 1)
            newton(dve, link, rs[:, s], ve[:, s], tn[:, s])

        row = lambda v: v.rearrange("(a n) -> a n", a=1)
        col = lambda v: v.rearrange("(d a) -> d a", a=1)
        small_inputs = [(o_scale[r * 2 * DH:(r + 1) * 2 * DH, :], col(rms_scale)) for r in range(P // (2 * DH))]
        small_inputs += [(lam_in[:, i, :], L.rearrange("h d -> (h d)").rearrange("(a n) -> a n", a=1)
                   .to_broadcast([P, H * DH])) for i, L in enumerate((lq1, lq2, lk1, lk2))]
        small_inputs += [(route_row[:, :], row(route).to_broadcast([P, D])),
                  (w1[:, 0:LIGHT], w1_l), (w1[:, LIGHT:], w1_h),
                  (gam[:, 0:1], col(g_l)), (gam[:, 1:2], col(g_h)),
                  (b1c[0:LIGHT, 0:1], col(b1_l)), (b1c[:, 1:], b1_h.rearrange("(c p) -> p c", p=P)),
                  (w2h[:, :, :], w2_h.rearrange("(c p) d -> p c d", p=P)), (w2l[0:LIGHT, :], w2_l),
                  (w2l[LIGHT:LIGHT + 1, :], row(b2_l)),
                  (b2[:, 0, :], row(b2_h).to_broadcast([P, D]))]
        with nc.Block() as block:
            @block.sync
            def _(sp):
                def load_x(rows_, s_x_half):
                    for b in rows_:
                        sp.dma_start(x[:, b * QB:(b + 1) * QB, :],
                                     X[b].rearrange("(t p) d -> p t d", p=P)).then_inc(s_x_half, 16)

                load_x(range(B // 2), s_x[0])
                for w, W in enumerate((Wq, Wk, Wv)):
                    for t in range(2):
                        sp.dma_start(w_rows[:, 2 * w + t, :], W[t * P:(t + 1) * P, :]).then_inc(s_wr, 16)
                for t in range(2):
                    sp.dma_start(w_rows[:, 6 + t, :], Wo[:, t * P:(t + 1) * P]).then_inc(s_wr, 16)
                load_x(range(B // 2, B), s_x[1])

            @block.gpsimd
            def _(pool):
                nc.gpsimd.memset(ident[:, :], 0.0).then_inc(s_const, 1)
                nc.gpsimd.memset(ident_bf[:, :], 0.0).then_inc(s_const, 1)
                nc.gpsimd.memset(causal_bf[:, :], 0.0).then_inc(s_const, 1)
                nc.gpsimd.memset(shift_col[:, :], 0.5 * LOG_SHIFT * LN2).then_inc(s_const, 1)
                pool.wait_ge(s_const, 4)
                for tile, op, fill in ((ident, ALU.not_equal, 1.0), (ident_bf, ALU.not_equal, 1.0),
                                       (causal_bf, ALU.is_ge, NEG)):
                    nc.gpsimd.affine_select(out=tile[:, :], in_=tile[:, :], compare_op=op, fill=fill, base=0,
                                            pattern=[[-1, P]], channel_multiplier=1).then_inc(s_const, 1)
                nc.gpsimd.memset(q_st[:, :, :].bitcast(U32), 0).then_inc(s_kones, 1)
                for half in range(2):
                    pool.wait_ge(s_kones, 1 + half)
                    nc.gpsimd.memset(k_st[64 * half:64 * half + 64, 1 - half::2, :].bitcast(U32), 0)\
                      .then_inc(s_kones, 1)

            @block.tensor
            def _(pe):
                pe.wait_ge(s_const, 7)
                pe.wait_ge(s_wr, 16 * 8)
                for i in range(8):
                    ins = nc.tensor.transpose(psum[:, i // 4, (i % 4) * P:(i % 4 + 1) * P], w_rows[:, i, :], ident[:, :])
                ins.then_inc(s_wt, 1)

            @block.vector
            def _(dve):
                link = dve_chain(dve)
                dve.wait_ge(s_x[0], 16 * B // 2)
                input_means(dve, link, 0)
                nc.vector.memset(coef[:, :, 0], 1.0)
                dve.wait_ge(s_wt, 1)
                nc.vector.tensor_copy(w_qkv[:, :, :].rearrange("p a n -> p (a n)"),
                                      psum[:, 0:2, :].rearrange("p a n -> p (a n)")[:, 0:6 * P])
                link(nc.vector.tensor_copy(w_o[:, :, :].rearrange("p a n -> p (a n)"), psum[:, 1, 2 * P:4 * P]))
                dve.wait_ge(s_x[1], 16 * B // 2)
                input_means(dve, link, 1)
                input_newton(dve, link, 0)
                dve_steps[0] += link.n

            @block.scalar
            def _(act):
                input_roots(act, 0)

        s_xn = sem("s_xn")
        s_xt = sem("s_xt")
        s_xtc = sem("s_xtc")
        s_proj = sem("s_proj")
        s_hi = sem("s_hi")
        s_res = sem("s_res")
        s_mid = sem("s_mid")
        s_low = sem("s_low")
        s_vp = sem("s_vp")
        s_v = sem("s_v")
        s_ones = sem("s_ones")
        s_zrow = sem("s_zrow")
        s_zout = sem("s_zout")
        s_qk_out = [sem(f"s_qk_out{s}") for s in range(2)]
        s_v_out = [sem(f"s_v_out{s}") for s in range(2)]
        Q_RUNS = ((0, 3), (0, 2), (0, 1))
        K_RUNS = ((0, 3), (1, 2), (2, 1))
        QK_OUT = 2 * 2 * 3 * 16
        EARLY_LOADS = 2
        s_load = [sem(f"s_load{p}") for p in range(PAIRS)]

        def written(sp, b):
            if isinstance(b, int) and b < 2:
                sp.wait_ge(s_qk_out[b], QK_OUT)
                sp.wait_ge(s_v_out[b], 16)
                sp.wait_ge(s_zout, 16 * B)
            else:
                for s in range(2):
                    sp.wait_ge(s_qk_out[s], QK_OUT * B // 2)
                    sp.wait_ge(s_v_out[s], 16 * B // 2)

        def load(sp, at):
            b, p, _ = at
            for half in range(2):
                src = slice(4 * p + half, 4 * p + half + 3, 2)
                sp.dma_start(q_st[64 * half:64 * half + KM, 2 * p:2 * p + 2, :],
                             q_dram[b, src].rearrange("s r n -> r s n")).then_inc(s_load[p], 16)
                sp.dma_start(k_st[64 * half:64 * half + KR, src, :],
                             k_dram[b, src].rearrange("s r n -> r s n")).then_inc(s_load[p], 16)

        def slot(i, part):
            return part if i < 2 else 2 - part

        def positive(count):
            return not isinstance(count, int) or count > 0

        def over_row_pairs(engine, body):
            for s in range(2):
                body(0, s, True)
            with engine.Fori(1, B // 2 - 1) as j:
                for s in range(2):
                    body(j, s, True)
            for s in range(2):
                body(B // 2 - 1, s, s == 0)

        with ExitStack() as local:
            def tmp(name, shape, dt=F32):
                return local.enter_context(nc.sbuf_tensor(name, shape, dt))
            xn = tmp("xn", [P, 2, QB, D])
            xn_t = tmp("xn_t", [P, 2, N])
            res = tmp("res", [P, 4, N])
            zrow = tmp("zrow", [COMBOS, (KM - KR) * N], BF16)
            block = local.enter_context(nc.Block())

            @block.gpsimd
            def _(pool):
                nc.gpsimd.memset(v_out[:, :, :, :, :, :], 1.0).then_inc(s_ones, 1)
                nc.gpsimd.memset(zrow[:, :], 0.0).then_inc(s_zrow, 1)

                def body(j, s, _):
                    b = 2 * j + s
                    for i in range(4):
                        pool.wait_ge(s_mid, 4 * b + i + 1)
                        pool.sem_inc(s_pool_go, 1)
                        nc.gpsimd.tensor_tensor(parts[:, s, i, slot(i, 2), :], res[:, i, :], parts[:, s, i, 1, :],
                                                ALU.subtract).then_inc(s_low, 1)
                    if isinstance(j, int) and j == 0:
                        pool.wait_ge(s_low, 4 * (b + 1))
                        nc.gpsimd.memset(k_st[64 * s:64 * s + 64, s::2, :], 1.0).then_inc(s_kones, 1)
                        pool.wait_ge(s_kones, 4 + s)

                over_row_pairs(pool, body)

            @block.vector
            def _(dve):
                def normed(b, s):
                    for t in range(QB):
                        i = b * QB + t
                        m, r = (mv[:, i, 0:1], rs[:, i:i + 1]) if isinstance(i, int) else \
                            (mv[:, i, 0:1], rs[:, bass.ds(i, 1)])
                        nc.vector.tensor_scalar(xn[:, s, t, :], x[:, i, :], m, r,
                                                ALU.subtract, ALU.mult).then_inc(s_xn, 1)

                def body(j, s, more):
                    b = 2 * j + s
                    if more:
                        if positive(b):
                            dve.wait_ge(s_xt, b)
                        normed(b + 1, 1 - s)
                    for i in range(4):
                        dve.wait_ge(s_hi, 4 * b + i + 1)
                        if positive(b):
                            dve.wait_ge(s_low, 4 * b + i - 3)
                        nc.vector.tensor_tensor(res[:, i, :], psum[:, 1 + i, :], parts[:, s, i, slot(i, 0), :],
                                                ALU.subtract).then_inc(s_res, 1)
                    for t in range(QB):
                        if t == 0:
                            if isinstance(b, int) and b == 0:
                                dve.wait_ge(s_ones, 1)
                            if positive(j):
                                dve.wait_ge(s_v_out[s], 16 * j)
                        dve.wait_ge(s_vp, QB * b + (t | 1) + 1)
                        nc.vector.tensor_copy(
                            v_out[:, s, :, t, :, 0:2 * DH],
                            psum[:, 5 + t // 2, (t % 2) * D2:(t % 2 + 1) * D2]
                            .rearrange("p (a h d) -> p a h d", a=PAIRS, h=2)).then_inc(s_v, 1)
                    if isinstance(j, int) and b == 1:
                        input_newton(dve, link, 1)

                link = dve_chain(dve)
                normed(0, 0)
                over_row_pairs(dve, body)
                dve.wait_ge(s_w, 16 * len(small_inputs))
                link(nc.vector.tensor_tensor(lam_prod[:, :, :], lam_in[:, 0:2, :], lam_in[:, 2:4, :], ALU.mult))
                nc.vector.tensor_reduce(lam_sum[:, :, :], lam_prod[:, :, :].rearrange("p a (h d) -> p a h d", d=DH),
                                        AX.X, ALU.add).then_inc(s_stat, 1)
                link(nc.vector.tensor_scalar(o_scale[:, :], o_scale[:, :], 1.0 - LAMBDA_INIT, None, ALU.mult))
                nc.vector.tensor_scalar(w_o[:, :, :], w_o[:, :, :], o_scale[:, 0:1], None, ALU.mult)
                nc.vector.tensor_scalar(w1g[:, 0:LIGHT], w1[:, 0:LIGHT], gam[:, 0:1], None, ALU.mult)
                nc.vector.tensor_scalar(w1g[:, LIGHT:], w1[:, LIGHT:], gam[:, 1:2], None, ALU.mult)
                dve.wait_ge(s_exp0, 3)
                link(nc.vector.tensor_tensor(coef[:, :, 1], lam_sum[:, 1, :], lam_sum[:, 0, :], ALU.subtract))
                link(nc.vector.tensor_scalar(coef[:, :, 1], coef[:, :, 1], -LAMBDA_INIT, None, ALU.add))
                dve_steps[0] += link.n

            @block.tensor
            def _(pe):
                def transposed(b, s):
                    pe.wait_ge(s_xn, QB * (b + 1))
                    for t in range(QB):
                        ins = nc.tensor.transpose(psum[:, 0, t * P:(t + 1) * P], xn[:, s, t, :], ident[:, :])
                    ins.then_inc(s_xt, 1)

                def body(j, s, more):
                    b = 2 * j + s
                    pe.wait_ge(s_xtc, b + 1)
                    for i in range(4):
                        if positive(b):
                            pe.wait_ge(s_res, 4 * b + i - 3)
                        nc.tensor.matmul(psum[:, 1 + i, :], w_qkv[:, i, :], xn_t[:, s, :],
                                         start=True, stop=True).then_inc(s_proj, 1)
                    if more:
                        transposed(b + 1, 1 - s)
                    for t in range(QB):
                        if positive(b) and t % 2 == 0:
                            pe.wait_ge(s_v, QB * b + t - 2)
                        nc.tensor.matmul(psum[:, 5 + t // 2, (t % 2) * D2:(t % 2 + 1) * D2],
                                         xn_t[:, s, t * P:(t + 1) * P],
                                         w_qkv[:, 4:6, :].rearrange("p a n -> p (a n)"),
                                         start=True, stop=True).then_inc(s_vp, 1)

                transposed(0, 0)
                over_row_pairs(pe, body)

            @block.scalar
            def _(act):
                def copied(b, s):
                    act.wait_ge(s_xt, b + 1)
                    if positive(b - 1):
                        act.wait_ge(s_vp, QB * (b - 1))
                    nc.scalar.copy(xn_t[:, s, :], psum[:, 0, :]).then_inc(s_xtc, 1)

                def middle(b, s, i):
                    act.wait_ge(s_res, 4 * b + i + 1)
                    nc.scalar.copy(parts[:, s, i, 1, :], res[:, i, :]).then_inc(s_mid, 1)

                def body(j, s, more):
                    b = 2 * j + s
                    if positive(j):
                        act.wait_ge(s_qk_out[s], QK_OUT * j)
                    for i in range(4):
                        act.wait_ge(s_proj, 4 * b + i + 1)
                        nc.scalar.copy(parts[:, s, i, slot(i, 0), :], psum[:, 1 + i, :]).then_inc(s_hi, 1)
                        if i > 0:
                            middle(b, s, i - 1)
                    if more:
                        copied(b + 1, 1 - s)
                    middle(b, s, 3)
                    if isinstance(j, int) and b == 0:
                        input_roots(act, 1)

                copied(0, 0)
                over_row_pairs(act, body)
                act.wait_ge(s_stat, 3)
                nc.scalar.activation(lam_sum[:, :, :], lam_sum[:, :, :], ACT.Exp).then_inc(s_exp0, 1)

            @block.sync
            def _(sp):
                for dst, src in small_inputs:
                    sp.dma_start(dst, src).then_inc(s_w, 16)

                def body(j, s, more):
                    b = 2 * j + s
                    if not more:
                        written(sp, 0)
                        sp.wait_ge(s_kones, 5)
                        for p in range(EARLY_LOADS):
                            load(sp, (0, p, p))
                    for which, dram, runs in ((0, q_dram, Q_RUNS), (1, k_dram, K_RUNS)):
                        for t in range(2):
                            i = 2 * which + t
                            sp.wait_ge(s_low, 4 * b + i + 1)
                            first_row = 0
                            for first, count in runs:
                                sp.dma_start(dram[b, t * H:(t + 1) * H, 0:KR, :]
                                             .rearrange("c (d j) n -> c d j n", j=SPLITS)[:, :, first_row:first_row + count, :],
                                             parts[:, s, i, first:first + count, :]).then_inc(s_qk_out[s], 16)
                                first_row += count
                    if isinstance(j, int) and b == 0:
                        sp.wait_ge(s_zrow, 1)
                        for row_ in range(B):
                            sp.dma_start(q_dram[row_, :, KR:KM, :], zrow[:, :].rearrange("c (r n) -> c r n", n=N))\
                              .then_inc(s_zout, 16)
                    sp.wait_ge(s_v, QB * (b + 1))
                    sp.dma_start(v_dram[b], v_out[:, s].rearrange("p a t h v -> p a (t h v)"))\
                      .then_inc(s_v_out[s], 16)

                over_row_pairs(sp, body)

        s_vload = [sem(f"s_vload{p}") for p in range(PAIRS)]
        s_mrow = [sem(f"s_mrow{p}") for p in range(PAIRS)]
        s_score = sem("s_score")
        s_prob = sem("s_prob")
        s_masked = sem("s_masked")
        s_pv = sem("s_pv")
        s_pvc = sem("s_pvc")
        s_ot = sem("s_ot")
        s_oh = sem("s_oh")
        s_rec = sem("s_rec")
        s_recl = sem("s_recl")
        s_o = sem("s_o")
        s_sq = sem("s_sq")
        s_ss = sem("s_ss")
        s_max = sem("s_max")
        s_maxr = sem("s_maxr")
        s_msplit = sem("s_msplit")
        s_mchain = sem("s_mchain")
        s_mt = sem("s_mt")
        s_mtc = sem("s_mtc")
        s_zero = sem("s_zero")
        s_hv = sem("s_hv")
        s_hl = sem("s_hl")
        s_hr = sem("s_hr")
        s_hn = sem("s_hn")
        s_hng_pool = sem("s_hng_pool")
        s_hng_dve = sem("s_hng_dve")
        NORMED_BY_DVE = (1, 3, 5)
        NORMED_EARLY = (0, 2)
        HEAD_PARTS = ((0, B - 1), (B - 1, B))

        def is_last(b):
            return isinstance(b, int) and b == B - 1

        def head_part(buf, k):
            first, end = HEAD_PARTS[k]
            return buf[:, first * QB * H:end * QB * H]

        def head_means(k):
            v = head_part(hv, k)
            nc.vector.tensor_scalar(v, v, 1.0 / (2 * DH), LN_EPS, ALU.mult, ALU.add).then_inc(s_hv, 1)

        def head_roots(act, k):
            act.wait_ge(s_hv, k + 1)
            nc.scalar.activation(head_part(ht, k), head_part(hv, k), ACT.Ln).then_inc(s_hl, 1)
            act.wait_ge(s_hl, k + 1)
            nc.scalar.activation(head_part(hy, k), head_part(ht, k), ACT.Exp, scale=-0.5).then_inc(s_hr, 1)

        def head_newton(dve, link, k):
            dve.wait_ge(s_hr, k + 1)
            y, t = head_part(hy, k), head_part(ht, k)
            link(nc.vector.tensor_tensor(t, y, y, ALU.mult))
            link(nc.vector.tensor_tensor(t, t, head_part(hv, k), ALU.mult))
            link(nc.vector.tensor_scalar(t, t, -0.5, 1.5, ALU.mult, ALU.add))
            nc.vector.tensor_tensor(y, y, t, ALU.mult).then_inc(s_hn, 1)

        def normed_heads(engine, b):
            a, r = attn[:, b], hy[:, b * QB * H:(b + 1) * QB * H].rearrange("p (t h) -> p t h", t=QB)
            return engine.tensor_tensor(a, a, r[:, :, :, None].to_broadcast([P, QB, H, 2 * DH]), ALU.mult)

        EXP_BANK, RING, PV_BANK, OT_BANK = (0, 2), (4, 5), 6, 7
        MAX_AHEAD = 3
        ROWS_AHEAD = MAX_AHEAD - 1
        GROUP_CELLS = (
            ((0, 0, 0, 0), (1, 0, 1, 0)),
            ((2, 0, 0, 0), (3, 0, 1, 0)),
            ((0, 1, 0, 0), (0, 3, 0, 384), (1, 1, 1, 0), (1, 3, 1, 384)),
            ((2, 1, 0, 0), (2, 3, 0, 384), (3, 1, 1, 0), (3, 3, 1, 384)),
            ((0, 2, 0, 0), (1, 2, 0, 256), (2, 2, 1, 0), (3, 2, 1, 256)))
        MAX_TILES = tuple((3, (c,)) for c in range(4)) + tuple((2, (c,)) for c in range(4)) \
            + ((1, (0, 1)), (1, (2, 3)), (0, (0, 1, 2, 3)))
        MT = len(MAX_TILES)
        HEADS_AT = 3
        SLOT_TILES = (2, 2, 2, 3, 2)

        def pair_at(b, p, shift):
            row, pair = b + (p + shift) // PAIRS, (p + shift) % PAIRS
            if isinstance(row, int) and not 0 <= row < B:
                return None
            return row, pair, PAIRS * row + pair

        with ExitStack() as local:
            def tmp(name, shape, dt=F32):
                return local.enter_context(nc.sbuf_tensor(name, shape, dt))
            nmax = tmp("nmax", [P, 2, QB, 4])
            nres = tmp("nres", [P, 2, QB, 4])
            nparts = tmp("nparts", [P, 2, QB, 4, 3], BF16)
            nrow = tmp("nrow", [12, 2, N], BF16)
            o_t = tmp("o_t", [P, N])
            recip = tmp("recip", [P, QB, 4])
            o_half = tmp("o_half", [P, 2, QB, 4, 2 * DH])
            sq = tmp("sq", [P, 2, QB, 2, 2 * DH])
            block = local.enter_context(nc.Block())

            def rows(pair, c):
                return 64 * (c % 2), 2 * pair + c // 2

            def over_rows(engine, body):
                body(0)
                with engine.Fori(1, B - 1) as b:
                    body(b)
                body(B - 1)

            @block.sync
            def _(sp):
                def load_v(at):
                    b, p, _ = at
                    sp.dma_start(v_aug[:, p, :], v_dram[b, :, p, :]).then_inc(s_vload[p], 16)

                def max_rows(at):
                    _, p, n = at
                    sp.wait_ge(s_mtc, n + 1)
                    for c in range(4):
                        r0, s = rows(p, c)
                        sp.dma_start(q_st[r0 + KR:r0 + KM, s, :], nrow[3 * c:3 * c + 3, p % 2, :])\
                          .then_inc(s_mrow[p], 16)

                def body(b):
                    for p in range(PAIRS):
                        n = PAIRS * b + p
                        at = pair_at(b, p, ROWS_AHEAD)
                        if at:
                            max_rows(at)
                        prev = pair_at(b, p, -1)
                        at = pair_at(b, p, PAIRS - 1)
                        if prev and at:
                            sp.wait_ge(s_pv, prev[2] + 1)
                            load_v(at)
                        at = pair_at(b, p, PAIRS)
                        if at:
                            sp.wait_ge(s_score, GROUPS * (n + 1))
                            if p == 0:
                                written(sp, at[0])
                            load(sp, at)

                for p in range(PAIRS):
                    if p >= EARLY_LOADS:
                        load(sp, (0, p, p))
                    load_v((0, p, p))
                for p in range(ROWS_AHEAD):
                    max_rows((0, p, p))
                over_rows(sp, body)

            @block.gpsimd
            def _(pool):
                def split_max(at):
                    _, p, n = at
                    pool.wait_ge(s_maxr, MT * (n + 1))
                    if positive(n - 1):
                        pool.wait_ge(s_mt, n - 1)
                    pool.sem_inc(s_pool_go, 1)
                    link = Chain(pool, s_mchain, 4 * n)
                    a, r, o = nmax[:, p % 2], nres[:, p % 2], nparts[:, p % 2]
                    link(nc.gpsimd.tensor_copy(o[:, :, :, 0], a))
                    link(nc.gpsimd.tensor_tensor(r, a, o[:, :, :, 0], ALU.subtract))
                    pool.sem_inc(s_pool_go, 1)
                    link(nc.gpsimd.tensor_copy(o[:, :, :, 1], r))
                    link(nc.gpsimd.tensor_tensor(r, r, o[:, :, :, 1], ALU.subtract))
                    pool.sem_inc(s_pool_go, 1)
                    nc.gpsimd.tensor_copy(o[:, :, :, 2], r).then_inc(s_msplit, 1)

                def mask(n, p, g):
                    pool.wait_ge(s_prob, GROUPS * n + g + 1)
                    cells = probs[:, p % 2, g]
                    if g < 2:
                        views = (cells[:, :, 0:P],)
                    elif g < 4:
                        views = (cells[:, :, 0:P], cells[:, :, 3 * P:4 * P])
                    else:
                        views = (cells.rearrange("p a (k n) -> p (a k) n", n=2 * P)[:, :, 0:P],)
                    pool.sem_inc(s_pool_go, 1)
                    for v in views:
                        ins = nc.gpsimd.affine_select(out=v, in_=v, compare_op=ALU.is_ge, fill=0.0, base=0,
                                                      pattern=[[0, v.shape[1]], [1, P]], channel_multiplier=-1)
                    ins.then_inc(s_masked, 1)

                def join(at):
                    b, p, n = at
                    pool.wait_ge(s_oh, n + 1)
                    oh = o_half[:, p % 2].rearrange("p t (h a) d -> p t h a d", a=2)
                    nc.gpsimd.tensor_tensor(attn[:, b, :, 2 * p:2 * p + 2, :], oh[:, :, :, 0, :], oh[:, :, :, 1, :],
                                            ALU.add).then_inc(s_o, 1)

                def square(at):
                    b, p, n = at
                    pool.wait_ge(s_o, n + 1)
                    if positive(n - 1):
                        pool.wait_ge(s_ss, n - 1)
                    pool.sem_inc(s_pool_go, 1)
                    o = attn[:, b, :, 2 * p:2 * p + 2, :]
                    nc.gpsimd.tensor_tensor(sq[:, p % 2], o, o, ALU.mult).then_inc(s_sq, 1)

                def body(b):
                    for p in range(PAIRS):
                        n = PAIRS * b + p
                        at = pair_at(b, p, MAX_AHEAD - 1)
                        if at and (at[2] if isinstance(at[2], int) else MAX_AHEAD) >= MAX_AHEAD:
                            split_max(at)
                        for g in range(GROUPS):
                            mask(n, p, g)
                            at = pair_at(b, p, -2)
                            if g == 3 and at:
                                join(at)
                            if g == 4 and at:
                                square(at)
                        if is_last(b) and p == PAIRS - 2:
                            pool.wait_ge(s_hn, 1)
                            for early in NORMED_EARLY:
                                normed_heads(nc.gpsimd, early).then_inc(s_hng_pool, 1)

                for n in range(MAX_AHEAD):
                    split_max((0, n, n))
                over_rows(pool, body)
                for p in range(PAIRS - 2, PAIRS):
                    join(pair_at(B - 1, 0, p))
                    square(pair_at(B - 1, 0, p))

            @block.tensor
            def _(pe):
                def max_tile(at, k):
                    _, p, n = at
                    i = MT * n + k
                    bank = psum[:, RING[(MT * p + k) % 2], :]
                    if k == 0:
                        b = at[0]
                        pe.wait_ge(s_load[p], 64 * (b + 1))
                    if positive(i - 1):
                        pe.wait_ge(s_maxr, i - 1)
                    qb, combos = MAX_TILES[k]
                    w = (qb + 1) * P
                    for a, c in enumerate(combos):
                        nc.tensor.matmul(bank[:, a * w:(a + 1) * w], q_st[:, rows(p, c)[1], qb * P:w],
                                         k_st[:, 4 * p + c, 0:w], start=True, stop=False)
                        ins = nc.tensor.matmul(bank[:, (a + 1) * w - P:(a + 1) * w], ident_bf[:, :],
                                               causal_bf[:, :], start=False, stop=True)
                    ins.then_inc(s_max, 1)

                def max_transpose(at):
                    _, p, n = at
                    pe.wait_ge(s_msplit, n + 1)
                    if positive(n - ROWS_AHEAD - 1):
                        pe.wait_ge(s_oh, n - ROWS_AHEAD - 1)
                    if positive(n):
                        pe.wait_ge(s_mtc, n)
                    dst = psum[:, OT_BANK, :].bitcast(BF16)
                    for t in range(QB):
                        ins = nc.tensor.transpose(dst[0:12, t * P:(t + 1) * P],
                                                  nparts[:, p % 2, t].rearrange("p c a -> p (c a)"), ident_bf[:, :])
                    ins.then_inc(s_mt, 1)

                def scores(b, p, g):
                    i = GROUPS * (PAIRS * b + p) + g
                    if g == 0:
                        pe.wait_ge(s_mrow[p], 64 * (b + 1))
                    if positive(i - 1):
                        pe.wait_ge(s_prob, i - 1)
                    base = EXP_BANK[(GROUPS * p + g) % 2]
                    for c, kb, bank, col in GROUP_CELLS[g]:
                        ins = nc.tensor.matmul(psum[:, base + bank, col:col + N - kb * P],
                                               k_st[:, 4 * p + c, kb * P:(kb + 1) * P],
                                               q_st[:, rows(p, c)[1], kb * P:N], start=True, stop=True)
                    ins.then_inc(s_score, 1)

                def values(at, part):
                    b, p, n = at
                    if part == 0:
                        pe.wait_ge(s_vload[p], 16 * (b + 1))
                        if positive(n):
                            pe.wait_ge(s_pvc, n)
                    groups = ((0, 1), (2, 3), (4,))[part]
                    pe.wait_ge(s_masked, GROUPS * n + groups[-1] + 1)
                    for kb in ((0,), (1, 3), (2,))[part]:
                        for c in range(4):
                            g, bank, col = [(g, bank, col) for g in groups
                                            for cc, k, bank, col in GROUP_CELLS[g] if (cc, k) == (c, kb)][0]
                            v = v_aug[:, p, :].rearrange("p (t h v) -> p t h v", t=QB, h=2)[:, kb, c // 2, :]
                            ins = nc.tensor.matmul(psum[32 * c:32 * c + HV, PV_BANK, kb * P:N], v,
                                                   probs[:, p % 2, g, bank, col:col + N - kb * P],
                                                   start=(kb == 0), stop=(kb == 2), tile_position=(0, 32 * c),
                                                   skip_group_check=True)
                    if part == 2:
                        ins.then_inc(s_pv, 1)

                def out_transpose(at):
                    _, p, n = at
                    pe.wait_ge(s_pvc, n + 1)
                    if positive(n):
                        pe.wait_ge(s_oh, n)
                    m = n + 1 + ROWS_AHEAD
                    pe.wait_ge(s_mtc, min(m + 1, PAIRS * B) if isinstance(m, int) else m + 1)
                    for t in range(QB):
                        ins = nc.tensor.transpose(psum[:, OT_BANK, t * P:(t + 1) * P], o_t[:, t * P:(t + 1) * P],
                                                  ident[:, :])
                    ins.then_inc(s_ot, 1)

                def body(b):
                    for p in range(PAIRS):
                        prev = pair_at(b, p, -1)
                        ahead = pair_at(b, p, MAX_AHEAD)
                        rows_ahead = pair_at(b, p, ROWS_AHEAD)
                        k = 0
                        for g in range(GROUPS):
                            scores(b, p, g)
                            for i in range(SLOT_TILES[g]):
                                if i == 1 and prev and g in (1, 2, 3):
                                    values(prev, g - 1)
                                if i == 1 and g == 4 and rows_ahead:
                                    max_transpose(rows_ahead)
                                if ahead:
                                    max_tile(ahead, k)
                                    k += 1
                            if g == 0 and pair_at(b, p, -2):
                                out_transpose(pair_at(b, p, -2))

                pe.wait_ge(s_zero, 1)
                for n in range(MAX_AHEAD):
                    for k in range(MT):
                        max_tile((0, n, n), k)
                    if n >= 1:
                        max_transpose((0, n - 1, n - 1))
                over_rows(pe, body)
                last = (B - 1, PAIRS - 1, PAIRS * B - 1)
                out_transpose((B - 1, PAIRS - 2, PAIRS * B - 2))
                for part in range(3):
                    values(last, part)
                out_transpose(last)

            @block.scalar
            def _(act):
                def rows_copy(at):
                    _, p, n = at
                    act.wait_ge(s_mt, n + 1)
                    if positive(n - 1):
                        b = at[0]
                        if p >= 2:
                            act.wait_ge(s_mrow[p - 2], 64 * (b + 1))
                        else:
                            act.wait_ge(s_mrow[PAIRS - 2 + p], 64 * b)
                    nc.scalar.copy(nrow[:, p % 2, :], psum[:, OT_BANK, :].bitcast(BF16)[0:12, 0:N]).then_inc(s_mtc, 1)

                def pv_copy(at):
                    _, p, n = at
                    act.wait_ge(s_pv, n + 1)
                    if positive(n):
                        act.wait_ge(s_ot, n)
                    nc.scalar.copy(o_t[:, :], psum[:, PV_BANK, :]).then_inc(s_pvc, 1)

                def body(b):
                    for p in range(PAIRS):
                        n = PAIRS * b + p
                        for g in range(GROUPS):
                            act.wait_ge(s_score, GROUPS * n + g + 1)
                            if g == 0 and positive(n - 1):
                                act.wait_ge(s_pv, n - 1)
                            base = EXP_BANK[(GROUPS * p + g) % 2]
                            nc.scalar.activation(probs[:, p % 2, g], psum[:, base:base + 2, :], ACT.Exp,
                                                 scale=SCALE).then_inc(s_prob, 1)
                            if g == 4 and pair_at(b, p, ROWS_AHEAD):
                                rows_copy(pair_at(b, p, ROWS_AHEAD))
                            if g == 3 and pair_at(b, p, -1):
                                pv_copy(pair_at(b, p, -1))
                            if g == 4 and is_last(b) and p == HEADS_AT + 1:
                                head_roots(act, 0)

                for n in range(ROWS_AHEAD):
                    rows_copy((0, n, n))
                for s in range(2):
                    act.wait_ge(s_qk_out[s], QK_OUT * B // 2)
                over_rows(act, body)
                pv_copy((B - 1, PAIRS - 1, PAIRS * B - 1))

            @block.vector
            def _(dve):
                def max_tile(at, k):
                    _, p, n = at
                    bank = psum[:, RING[(MT * p + k) % 2], :]
                    if k == 0 and positive(n - 1):
                        dve.wait_ge(s_msplit, n - 1)
                    dve.wait_ge(s_max, MT * n + k + 1)
                    qb, combos = MAX_TILES[k]
                    w = (qb + 1) * P
                    nc.vector.tensor_reduce(nmax[:, p % 2, qb, combos[0]:combos[-1] + 1],
                                            bank[:, 0:len(combos) * w].rearrange("p (a n) -> p a n", n=w),
                                            AX.X, ALU.max, negate=True).then_inc(s_maxr, 1)

                def normalise(at):
                    _, p, n = at
                    dve.wait_ge(s_ot, n + 1)
                    ot = psum[:, OT_BANK, :].rearrange("p (t c v) -> p t c v", t=QB, c=4)
                    nc.vector.reciprocal(recip[:, :, :], ot[:, :, :, 2 * DH]).then_inc(s_rec, 1)
                    dve.wait_ge(s_rec, n + 1)
                    cf = coef[:, 2 * p:2 * p + 2, :].rearrange("p h a -> p (h a)")[:, None, :].to_broadcast([P, QB, 4])
                    nc.vector.tensor_tensor(recip[:, :, :], recip[:, :, :], cf, ALU.mult).then_inc(s_recl, 1)
                    dve.wait_ge(s_recl, n + 1)
                    if positive(n - 1):
                        dve.wait_ge(s_o, n - 1)
                    nc.vector.tensor_tensor(o_half[:, p % 2], ot[:, :, :, 0:2 * DH],
                                            recip[:, :, :, None].to_broadcast([P, QB, 4, 2 * DH]),
                                            ALU.mult).then_inc(s_oh, 1)

                def square_sum(at):
                    b, p, n = at
                    dve.wait_ge(s_sq, n + 1)
                    nc.vector.tensor_reduce(hv[:, :].rearrange("p (b t h) -> p b t h", b=B, t=QB)[:, b, :, 2 * p:2 * p + 2],
                                            sq[:, p % 2], AX.X, ALU.add).then_inc(s_ss, 1)

                def body(b):
                    for p in range(PAIRS):
                        ahead = pair_at(b, p, MAX_AHEAD)
                        k = 0
                        for g in range(GROUPS):
                            for _ in range(SLOT_TILES[g]):
                                if ahead:
                                    max_tile(ahead, k)
                                    k += 1
                            if g == 0 and pair_at(b, p, -2):
                                normalise(pair_at(b, p, -2))
                            if g == 4 and is_last(b) and p == HEADS_AT:
                                head_means(0)
                            if g == 4 and is_last(b) and p == HEADS_AT + 2:
                                head_newton(dve, heads_link, 0)
                            if g == 3 and pair_at(b, p, -3):
                                square_sum(pair_at(b, p, -3))

                heads_link = dve_chain(dve)
                nc.vector.memset(psum[:, PV_BANK, :], 0.0).then_inc(s_zero, 1)
                for n in range(MAX_AHEAD):
                    for k in range(MT):
                        max_tile((0, n, n), k)
                over_rows(dve, body)
                for p in range(PAIRS - 2, PAIRS):
                    normalise((B - 1, p, PAIRS * (B - 1) + p))
                for p in range(PAIRS - 3, PAIRS):
                    square_sum((B - 1, p, PAIRS * (B - 1) + p))
                dve_steps[0] += heads_link.n

        stacks.close()

        s_at = sem("s_at")
        s_atc = sem("s_atc")
        s_op = sem("s_op")
        s_opc = sem("s_opc")
        s_ln = [sem(f"s_ln{k}") for k in range(3)]
        s_rsq = [sem(f"s_rsq{k}") for k in range(3)]
        s_an = sem("s_an")
        s_x2 = sem("s_x2")
        s_u = sem("s_u")
        s_tu = sem("s_tu")
        s_xr = sem("s_xr")
        s_ft = sem("s_ft")
        s_ftc = sem("s_ftc")
        s_hid = sem("s_hid")
        s_gelu = sem("s_gelu")
        s_ff = sem("s_ff")
        s_ffc = sem("s_ffc")
        s_bias = sem("s_bias")
        s_hones = sem("s_hones")
        s_r = sem("s_r")
        s_ra = sem("s_ra")
        s_wsel = sem("s_wsel")
        s_zt = sem("s_zt")
        s_wcol = sem("s_wcol")
        s_rp = sem("s_rp")
        ROUTED_BY_POOL = (2, 3, 6, 7)
        s_nm = sem("s_nm")
        s_on = [sem(f"s_on{r}") for r in range(2)]
        s_fin = [sem(f"s_fin{r}") for r in range(2)]
        s_out = sem("s_out")
        GROUP_STEPS = [min(REBASE, ITERS - 1 - REBASE * r) for r in range(REBASES)]
        HALF_ROWS = B // 2
        HT = TILES // 2
        L1 = 1 + HC
        BANK_AT, BANK_OP, BANK_XT, BANK_HID, BANK_LIGHT, BANK_HEAVY = (0, 4), 2, 3, (0, 1, 4, 5), 6, 7
        with ExitStack() as local:
            def tmp(name, shape, dt=F32):
                return local.enter_context(nc.sbuf_tensor(name, shape, dt))
            a_t = tmp("a_t", [P, 2, 2, N])
            ao = tmp("ao", [P, TILES, D])
            vg = tmp("vg", [P, 2, TILES])
            vl = tmp("vl", [P, 2, TILES])
            vr = tmp("vr", [P, 2, TILES])
            vt = tmp("vt", [P, 2, TILES])
            nm = tmp("nm", [P, TILES])
            xr = tmp("xr", [P, TILES, D])
            u_col = tmp("u_col", [P, QB, B])
            xr_t = tmp("xr_t", [P, 2, N])
            hid = tmp("hid", [P, 2, L1, N])
            light = tmp("light", [P, TILES, D])
            heavy = tmp("heavy", [P, TILES, D])
            u = tmp("u", [B, N])
            z = tmp("z", [B, N])
            e = tmp("e", [B, N])
            f = tmp("f", [B, N])
            key = tmp("key", [B, 2, N])
            sel = tmp("sel", [B, N])
            top = tmp("top", [B, 8])
            umax = tmp("umax", [B, 1])
            zmax = tmp("zmax", [B, 1])
            zsum = tmp("zsum", [B, 1])
            beta = tmp("beta", [B, 1])
            ts = tmp("ts", [B, 1])
            tt = tmp("tt", [B, REBASE + 1])
            wcol = tmp("wcol", [P, QB, B])
            block = local.enter_context(nc.Block())

            def half(h):
                return range(HALF_ROWS * h, HALF_ROWS * (h + 1))

            def tiles(h):
                return slice(HT * h, HT * (h + 1))

            @block.gpsimd
            def _(pool):
                for b in range(B):
                    if b == B - 1:
                        pool.wait_ge(s_hn, 2)
                    if b not in NORMED_BY_DVE + NORMED_EARLY:
                        normed_heads(nc.gpsimd, b).then_inc(s_hng_pool, 1)
                pool.wait_ge(s_hng_pool, B - len(NORMED_BY_DVE))
                nc.gpsimd.memset(hid[LIGHT:P, :, 0, :], 1.0).then_inc(s_hones, 1)
                pool.wait_ge(s_hones, 1)
                for b in range(B):
                    pool.wait_ge(s_an, b + 1)
                    row = slice(b * QB, (b + 1) * QB)
                    nc.gpsimd.tensor_tensor(x[:, row, :], x[:, row, :], ao[:, row, :], ALU.add).then_inc(s_x2, 1)
                for b in range(B):
                    pool.wait_ge(s_ffc, 2 * (b + 1))
                    row = slice(b * QB, (b + 1) * QB)
                    nc.gpsimd.tensor_tensor(heavy[:, row, :], heavy[:, row, :],
                                            b2[:, :, :].to_broadcast([P, QB, D]), ALU.add).then_inc(s_bias, 1)
                pool.wait_ge(s_wcol, 1)
                for k, b in enumerate(ROUTED_BY_POOL):
                    row = slice(b * QB, (b + 1) * QB)
                    pool.wait_ge(s_bias, b + 1)
                    nc.gpsimd.tensor_tensor(heavy[:, row, :], heavy[:, row, :],
                                            wcol[:, :, b:b + 1].to_broadcast([P, QB, D]), ALU.mult).then_inc(s_rp, 1)
                    pool.wait_ge(s_rp, 2 * k + 1)
                    nc.gpsimd.tensor_tensor(heavy[:, row, :], heavy[:, row, :], light[:, row, :],
                                            ALU.add).then_inc(s_rp, 1)
                for b in range(0, B, 2):
                    pool.wait_ge(s_on[0], b // 2 + 1)
                    row = slice(b * QB, (b + 1) * QB)
                    nc.gpsimd.tensor_tensor(heavy[:, row, :], heavy[:, row, :], x[:, row, :],
                                            ALU.add).then_inc(s_fin[0], 1)

            @block.scalar
            def _(act):
                logs = [len(HEAD_PARTS)]

                def rsqrt(outs):
                    for _, log, v, shift in outs:
                        ins = nc.scalar.activation(log, v, ACT.Ln, scale=float(2 ** shift))
                    ins.then_inc(s_hl, 1)
                    logs[0] += 1
                    act.wait_ge(s_hl, logs[0])
                    for out_, log, _, shift in outs:
                        if shift:
                            ins = nc.scalar.activation(out_, log, ACT.Exp, scale=-0.5, bias=shift_col[:, 0:1])
                        else:
                            ins = nc.scalar.activation(out_, log, ACT.Exp, scale=-0.5)
                    return ins

                def layer_norm(k, h):
                    act.wait_ge(s_ln[k], h + 1)
                    s = tiles(h)
                    pairs = [(vr[:, 0, s], vl[:, 0, s], vg[:, 0, s], 0)]
                    if k == 1:
                        pairs.append((vr[:, 1, s], vl[:, 1, s], vg[:, 1, s], LOG_SHIFT))
                    rsqrt(pairs).then_inc(s_rsq[k], 1)

                def normed(h):
                    act.wait_ge(s_nm, h + 1)
                    for b in half(h)[1::2]:
                        for i in range(b * QB, (b + 1) * QB):
                            ins = nc.scalar.activation(heavy[:, i, :], heavy[:, i, :], ACT.Identity,
                                                       scale=vr[:, 0, i:i + 1], bias=nm[:, i:i + 1])
                        ins.then_inc(s_on[1], 1)

                def a_copy(b):
                    act.wait_ge(s_at, b + 1)
                    if b >= 2:
                        act.wait_ge(s_op, b - 1)
                    base = BANK_AT[b % 2]
                    nc.scalar.copy(a_t[:, b % 2], psum[:, base:base + 2, :]).then_inc(s_atc, 1)

                def out_rows(b):
                    if b + 1 < B:
                        a_copy(b + 1)
                    act.wait_ge(s_op, b + 1)
                    nc.scalar.copy(ao[:, b * QB:(b + 1) * QB, :].rearrange("p t d -> p (t d)"),
                                   psum[:, BANK_OP, :]).then_inc(s_opc, 1)

                def xr_copy(b):
                    act.wait_ge(s_ft, b + 1)
                    nc.scalar.copy(xr_t[:, b % 2, :], psum[:, BANK_XT, :]).then_inc(s_ftc, 1)

                def ff_copy(b):
                    for k, (dst, bank) in enumerate(((light, BANK_LIGHT), (heavy, BANK_HEAVY))):
                        act.wait_ge(s_ff, 2 * b + k + 1)
                        nc.scalar.copy(dst[:, b * QB:(b + 1) * QB, :].rearrange("p t d -> p (t d)"),
                                       psum[:, bank, :]).then_inc(s_ffc, 1)

                def gelus(b):
                    if b >= 2:
                        ff_copy(b - 2)
                    for c in range(L1):
                        n = L1 * b + c
                        act.wait_ge(s_hid, n + 1)
                        if b >= 2 and c == 0:
                            act.wait_ge(s_ff, 2 * (b - 1))
                        m = LIGHT if c == 0 else P
                        nc.scalar.activation(hid[0:m, b % 2, c, :], psum[0:m, BANK_HID[n % 4], :],
                                             ACT.Gelu, bias=b1c[0:m, c:c + 1]).then_inc(s_gelu, 1)
                    if b + 1 < B:
                        xr_copy(b + 1)

                a_copy(0)
                for b in half(0):
                    if b == 1:
                        head_roots(act, 1)
                    out_rows(b)
                layer_norm(0, 0)
                for b in half(1):
                    out_rows(b)
                layer_norm(1, 0)
                layer_norm(0, 1)
                xr_copy(0)
                gelus(0)
                gelus(1)
                layer_norm(1, 1)
                act.wait_ge(s_r, 1)
                nc.scalar.activation(e[:, :], z[:, :], ACT.Exp, accum_out=zsum[:, :]).then_inc(s_ra, 1)
                act.wait_ge(s_ra, 1)
                nc.scalar.activation(ts[:, :], zsum[:, :], ACT.Ln).then_inc(s_ra, 1)
                done = 2
                for r in range(REBASES):
                    act.wait_ge(s_r, 2 + 2 * r)
                    nc.scalar.activation(f[:, :], z[:, :], ACT.Exp).then_inc(s_ra, 1)
                    for b in range(done, min(done + GELUS_BESIDE[r], B)):
                        gelus(b)
                    done += GELUS_BESIDE[r]
                    act.wait_ge(s_r, 3 + 2 * r)
                    n = GROUP_STEPS[r]
                    nc.scalar.activation(ts[:, :], tt[:, n:n + 1], ACT.Ln,
                                         scale=float(K_ROUTE ** -n * 2.0 ** -T_SHIFT)).then_inc(s_ra, 1)
                act.wait_ge(s_r, 2 + 2 * REBASES)
                nc.scalar.activation(e[:, :], z[:, :], ACT.Exp).then_inc(s_ra, 1)
                for b in range(done, B):
                    gelus(b)
                ff_copy(B - 2)
                ff_copy(B - 1)
                for h in range(2):
                    layer_norm(2, h)
                for h in range(2):
                    normed(h)

            @block.tensor
            def _(pe):
                def project(b):
                    for t in range(QB):
                        for k in range(2):
                            ins = nc.tensor.matmul(psum[:, BANK_OP, t * P:(t + 1) * P],
                                                   a_t[:, b % 2, k, t * P:(t + 1) * P], w_o[:, k, :],
                                                   start=(k == 0), stop=(k == 1))
                    ins.then_inc(s_op, 1)

                def heads_transposed(b):
                    if b in NORMED_BY_DVE:
                        pe.wait_ge(s_hng_dve, NORMED_BY_DVE.index(b) + 1)
                    else:
                        pe.wait_ge(s_hng_pool, sum(1 for a in range(b + 1) if a not in NORMED_BY_DVE))
                    if b >= 2:
                        pe.wait_ge(s_atc, b - 1)
                    for k in range(2):
                        for t in range(QB):
                            ins = nc.tensor.transpose(psum[:, BANK_AT[b % 2] + k, t * P:(t + 1) * P],
                                                      attn[:, b, t].rearrange("p h d -> p (h d)")[:, k * P:(k + 1) * P],
                                                      ident[:, :])
                    ins.then_inc(s_at, 1)

                heads_transposed(0)
                for b in range(B):
                    if b + 1 < B:
                        heads_transposed(b + 1)
                    pe.wait_ge(s_atc, b + 1)
                    if b >= 1:
                        pe.wait_ge(s_opc, b)
                    project(b)

                def transposed(b):
                    pe.wait_ge(s_xr, b + 1)
                    if b >= 1:
                        pe.wait_ge(s_ftc, b)
                    for t in range(QB):
                        ins = nc.tensor.transpose(psum[:, BANK_XT, t * P:(t + 1) * P], xr[:, b * QB + t, :], ident[:, :])
                    ins.then_inc(s_ft, 1)

                def second_layer(b):
                    pe.wait_ge(s_gelu, L1 * b + 1)
                    if b >= 1:
                        pe.wait_ge(s_ffc, 2 * b - 1)
                    for t in range(QB):
                        ins = nc.tensor.matmul(psum[:, BANK_LIGHT, t * P:(t + 1) * P],
                                               hid[0:LIGHT + 1, b % 2, 0, t * P:(t + 1) * P],
                                               w2l[:, :], start=True, stop=True)
                    ins.then_inc(s_ff, 1)
                    pe.wait_ge(s_gelu, L1 * (b + 1))
                    if b >= 1:
                        pe.wait_ge(s_ffc, 2 * b)
                    for t in range(QB):
                        for c in range(HC):
                            ins = nc.tensor.matmul(psum[:, BANK_HEAVY, t * P:(t + 1) * P],
                                                   hid[:, b % 2, 1 + c, t * P:(t + 1) * P], w2h[:, c, :],
                                                   start=(c == 0), stop=(c == HC - 1))
                    ins.then_inc(s_ff, 1)

                transposed(0)
                pe.wait_ge(s_hones, 1)
                for b in range(B):
                    pe.wait_ge(s_ftc, b + 1)
                    for c in range(L1):
                        n = L1 * b + c
                        if n >= 4:
                            pe.wait_ge(s_gelu, n - 3)
                        m = LIGHT if c == 0 else P
                        w0 = 0 if c == 0 else LIGHT + (c - 1) * P
                        nc.tensor.matmul(psum[0:m, BANK_HID[n % 4], :], w1g[:, w0:w0 + m], xr_t[:, b % 2, :],
                                         start=True, stop=True).then_inc(s_hid, 1)
                    if b + 1 < B:
                        transposed(b + 1)
                    if b == 1:
                        pe.wait_ge(s_u, 1)
                        pe.wait_ge(s_opc, B)
                        for t in range(QB):
                            ins = nc.tensor.transpose(psum[0:B, BANK_OP, t * P:(t + 1) * P], u_col[:, t, :], ident[:, :])
                        ins.then_inc(s_tu, 1)
                    if b >= 1:
                        second_layer(b - 1)
                second_layer(B - 1)
                pe.wait_ge(s_wsel, 1)
                for t in range(QB):
                    ins = nc.tensor.transpose(psum[:, BANK_OP, t * B:(t + 1) * B], sel[:, t * P:(t + 1) * P],
                                              ident[0:B, 0:B])
                ins.then_inc(s_zt, 1)

            @block.sync
            def _(sp):
                for b in range(B):
                    sp.wait_ge(s_fin[b % 2], b // 2 + 1)
                    sp.dma_start(out[b].rearrange("(t p) d -> p t d", p=P), heavy[:, b * QB:(b + 1) * QB, :])\
                      .then_inc(s_out, 16)
                sp.wait_ge(s_out, 16 * B)

            @block.vector
            def _(dve):
                link = dve_chain(dve)

                def half_stats(src, h, ready):
                    for b in half(h):
                        ready(b)
                        for i in range(b * QB, (b + 1) * QB):
                            ins = nc.vector.bn_stats(st[:, i, :], src[:, i, :])
                    link(ins)
                    for i in range(HT * h, HT * (h + 1)):
                        ins = nc.vector.bn_aggr(mv[:, i, :], st[:, i, :])
                    link(ins)
                    return nc.vector.tensor_scalar(vg[:, 0, tiles(h)], mv[:, tiles(h), 1], LN_EPS, None, ALU.add)

                def normed(dst, src, rows_, scale, done):
                    for b in rows_:
                        for i in range(b * QB, (b + 1) * QB):
                            ins = nc.vector.tensor_scalar(dst[:, i, :], src[:, i, :], mv[:, i, 0:1], scale(i),
                                                          ALU.subtract, ALU.mult)
                        ins.then_inc(done, 1)

                head_means(1)
                for b in NORMED_BY_DVE:
                    normed_heads(nc.vector, b).then_inc(s_hng_dve, 1)
                head_newton(dve, link, 1)

                def attention_stats(h):
                    half_stats(ao, h, lambda b: dve.wait_ge(s_opc, b + 1)).then_inc(s_ln[0], 1)

                def attention_norm(h):
                    dve.wait_ge(s_rsq[0], h + 1)
                    s = tiles(h)
                    newton(dve, link, vr[:, 0, s], vg[:, 0, s], vt[:, 0, s])
                    normed(ao, ao, half(h), lambda i: vr[:, 0, i:i + 1], s_an)

                def input_stats(h):
                    s = tiles(h)
                    link(half_stats(x, h, lambda b: dve.wait_ge(s_x2, b + 1)))
                    link(nc.vector.reciprocal(vg[:, 1, s], vg[:, 0, s]))
                    link(nc.vector.tensor_tensor(vg[:, 1, s], vg[:, 1, s], mv[:, s, 1], ALU.mult))
                    nc.vector.tensor_scalar(vg[:, 1, s], vg[:, 1, s], float(D), 1e-24, ALU.mult, ALU.max)\
                      .then_inc(s_ln[1], 1)

                def input_norm(h):
                    dve.wait_ge(s_rsq[1], h + 1)
                    s = tiles(h)
                    newton(dve, link, vr[:, :, s], vg[:, :, s], vt[:, :, s])
                    link(nc.vector.scalar_tensor_tensor(out=vt[:, 0, s], in0=vr[:, 0, s], scalar=float(D) ** 0.5,
                                                        in1=vr[:, 1, s], op0=ALU.mult, op1=ALU.mult))
                    normed(xr, x, half(h), lambda i: vt[:, 0, i:i + 1], s_xr)

                def routing_scores(h):
                    dve.wait_ge(s_xr, HALF_ROWS * (h + 1))
                    for i in range(HT * h, HT * (h + 1)):
                        ins = nc.vector.tensor_tensor_reduce(out=ao[:, i, :], in0=xr[:, i, :], in1=route_row[:, :],
                                                             scale=1.0, scalar=0.0, op0=ALU.mult, op1=ALU.add,
                                                             accum_out=u_col[:, i % QB, i // QB:i // QB + 1])
                    link(ins)

                attention_stats(0)
                attention_norm(0)
                input_stats(0)
                attention_stats(1)
                input_norm(0)
                attention_norm(1)
                routing_scores(0)
                input_stats(1)
                input_norm(1)
                routing_scores(1)
                by_tile = lambda v: v.rearrange("p (b t) -> p t b", t=QB)
                link(nc.vector.scalar_tensor_tensor(out=u_col[:, :, :], in0=u_col[:, :, :], scalar=10.0 * float(D) ** -0.5,
                                                    in1=by_tile(vg[:, 1, :]), op0=ALU.mult, op1=ALU.mult))
                nc.vector.tensor_tensor(u_col[:, :, :], u_col[:, :, :], by_tile(vr[:, 1, :]), ALU.mult)\
                  .then_inc(s_u, 1)

                dve.wait_ge(s_tu, 1)
                link(nc.vector.reduce_max(umax[:, :], psum[0:B, BANK_OP, :], AX.X))
                link(nc.vector.tensor_scalar(zmax[:, :], umax[:, :], 0.0, None, ALU.min))
                nc.vector.tensor_scalar(z[:, :], psum[0:B, BANK_OP, :], 0.0, zmax[:, 0:1], ALU.min, ALU.subtract)\
                  .then_inc(s_r, 1)
                link(nc.vector.tensor_copy(u[:, :], psum[0:B, BANK_OP, :]))
                dve.wait_ge(s_ra, 2)
                link(nc.vector.tensor_scalar(beta[:, :], ts[:, :], zmax[:, 0:1], LOG_K, ALU.add, ALU.subtract))
                for r in range(REBASES):
                    nc.vector.tensor_scalar(z[:, :], u[:, :], beta[:, 0:1], CLIP, ALU.subtract, ALU.min)\
                      .then_inc(s_r, 1)
                    link(nc.vector.memset(tt[:, 0:1], 1.0))
                    dve.wait_ge(s_ra, 3 + 2 * r)
                    for k in range(GROUP_STEPS[r]):
                        last = nc.vector.scalar_tensor_tensor(
                            out=key[:, 0, :], in0=f[:, :], scalar=K_ROUTE ** k,
                            in1=tt[:, k:k + 1].to_broadcast([B, N]), op0=ALU.mult, op1=ALU.min,
                            accum_out=tt[:, k + 1:k + 2])
                        if k + 1 < GROUP_STEPS[r]:
                            link(last)
                    last.then_inc(s_r, 1)
                    dve.wait_ge(s_ra, 4 + 2 * r)
                    link(nc.vector.scalar_tensor_tensor(out=beta[:, :], in0=ts[:, :], scalar=T_SHIFT * LN2,
                                                        in1=beta[:, :], op0=ALU.add, op1=ALU.add))
                nc.vector.tensor_scalar(z[:, :], u[:, :], beta[:, 0:1], 0.0, ALU.subtract, ALU.min).then_inc(s_r, 1)
                dve.wait_ge(s_r, 2 + 2 * REBASES)
                link(nc.vector.tensor_scalar(key[:, 0, :], z[:, :], CUT, None, ALU.max))
                for k in range(TOPK // 8):
                    link(nc.vector.max(top[:, :], key[:, k % 2, :]))
                    link(nc.vector.match_replace(out=key[:, (k + 1) % 2, :], in_to_replace=top[:, :],
                                                 in_values=key[:, k % 2, :], imm_value=2 * CUT))
                link(nc.vector.tensor_scalar(sel[:, :], key[:, (TOPK // 8) % 2, :], 1.5 * CUT, None, ALU.is_lt))
                dve.wait_ge(s_ra, 3 + 2 * REBASES)
                link(nc.vector.tensor_scalar(f[:, :], e[:, :], -1.0, 1.0, ALU.mult, ALU.add))
                link(nc.vector.tensor_tensor(e[:, :], e[:, :], f[:, :], ALU.add))
                nc.vector.tensor_tensor(sel[:, :], sel[:, :], e[:, :], ALU.mult).then_inc(s_wsel, 1)
                dve.wait_ge(s_zt, 1)
                nc.vector.tensor_copy(wcol[:, :, :].rearrange("p t b -> p (t b)"), psum[:, BANK_OP, 0:TILES])\
                  .then_inc(s_wcol, 1)
                dve.wait_ge(s_wcol, 1)

                def routed_sum(b):
                    if b in ROUTED_BY_POOL:
                        dve.wait_ge(s_rp, 2 * ROUTED_BY_POOL.index(b) + 2)
                        return
                    dve.wait_ge(s_bias, b + 1)
                    for i in range(b * QB, (b + 1) * QB):
                        ins = nc.vector.scalar_tensor_tensor(out=heavy[:, i, :], in0=heavy[:, i, :],
                                                             scalar=wcol[:, i % QB, i // QB:i // QB + 1],
                                                             in1=light[:, i, :], op0=ALU.mult, op1=ALU.add)
                    link(ins)

                for h in range(2):
                    half_stats(heavy, h, routed_sum).then_inc(s_ln[2], 1)
                for h in range(2):
                    dve.wait_ge(s_rsq[2], h + 1)
                    s = tiles(h)
                    newton(dve, link, vr[:, 0, s], vg[:, 0, s], vt[:, 0, s])
                    nc.vector.scalar_tensor_tensor(out=nm[:, s], in0=mv[:, s, 0], scalar=-1.0, in1=vr[:, 0, s],
                                                   op0=ALU.mult, op1=ALU.mult).then_inc(s_nm, 1)
                    normed(heavy, heavy, half(h)[::2], lambda i: vr[:, 0, i:i + 1], s_on[0])
                for b in range(1, B, 2):
                    dve.wait_ge(s_on[1], b // 2 + 1)
                    row = slice(b * QB, (b + 1) * QB)
                    nc.vector.tensor_tensor(heavy[:, row, :], heavy[:, row, :], x[:, row, :],
                                            ALU.add).then_inc(s_fin[1], 1)
                dve_steps[0] += link.n


_INS = ['L0_attn_X', 'L0_attn_W_q', 'L0_attn_W_k', 'L0_attn_W_v', 'L0_attn_W_o', 'L0_attn_lambda_q1',
        'L0_attn_lambda_k1', 'L0_attn_lambda_q2', 'L0_attn_lambda_k2', 'L0_attn_rms_scale',
        'L0_ffn_routing_token', 'L0_ffn_gamma_light', 'L0_ffn_w1_light', 'L0_ffn_b1_light', 'L0_ffn_w2_light',
        'L0_ffn_b2_light', 'L0_ffn_gamma_heavy', 'L0_ffn_w1_heavy', 'L0_ffn_b1_heavy', 'L0_ffn_w2_heavy',
        'L0_ffn_b2_heavy']


def kernel(**inputs):
    import numpy as _np
    import concourse.bacc as _bacc
    from concourse import mybir as _mybir
    from concourse.bass_utils import run_bass_kernel_spmd as _run

    nc = _bacc.Bacc("TRN2", target_bir_lowering=False, num_devices=1)
    arrays, args = {}, []
    for name in _INS:
        a = _np.ascontiguousarray(inputs[name])
        arrays[f"in_{name}_dram"] = a
        args.append(nc.dram_tensor(f"in_{name}_dram", a.shape, _mybir.dt.from_np(a.dtype), kind="ExternalInput").ap())
    args.append(nc.dram_tensor("out_0_dram", (B, N, D), F32, kind="ExternalOutput").ap())
    program(nc, *args)
    r = _run(nc, [arrays], core_ids=[0])
    return r.results[0]["out_0_dram"]
```
